# Optimizing a Trainium2 kernel written in Bass

```python
import numpy as np
import jax
import jax.numpy as jnp

def _softmax(x, axis=-1):
    return jax.nn.softmax(x, axis=axis)

def _gelu(x):
    return jax.nn.gelu(x, approximate=True)

def _silu(x):
    return jax.nn.silu(x)

def _sigmoid(x):
    return jax.nn.sigmoid(x)

def _layernorm(x, axis=-1, eps=1e-05):
    m = jnp.mean(x, axis=axis, keepdims=True)
    v = jnp.var(x, axis=axis, keepdims=True)
    return (x - m) / jnp.sqrt(v + eps)

def _scatter_add(tgt, idx, src, axis=0):
    return tgt.at[idx].add(src)

def _segment_sum(src, seg, n):
    return jax.ops.segment_sum(src, seg, n)
kernel_name = 'mk_xattn_ffn_d4_seqx_r8_2cd600'

def setup_inputs(seed: int=0):
    np.random.seed(seed)
    _w = jnp.asarray

    def _rec_inputs():
        import jax
        import jax.numpy as jnp
        _rk = jax.random.key(seed)
        x = -0.0002928 + 1 * jax.random.normal(jax.random.fold_in(_rk, 1), (8, 128, 512), jnp.float32)
        _lenS = 128 - jax.random.randint(jax.random.fold_in(_rk, 7), (8,), 0, max(1, 128 // 4) + 1, jnp.int32)
        _lenS2 = 128 - jax.random.randint(jax.random.fold_in(_rk, 8), (8,), 0, max(1, 128 // 4) + 1, jnp.int32)
        _ctx_4096P = jax.random.normal(jax.random.fold_in(_rk, 11), (8, 16, 512), jnp.float32)
        _ctx_4096c = jax.random.dirichlet(jax.random.fold_in(_rk, 511), 0.3 * jnp.ones((16,), jnp.float32), (8, 128))
        _ctx_4096t = jnp.einsum('bsk,bkd->bsd', _ctx_4096c, _ctx_4096P)
        _ctx_4096t = _ctx_4096t * jax.lax.rsqrt(jnp.mean(jnp.square(_ctx_4096t)) + 1e-12) * 0.953939
        ctx_4096 = -2.8382e-05 + 0.999851 * (_ctx_4096t + 0.3 * jax.random.normal(jax.random.fold_in(_rk, 611), (8, 128, 512), jnp.float32))
        _validS = jnp.arange(128)[None, :] < _lenS[:, None]
        _validS2 = jnp.arange(128)[None, :] < _lenS2[:, None]
        _causal = jnp.tril(jnp.ones((128, 128), dtype=bool))
        mask_1x1xSxS2_ff0 = jnp.where(jnp.ones((1, 1, 128, 128), dtype=bool), 0.0, -1000000000.0).astype(jnp.float32)
        return (x, ctx_4096, mask_1x1xSxS2_ff0)
    x, ctx_4096, mask_1x1xSxS2_ff0 = _rec_inputs()

    def _L0_xattn_setup():
        import jax, jax.numpy as jnp
        import numpy as np
        B, Q, K, D = (1, 128, 6404, 512)
        H, KVH, HD = (32, 8, 128)
        GROUPS = H // KVH
        EPS = 1e-05

        def _rmsnorm(x, w):
            xf = x.astype(jnp.float32)
            var = jnp.mean(xf * xf, axis=-1, keepdims=True)
            return (xf * jax.lax.rsqrt(var + EPS)).astype(x.dtype) * w
        key = jax.random.key(seed)
        ks = jax.random.split(key, 8)
        s = 0.02
        return {'hidden_states': jax.random.normal(ks[0], (B, Q, D), jnp.float32), 'cross_attention_states': jax.random.normal(ks[1], (B, K, D), jnp.float32), 'attention_mask': jnp.zeros((B, 1, Q, K), jnp.float32), 'Wq': jax.random.normal(ks[2], (H * HD, D), jnp.float32) * s, 'Wk': jax.random.normal(ks[3], (KVH * HD, D), jnp.float32) * s, 'Wv': jax.random.normal(ks[4], (KVH * HD, D), jnp.float32) * s, 'Wo': jax.random.normal(ks[5], (D, H * HD), jnp.float32) * s, 'q_norm_w': jnp.ones((HD,), jnp.float32), 'k_norm_w': jnp.ones((HD,), jnp.float32)}
    _L0_xattn_all = _L0_xattn_setup()
    _L0_xattn_in = {k: v for k, v in _L0_xattn_all.items() if k in ('Wq', 'Wk', 'Wv', 'Wo', 'q_norm_w', 'k_norm_w')}
    del _L0_xattn_all

    def _L0_ffn_setup():
        import jax, jax.numpy as jnp
        import numpy as np
        RMS_EPS = 1e-05
        key = jax.random.key(seed)
        k1, k2, k3, k4 = jax.random.split(key, 4)
        B, S, H, I = (1, 256, 512, 1792)
        x = jax.random.normal(k1, (B, S, H), dtype=jnp.float32)
        ln_w = jnp.ones((H,), dtype=jnp.float32)
        gate_w = jax.random.normal(k2, (I, H), dtype=jnp.float32) * 0.02
        up_w = jax.random.normal(k3, (I, H), dtype=jnp.float32) * 0.02
        down_w = jax.random.normal(k4, (H, I), dtype=jnp.float32) * 0.02
        return {'x': x, 'ln_w': ln_w, 'gate_w': gate_w, 'up_w': up_w, 'down_w': down_w}
    _L0_ffn_all = _L0_ffn_setup()
    _L0_ffn_in = {k: v for k, v in _L0_ffn_all.items() if k in ('ln_w', 'gate_w', 'up_w', 'down_w')}
    del _L0_ffn_all

    def _L1_xattn_setup():
        import jax, jax.numpy as jnp
        import numpy as np
        DIM = 512
        NUM_HEADS = 32
        NUM_KV_HEADS = 8
        HEAD_DIM = DIM // NUM_HEADS
        KV_DIM = DIM // (NUM_HEADS // NUM_KV_HEADS)
        B, S = (1, 256)
        key = jax.random.key(seed)
        ks = jax.random.split(key, 7)
        w_scale = DIM ** (-0.5)
        return {'query': jax.random.normal(ks[0], (B, S, DIM), jnp.float32), 'key': jax.random.normal(ks[1], (B, S, DIM), jnp.float32), 'value': jax.random.normal(ks[2], (B, S, DIM), jnp.float32), 'Wq': jax.random.normal(ks[3], (DIM, DIM), jnp.float32) * w_scale, 'Wk': jax.random.normal(ks[4], (DIM, KV_DIM), jnp.float32) * w_scale, 'Wv': jax.random.normal(ks[5], (DIM, KV_DIM), jnp.float32) * w_scale, 'Wo': jax.random.normal(ks[6], (DIM, DIM), jnp.float32) * w_scale}
    _L1_xattn_all = _L1_xattn_setup()
    _L1_xattn_in = {k: v for k, v in _L1_xattn_all.items() if k in ('Wq', 'Wk', 'Wv', 'Wo')}
    del _L1_xattn_all

    def _L1_ffn_setup():
        import jax, jax.numpy as jnp
        import numpy as np
        R = 16
        ALPHA = 32
        SCALING = ALPHA / R
        E = 8
        TOP_K = 2
        key = jax.random.key(seed)
        ks = jax.random.split(key, 5)
        B, S, D = (4, 256, 512)
        x = jax.random.normal(ks[0], (B, S, D), dtype=jnp.float32)
        base_W = jax.random.normal(ks[1], (D, D), dtype=jnp.float32) * 0.02
        router_W = jax.random.normal(ks[2], (E, D), dtype=jnp.float32) * 0.02
        lora_A = jax.random.normal(ks[3], (E, D, R), dtype=jnp.float32) * 0.02
        lora_B = jax.random.normal(ks[4], (E, R, D), dtype=jnp.float32) * 0.02
        return {'x': x, 'base_W': base_W, 'router_W': router_W, 'lora_A': lora_A, 'lora_B': lora_B}
    _L1_ffn_all = _L1_ffn_setup()
    _L1_ffn_in = {k: v for k, v in _L1_ffn_all.items() if k in ('base_W', 'router_W', 'lora_A', 'lora_B')}
    del _L1_ffn_all

    def _L2_xattn_setup():
        import jax, jax.numpy as jnp
        import numpy as np
        import math
        HIDDEN = 512
        N_HEADS = 32
        HEAD_DIM = 128
        N_KV_HEADS = 4
        N_GROUPS = N_HEADS // N_KV_HEADS
        key = jax.random.key(seed)
        ks = jax.random.split(key, 6)
        B, NL, S = (8, 64, 512)
        latents = jax.random.normal(ks[0], (B, NL, HIDDEN), dtype=jnp.float32)
        context = jax.random.normal(ks[1], (B, S, HIDDEN), dtype=jnp.float32)
        scale = 1.0 / math.sqrt(HIDDEN)
        Wq = jax.random.normal(ks[2], (HIDDEN, N_HEADS * HEAD_DIM), dtype=jnp.float32) * scale
        Wk = jax.random.normal(ks[3], (HIDDEN, N_KV_HEADS * HEAD_DIM), dtype=jnp.float32) * scale
        Wv = jax.random.normal(ks[4], (HIDDEN, N_KV_HEADS * HEAD_DIM), dtype=jnp.float32) * scale
        Wo = jax.random.normal(ks[5], (N_HEADS * HEAD_DIM, HIDDEN), dtype=jnp.float32) * scale
        return {'latents': latents, 'context': context, 'Wq': Wq, 'Wk': Wk, 'Wv': Wv, 'Wo': Wo}
    _L2_xattn_all = _L2_xattn_setup()
    _L2_xattn_in = {k: v for k, v in _L2_xattn_all.items() if k in ('Wq', 'Wk', 'Wv', 'Wo')}
    del _L2_xattn_all

    def _L2_ffn_setup():
        import jax, jax.numpy as jnp
        import numpy as np
        BLOCK = 32
        WBITS = 4
        ABITS = 16

        def _ste(x, dq):
            return x + jax.lax.stop_gradient(dq - x)

        def block_qdq_weight(w, block=BLOCK, bits=WBITS):
            out_f, in_f = w.shape
            wb = w.reshape(out_f, in_f // block, block)
            qmax = 2 ** (bits - 1) - 1
            scale = jnp.maximum(jnp.max(jnp.abs(wb), axis=-1, keepdims=True) / qmax, 1e-12)
            wq = jnp.clip(jnp.round(wb / scale), -qmax - 1, qmax) * scale
            return _ste(w, wq.reshape(out_f, in_f))

        def act_qdq(x, bits=ABITS):
            qmax = 2 ** bits - 1
            mn = jnp.minimum(jnp.min(x), 0.0)
            mx = jnp.maximum(jnp.max(x), 0.0)
            scale = jnp.maximum((mx - mn) / qmax, 1e-12)
            zp = jnp.clip(jnp.round(-mn / scale), 0, qmax)
            q = jnp.clip(jnp.round(x / scale) + zp, 0, qmax)
            return _ste(x, (q - zp) * scale)

        def fixed_qdq(x, scale, zp=0.0, bits=ABITS):
            qmax = 2 ** bits - 1
            q = jnp.clip(jnp.round(x / scale) + zp, 0, qmax)
            return _ste(x, (q - zp) * scale)
        key = jax.random.key(seed)
        k1, k2, k3, k4 = jax.random.split(key, 4)
        H, I = (512, 1376)
        x = jax.random.normal(k1, (2, 256, H), dtype=jnp.float32)
        w_gate = jax.random.normal(k2, (I, H), dtype=jnp.float32) * H ** (-0.5)
        w_up = jax.random.normal(k3, (I, H), dtype=jnp.float32) * H ** (-0.5)
        w_down = jax.random.normal(k4, (H, I), dtype=jnp.float32) * I ** (-0.5)
        return {'x': x, 'w_gate': w_gate, 'w_up': w_up, 'w_down': w_down}
    _L2_ffn_all = _L2_ffn_setup()
    _L2_ffn_in = {k: v for k, v in _L2_ffn_all.items() if k in ('w_gate', 'w_up', 'w_down')}
    del _L2_ffn_all

    def _L3_xattn_setup():
        import jax, jax.numpy as jnp
        import numpy as np
        TEXT_DIM = 512
        FEATURE_DIM = 512

        def _xavier_uniform(key, shape):
            fan_in, fan_out = (shape[1], shape[0])
            limit = float(np.sqrt(6.0 / (fan_in + fan_out)))
            return jax.random.uniform(key, shape, jnp.float32, -limit, limit)
        key = jax.random.key(seed)
        k1, k2, k3, k4 = jax.random.split(key, 4)
        text = jax.random.normal(k1, (8, 256, TEXT_DIM), jnp.float32)
        features = jax.random.normal(k2, (8, 72, FEATURE_DIM), jnp.float32)
        Wq = _xavier_uniform(k3, (FEATURE_DIM, TEXT_DIM))
        bq = jnp.zeros((FEATURE_DIM,), jnp.float32)
        Wk = _xavier_uniform(k4, (FEATURE_DIM, FEATURE_DIM))
        bk = jnp.zeros((FEATURE_DIM,), jnp.float32)
        return {'text': text, 'features': features, 'Wq': Wq, 'bq': bq, 'Wk': Wk, 'bk': bk}
    _L3_xattn_all = _L3_xattn_setup()
    _L3_xattn_in = {k: v for k, v in _L3_xattn_all.items() if k in ('Wq', 'bq', 'Wk', 'bk')}
    del _L3_xattn_all

    def _L3_ffn_setup():
        import jax, jax.numpy as jnp
        import numpy as np
        N_STREAMS = 4
        DIM = 128
        SINKHORN_ITERS = 50
        SINKHORN_TAU = 0.1
        RMS_EPS = 1.1920929e-07

        def sinkhorn_log(logits, num_iters=SINKHORN_ITERS, tau=SINKHORN_TAU):
            Z = logits / tau
            u0 = jnp.zeros(Z.shape[:-1], Z.dtype)
            v0 = jnp.zeros_like(u0)

            def step(carry, _):
                u, v = carry
                u = -jax.nn.logsumexp(Z + v[..., None, :], axis=-1)
                v = -jax.nn.logsumexp(Z + u[..., :, None], axis=-2)
                return ((u, v), None)
            (u, v), _ = jax.lax.scan(step, (u0, v0), None, length=num_iters)
            return jnp.exp(Z + u[..., :, None] + v[..., None, :])
        key = jax.random.key(seed)
        ks = jax.random.split(key, 6)
        B, T = (4, 256)
        n, C = (N_STREAMS, DIM)
        wd = n * C
        x = jax.random.normal(ks[0], (B, T, wd), dtype=jnp.float32)
        W_res = 0.01 * jax.random.normal(ks[1], (n * n, wd), dtype=jnp.float32)
        W_pre = 0.01 * jax.random.normal(ks[2], (n, wd), dtype=jnp.float32)
        W_post = 0.01 * jax.random.normal(ks[3], (n, wd), dtype=jnp.float32)
        H_res_base = jnp.full((n, n), -0.5, dtype=jnp.float32)
        H_res_base = H_res_base.at[jnp.arange(n), jnp.arange(n)].set(0.0)
        H_pre_base = jnp.zeros((n,), dtype=jnp.float32).at[0].set(1.0)
        H_post_base = jnp.zeros((n,), dtype=jnp.float32)
        gate = jnp.array([5.0], dtype=jnp.float32)
        W_branch = 1.0 / np.sqrt(C) * jax.random.normal(ks[4], (C, C), dtype=jnp.float32)
        return {'x': x, 'W_res': W_res, 'W_pre': W_pre, 'W_post': W_post, 'H_res_base': H_res_base, 'H_pre_base': H_pre_base, 'H_post_base': H_post_base, 'gate': gate, 'W_branch': W_branch}
    _L3_ffn_all = _L3_ffn_setup()
    _L3_ffn_in = {k: v for k, v in _L3_ffn_all.items() if k in ('W_res', 'W_pre', 'W_post', 'H_res_base', 'H_pre_base', 'H_post_base', 'gate', 'W_branch')}
    del _L3_ffn_all
    return {'x': x, 'ctx_4096': ctx_4096, 'mask_1x1xSxS2_ff0': mask_1x1xSxS2_ff0, 'L0_xattn_Wq': _L0_xattn_in['Wq'], 'L0_xattn_Wk': _L0_xattn_in['Wk'], 'L0_xattn_Wv': _L0_xattn_in['Wv'], 'L0_xattn_Wo': _L0_xattn_in['Wo'], 'L0_xattn_q_norm_w': _L0_xattn_in['q_norm_w'], 'L0_xattn_k_norm_w': _L0_xattn_in['k_norm_w'], 'L0_ffn_ln_w': _L0_ffn_in['ln_w'], 'L0_ffn_gate_w': _L0_ffn_in['gate_w'], 'L0_ffn_up_w': _L0_ffn_in['up_w'], 'L0_ffn_down_w': _L0_ffn_in['down_w'], 'L1_xattn_Wq': _L1_xattn_in['Wq'], 'L1_xattn_Wk': _L1_xattn_in['Wk'], 'L1_xattn_Wv': _L1_xattn_in['Wv'], 'L1_xattn_Wo': _L1_xattn_in['Wo'], 'L1_ffn_base_W': _L1_ffn_in['base_W'], 'L1_ffn_router_W': _L1_ffn_in['router_W'], 'L1_ffn_lora_A': _L1_ffn_in['lora_A'], 'L1_ffn_lora_B': _L1_ffn_in['lora_B'], 'L2_xattn_Wq': _L2_xattn_in['Wq'], 'L2_xattn_Wk': _L2_xattn_in['Wk'], 'L2_xattn_Wv': _L2_xattn_in['Wv'], 'L2_xattn_Wo': _L2_xattn_in['Wo'], 'L2_ffn_w_gate': _L2_ffn_in['w_gate'], 'L2_ffn_w_up': _L2_ffn_in['w_up'], 'L2_ffn_w_down': _L2_ffn_in['w_down'], 'L3_xattn_Wq': _L3_xattn_in['Wq'], 'L3_xattn_bq': _L3_xattn_in['bq'], 'L3_xattn_Wk': _L3_xattn_in['Wk'], 'L3_xattn_bk': _L3_xattn_in['bk'], 'L3_ffn_W_res': _L3_ffn_in['W_res'], 'L3_ffn_W_pre': _L3_ffn_in['W_pre'], 'L3_ffn_W_post': _L3_ffn_in['W_post'], 'L3_ffn_H_res_base': _L3_ffn_in['H_res_base'], 'L3_ffn_H_pre_base': _L3_ffn_in['H_pre_base'], 'L3_ffn_H_post_base': _L3_ffn_in['H_post_base'], 'L3_ffn_gate': _L3_ffn_in['gate'], 'L3_ffn_W_branch': _L3_ffn_in['W_branch']}

def reference(x, ctx_4096, mask_1x1xSxS2_ff0, L0_xattn_Wq, L0_xattn_Wk, L0_xattn_Wv, L0_xattn_Wo, L0_xattn_q_norm_w, L0_xattn_k_norm_w, L0_ffn_ln_w, L0_ffn_gate_w, L0_ffn_up_w, L0_ffn_down_w, L1_xattn_Wq, L1_xattn_Wk, L1_xattn_Wv, L1_xattn_Wo, L1_ffn_base_W, L1_ffn_router_W, L1_ffn_lora_A, L1_ffn_lora_B, L2_xattn_Wq, L2_xattn_Wk, L2_xattn_Wv, L2_xattn_Wo, L2_ffn_w_gate, L2_ffn_w_up, L2_ffn_w_down, L3_xattn_Wq, L3_xattn_bq, L3_xattn_Wk, L3_xattn_bk, L3_ffn_W_res, L3_ffn_W_pre, L3_ffn_W_post, L3_ffn_H_res_base, L3_ffn_H_pre_base, L3_ffn_H_post_base, L3_ffn_gate, L3_ffn_W_branch):
    import jax
    import jax.numpy as jnp

    def _L0_xattn_ref(hidden_states, cross_attention_states, attention_mask, Wq, Wk, Wv, Wo, q_norm_w, k_norm_w):
        import jax, jax.numpy as jnp
        import numpy as np
        B, Q, K, D = (1, 128, 6404, 512)
        H, KVH, HD = (32, 8, 128)
        GROUPS = H // KVH
        EPS = 1e-05

        def _rmsnorm(x, w):
            xf = x.astype(jnp.float32)
            var = jnp.mean(xf * xf, axis=-1, keepdims=True)
            return (xf * jax.lax.rsqrt(var + EPS)).astype(x.dtype) * w
        bsz, q_len, _ = hidden_states.shape
        kv_len = cross_attention_states.shape[1]
        q = (hidden_states @ Wq.T).reshape(bsz, q_len, H, HD).transpose(0, 2, 1, 3)
        k = (cross_attention_states @ Wk.T).reshape(bsz, kv_len, KVH, HD).transpose(0, 2, 1, 3)
        v = (cross_attention_states @ Wv.T).reshape(bsz, kv_len, KVH, HD).transpose(0, 2, 1, 3)
        q = _rmsnorm(q, q_norm_w)
        k = jnp.repeat(k, GROUPS, axis=1)
        v = jnp.repeat(v, GROUPS, axis=1)
        k = _rmsnorm(k, k_norm_w)
        scale = 1.0 / np.sqrt(HD)
        scores = jnp.einsum('bhqd,bhkd->bhqk', q, k) * scale
        scores = scores + attention_mask[:, :, :, :kv_len]
        probs = jax.nn.softmax(scores.astype(jnp.float32), axis=-1).astype(q.dtype)
        out = jnp.einsum('bhqk,bhkd->bhqd', probs, v)
        out = out.transpose(0, 2, 1, 3).reshape(bsz, q_len, H * HD)
        return out @ Wo.T

    def _L0_ffn_ref(x, ln_w, gate_w, up_w, down_w):
        import jax, jax.numpy as jnp
        import numpy as np
        RMS_EPS = 1e-05
        var = jnp.mean(jnp.square(x), axis=-1, keepdims=True)
        nx = x * jax.lax.rsqrt(var + RMS_EPS) * ln_w
        g = jnp.einsum('bsh,ih->bsi', nx, gate_w)
        u = jnp.einsum('bsh,ih->bsi', nx, up_w)
        return jnp.einsum('bsi,hi->bsh', jax.nn.silu(g) * u, down_w)

    def _L1_xattn_ref(query, key, value, Wq, Wk, Wv, Wo):
        import jax, jax.numpy as jnp
        import numpy as np
        DIM = 512
        NUM_HEADS = 32
        NUM_KV_HEADS = 8
        HEAD_DIM = DIM // NUM_HEADS
        KV_DIM = DIM // (NUM_HEADS // NUM_KV_HEADS)
        B, S = (1, 256)
        b, sq, _ = query.shape
        _, sk, _ = key.shape
        rep = NUM_HEADS // NUM_KV_HEADS
        q = (query @ Wq).reshape(b, sq, NUM_HEADS, HEAD_DIM).transpose(0, 2, 1, 3)
        k = (key @ Wk).reshape(b, sk, NUM_KV_HEADS, HEAD_DIM).transpose(0, 2, 1, 3)
        v = (value @ Wv).reshape(b, sk, NUM_KV_HEADS, HEAD_DIM).transpose(0, 2, 1, 3)
        k = jnp.repeat(k, rep, axis=1)
        v = jnp.repeat(v, rep, axis=1)
        scale = HEAD_DIM ** (-0.5)
        scores = jnp.einsum('bhqd,bhkd->bhqk', q, k) * scale
        probs = jax.nn.softmax(scores, axis=-1)
        out = jnp.einsum('bhqk,bhkd->bhqd', probs, v)
        out = out.transpose(0, 2, 1, 3).reshape(b, sq, DIM)
        return out @ Wo

    def _L1_ffn_ref(x, base_W, router_W, lora_A, lora_B):
        import jax, jax.numpy as jnp
        import numpy as np
        R = 16
        ALPHA = 32
        SCALING = ALPHA / R
        E = 8
        TOP_K = 2
        base = jnp.einsum('bsd,od->bso', x, base_W)
        logits = jnp.einsum('bsd,ed->bse', x, router_W)
        probs = jax.nn.softmax(logits.astype(jnp.float32), axis=-1)
        top_vals, top_idx = jax.lax.top_k(probs, TOP_K)
        rw = top_vals / jnp.sum(top_vals, axis=-1, keepdims=True)
        w_dense = jnp.sum(jax.nn.one_hot(top_idx, E, dtype=rw.dtype) * rw[..., None], axis=-2).astype(x.dtype)
        mid = jnp.einsum('bsd,edr->bser', x, lora_A)
        mid = mid * w_dense[..., None]
        inc = jnp.einsum('bser,erd->bsd', mid, lora_B)
        return base + inc * SCALING

    def _L2_xattn_ref(latents, context, Wq, Wk, Wv, Wo):
        import jax, jax.numpy as jnp
        import numpy as np
        import math
        HIDDEN = 512
        N_HEADS = 32
        HEAD_DIM = 128
        N_KV_HEADS = 4
        N_GROUPS = N_HEADS // N_KV_HEADS
        b, q_len, _ = latents.shape
        kv_len = q_len + context.shape[1]
        hidden_states = jnp.concatenate([context, latents], axis=1)
        q = (latents @ Wq).reshape(b, q_len, N_KV_HEADS, N_GROUPS, HEAD_DIM)
        k = (hidden_states @ Wk).reshape(b, kv_len, N_KV_HEADS, HEAD_DIM)
        v = (hidden_states @ Wv).reshape(b, kv_len, N_KV_HEADS, HEAD_DIM)
        scale = 1.0 / math.sqrt(HEAD_DIM)
        scores = jnp.einsum('bqhgd,bkhd->bhgqk', q, k) * scale
        attn = jax.nn.softmax(scores.astype(jnp.float32), axis=-1).astype(q.dtype)
        out = jnp.einsum('bhgqk,bkhd->bqhgd', attn, v)
        out = out.reshape(b, q_len, N_HEADS * HEAD_DIM)
        return out @ Wo

    def _L2_ffn_ref(x, w_gate, w_up, w_down):
        import jax, jax.numpy as jnp
        import numpy as np
        BLOCK = 32
        WBITS = 4
        ABITS = 16

        def _ste(x, dq):
            return x + jax.lax.stop_gradient(dq - x)

        def block_qdq_weight(w, block=BLOCK, bits=WBITS):
            out_f, in_f = w.shape
            wb = w.reshape(out_f, in_f // block, block)
            qmax = 2 ** (bits - 1) - 1
            scale = jnp.maximum(jnp.max(jnp.abs(wb), axis=-1, keepdims=True) / qmax, 1e-12)
            wq = jnp.clip(jnp.round(wb / scale), -qmax - 1, qmax) * scale
            return _ste(w, wq.reshape(out_f, in_f))

        def act_qdq(x, bits=ABITS):
            qmax = 2 ** bits - 1
            mn = jnp.minimum(jnp.min(x), 0.0)
            mx = jnp.maximum(jnp.max(x), 0.0)
            scale = jnp.maximum((mx - mn) / qmax, 1e-12)
            zp = jnp.clip(jnp.round(-mn / scale), 0, qmax)
            q = jnp.clip(jnp.round(x / scale) + zp, 0, qmax)
            return _ste(x, (q - zp) * scale)

        def fixed_qdq(x, scale, zp=0.0, bits=ABITS):
            qmax = 2 ** bits - 1
            q = jnp.clip(jnp.round(x / scale) + zp, 0, qmax)
            return _ste(x, (q - zp) * scale)
        sigmoid_scale = 1.0 / 65536.0
        wg = block_qdq_weight(w_gate)
        wu = block_qdq_weight(w_up)
        wd = block_qdq_weight(w_down)
        xq = act_qdq(x)
        up = act_qdq(jnp.einsum('bsh,ih->bsi', xq, wu))
        gate = act_qdq(jnp.einsum('bsh,ih->bsi', xq, wg))
        sig = fixed_qdq(jax.nn.sigmoid(gate), sigmoid_scale)
        gate = act_qdq(gate * sig)
        o = act_qdq(gate * up)
        return jnp.einsum('bsi,hi->bsh', o, wd)

    def _L3_xattn_ref(text, features, Wq, bq, Wk, bk):
        import jax, jax.numpy as jnp
        import numpy as np
        TEXT_DIM = 512
        FEATURE_DIM = 512

        def _xavier_uniform(key, shape):
            fan_in, fan_out = (shape[1], shape[0])
            limit = float(np.sqrt(6.0 / (fan_in + fan_out)))
            return jax.random.uniform(key, shape, jnp.float32, -limit, limit)
        Q = jnp.einsum('btx,dx->btd', text, Wq) + bq
        K = jnp.einsum('bpx,dx->bpd', features, Wk) + bk
        scale = 1.0 / jnp.sqrt(jnp.asarray(K.shape[-1], K.dtype))
        scores = jnp.einsum('btd,bpd->btp', Q, K) * scale
        attn = jax.nn.softmax(scores, axis=-1)
        attended = jnp.einsum('btp,bpd->btd', attn, features)
        return attended

    def _L3_ffn_ref(x, W_res, W_pre, W_post, H_res_base, H_pre_base, H_post_base, gate, W_branch):
        import jax, jax.numpy as jnp
        import numpy as np
        N_STREAMS = 4
        DIM = 128
        SINKHORN_ITERS = 50
        SINKHORN_TAU = 0.1
        RMS_EPS = 1.1920929e-07

        def sinkhorn_log(logits, num_iters=SINKHORN_ITERS, tau=SINKHORN_TAU):
            Z = logits / tau
            u0 = jnp.zeros(Z.shape[:-1], Z.dtype)
            v0 = jnp.zeros_like(u0)

            def step(carry, _):
                u, v = carry
                u = -jax.nn.logsumexp(Z + v[..., None, :], axis=-1)
                v = -jax.nn.logsumexp(Z + u[..., :, None], axis=-2)
                return ((u, v), None)
            (u, v), _ = jax.lax.scan(step, (u0, v0), None, length=num_iters)
            return jnp.exp(Z + u[..., :, None] + v[..., None, :])
        B, T, nC = x.shape
        n = N_STREAMS
        C = nC // n
        x_norm = x * jax.lax.rsqrt(jnp.mean(x * x, axis=-1, keepdims=True) + RMS_EPS)
        H_res_logits = (x_norm @ W_res.T).reshape(B, T, n, n) + H_res_base
        H_pre_logits = x_norm @ W_pre.T + H_pre_base
        H_post_logits = x_norm @ W_post.T + H_post_base
        H_res = sinkhorn_log(H_res_logits)
        H_pre = jax.nn.softmax(H_pre_logits, axis=-1)
        H_post = jax.nn.softmax(H_post_logits, axis=-1)
        g = jax.nn.sigmoid(gate)[0]
        I = jnp.eye(n, dtype=H_res.dtype)
        H_res = (1.0 - g) * I + g * H_res
        x_streams = x.reshape(B, T, n, C)
        x_pre = jnp.einsum('btnc,btn->btc', x_streams, H_pre)
        y = x_pre @ W_branch
        x_mixed = jnp.einsum('btij,btjc->btic', H_res, x_streams)
        y_distributed = jnp.einsum('btc,btn->btnc', y, H_post)
        return (x_mixed + y_distributed).reshape(B, T, nC)
    x = x + _L0_xattn_ref(_layernorm(x, axis=-1), ctx_4096, mask_1x1xSxS2_ff0, L0_xattn_Wq, L0_xattn_Wk, L0_xattn_Wv, L0_xattn_Wo, L0_xattn_q_norm_w, L0_xattn_k_norm_w)
    x = x + _L0_ffn_ref(_layernorm(x, axis=-1), L0_ffn_ln_w, L0_ffn_gate_w, L0_ffn_up_w, L0_ffn_down_w)
    x = x + _L1_xattn_ref(_layernorm(x, axis=-1), ctx_4096, ctx_4096, L1_xattn_Wq, L1_xattn_Wk, L1_xattn_Wv, L1_xattn_Wo)
    x = x + _L1_ffn_ref(_layernorm(x, axis=-1), L1_ffn_base_W, L1_ffn_router_W, L1_ffn_lora_A, L1_ffn_lora_B)
    x = x + _L2_xattn_ref(_layernorm(x, axis=-1), ctx_4096, L2_xattn_Wq, L2_xattn_Wk, L2_xattn_Wv, L2_xattn_Wo)
    x = x + _L2_ffn_ref(_layernorm(x, axis=-1), L2_ffn_w_gate, L2_ffn_w_up, L2_ffn_w_down)
    x = x + _L3_xattn_ref(_layernorm(x, axis=-1), ctx_4096, L3_xattn_Wq, L3_xattn_bq, L3_xattn_Wk, L3_xattn_bk)
    x = x + _L3_ffn_ref(_layernorm(x, axis=-1), L3_ffn_W_res, L3_ffn_W_pre, L3_ffn_W_post, L3_ffn_H_res_base, L3_ffn_H_pre_base, L3_ffn_H_post_base, L3_ffn_gate, L3_ffn_W_branch)
    return x

_drawn_inputs = setup_inputs


def setup_inputs(seed=0):
    import zlib

    import numpy as np

    out = dict(_drawn_inputs(seed))
    spreads = {'L0_xattn_q_norm_w': (1.0, 0.6),
     'L0_xattn_k_norm_w': (1.0, 0.6),
     'L0_ffn_ln_w': (1.0, 0.6),
     'L3_xattn_bq': (0.0, 0.8),
     'L3_xattn_bk': (0.0, 2.0),
     'L3_ffn_H_post_base': (0.0, 2.0)}
    factors = {'L3_ffn_W_pre': 6.194, 'L3_ffn_W_post': 6.262}
    for name, (base, spread) in spreads.items():
        noise = np.random.default_rng([zlib.crc32(name.encode()), seed]).standard_normal(out[name].shape)
        drawn = base * np.exp(spread * noise) if base else spread * noise
        out[name] = jnp.asarray(drawn.astype(out[name].dtype))
    for name, factor in factors.items():
        out[name] = (out[name] * factor).astype(out[name].dtype)
    return out
```

```python
from contextlib import ExitStack

import numpy as np

import concourse.bass as bass
from concourse import mybir

F32 = mybir.dt.float32
F32R = mybir.dt.float32r
ALU = mybir.AluOpType
ACT = mybir.ActivationFunctionType
AX = mybir.AxisListType

P = 128
NB = 8
TOK = NB * P
D = 512
KC = D // P
HALF = TOK // 2
LN_EPS = 1e-5
RMS3_EPS = 1.1920929e-07
BIG_HEADS = 32
QUAD = 4
ROUND = 1.5 * 2.0 ** 23


def nth(turn, per_turn, n):
    return turn * per_turn + n


def primed(turn, per_turn, n):
    return turn * per_turn + n + 1


def f32(ap):
    return ap.bitcast(F32)


def mm3(pe, out, stationary, moving, first, last):
    (sh, sl), (mh, ml) = stationary, moving
    pe.matmul(out, sh, mh, start=first, stop=False)
    pe.matmul(out, sh, ml, start=False, stop=False)
    return pe.matmul(out, sl, mh, start=False, stop=last)


class Named:
    pass


class Scope:

    def __init__(self, nc, M, ctx, prefix):
        self.nc, self.M, self.ctx, self.prefix = nc, M, ctx, prefix
        self.primed = False

    def sb(self, name, shape, dtype=F32):
        return self.ctx.enter_context(self.nc.sbuf_tensor(f"{self.prefix}_{name}", shape, dtype))

    def pair(self, name, shape):
        return self.sb(name + "_hi", shape, F32R), self.sb(name + "_lo", shape, F32R)

    def sems(self, names, primed=False):
        sems = [self.nc.alloc_semaphore(name=f"{self.prefix}_{n}") for n in names.split()]
        self.M.used_semaphores.extend(sems)
        for sem in sems if primed else []:
            self.nc.gpsimd.sem_inc(sem, 1)
            self.primed = True
        return sems

    def block(self):
        if self.primed:
            self.nc.all_engine_barrier()
        return self.ctx.enter_context(self.nc.Block())


def clear_semaphores(nc, M):
    nc.clear_and_free_semaphores(list(M.used_semaphores))
    M.used_semaphores.clear()
    nc.all_engine_barrier()


def part(pair, *index):
    return pair[0][index], pair[1][index]


def tile_of(b):
    return slice(b * P, (b + 1) * P)



def load_stage(nc, M, A, name, x=None):
    with ExitStack() as ctx:
        S = Scope(nc, M, ctx, name)
        raw = S.sb("raw", [P, KC, TOK])
        s = Named()
        s.x_loaded, s.ctx_loaded, s.zeroed, s.made, s.hi_made = S.sems("x_loaded ctx_loaded zeroed made hi_made")
        block = S.block()

        @block.sync
        def _(sp):
            if x is not None:
                sp.dma_start(M.x[:], x.rearrange("b p d -> p b d")).then_inc(s.x_loaded, 16)
            sp.dma_start(raw[:], A["ctxT"].rearrange("(c p) t -> p c t", p=P)).then_inc(s.ctx_loaded, 16)
            if x is not None:
                sp.wait_ge(s.x_loaded, 16)

        @block.gpsimd
        def _(pool):
            if x is None:
                return
            pool.memset(M.ident[:], 0.0).then_inc(s.zeroed, 1)
            pool.memset(M.neg_half[:], -0.5).then_inc(s.zeroed, 1)
            pool.memset(M.eps[:], LN_EPS).then_inc(s.zeroed, 1)
            pool.wait_ge(s.zeroed, 3)
            pool.affine_select(out=M.ident[:], in_=M.ident[:], compare_op=ALU.not_equal, fill=1.0,
                               base=0, pattern=[[-1, P]], channel_multiplier=1).then_inc(s.made, 1)

        @block.scalar
        def _(act):
            act.wait_ge(s.ctx_loaded, 16)
            for c in range(KC):
                act.activation(M.cT[0][:, c, :], raw[:, c, :], ACT.Copy).then_inc(s.hi_made, 1)

        @block.vector
        def _(dve):
            dve.wait_ge(s.ctx_loaded, 16)
            for c in range(KC):
                dve.wait_ge(s.hi_made, c + 1)
                dve.tensor_tensor(M.cT[1][:, c, :], raw[:, c, :], f32(M.cT[0][:, c, :]), ALU.subtract)



def norm_stage(nc, M, name, rms_eps=None, feature_scale=None, load_scale=None, keep_rms=None, xn=None,
               normalize=True, turn=True):
    with ExitStack() as ctx:
        S = Scope(nc, M, ctx, name)
        s = Named()
        s.stats, s.aggregated, s.pow_step, s.rstd_ready = S.sems("stats aggregated pow_step rstd_ready")
        s.normed, s.turned, s.hi_made, s.split, s.scale_loaded = S.sems("normed turned hi_made split scale_loaded")
        xn = xn if xn is not None else S.sb("xn", [P, NB, D])
        stats = S.sb("stats", [P, NB, 6])
        mv = S.sb("mv", [P, NB, 2])
        shifted = S.sb("shifted", [P, NB])
        rstd = S.sb("rstd", [P, NB])
        sq = S.sb("sq", [P, NB])
        rms = keep_rms if keep_rms is not None else S.sb("rms", [P, NB])
        both = S.sb("both", [P, NB])
        factor = both if rms_eps is not None and keep_rms is None else rstd
        bank = [M.bank[i] for i in range(4)]
        block = S.block()

        if feature_scale is not None:
            @block.sync
            def _(sp):
                sp.dma_start(feature_scale[:], load_scale).then_inc(s.scale_loaded, 16)

        @block.gpsimd
        def _(pool):
            steps = [0]

            def step(ins):
                ins.then_inc(s.pow_step, 1)
                steps[0] += 1
                pool.wait_ge(s.pow_step, steps[0])

            if not normalize:
                return
            pool.wait_ge(s.aggregated, NB)
            step(pool.tensor_scalar(shifted[:], mv[:, :, 1], LN_EPS, None, ALU.add))
            step(pool.tensor_tensor(rstd[:], shifted[:], M.neg_half[:, 0:NB], ALU.pow))
            if rms_eps is not None:
                step(pool.tensor_tensor(sq[:], rstd[:], rstd[:], ALU.mult))
                step(pool.tensor_tensor(sq[:], sq[:], mv[:, :, 1], ALU.mult))
                step(pool.tensor_scalar(sq[:], sq[:], rms_eps, None, ALU.add))
                step(pool.tensor_tensor(rms[:], sq[:], M.neg_half[:, 0:NB], ALU.pow))
            pool.tensor_tensor(both[:], rstd[:], rms[:] if rms_eps is not None else rstd[:],
                               ALU.mult).then_inc(s.rstd_ready, 1)

        @block.vector
        def _(dve):
            if normalize:
                for b in range(NB):
                    dve.bn_stats(stats[:, b, :], M.x[:, b, :]).then_inc(s.stats, 1)
                for b in range(NB):
                    dve.wait_ge(s.stats, b + 1)
                    dve.bn_aggr(mv[:, b, :], stats[:, b, :]).then_inc(s.aggregated, 1)
                dve.wait_ge(s.aggregated, NB)
                dve.wait_ge(s.rstd_ready, 1)
                for b in range(NB):
                    dve.tensor_scalar(xn[:, b, :], M.x[:, b, :], mv[:, b, 0:1], factor[:, b:b + 1],
                                      ALU.subtract, ALU.mult).then_inc(s.normed, 1)
            if not turn:
                return
            if feature_scale is not None:
                dve.wait_ge(s.scale_loaded, 16)
            for b in range(NB):
                dve.wait_ge(s.hi_made, b + 1)
                if feature_scale is None:
                    dve.tensor_tensor(M.nT[1][:, :, tile_of(b)],
                                      bank[b % 4].rearrange("p (c t) -> p c t", c=KC),
                                      f32(M.nT[0][:, :, tile_of(b)]), ALU.subtract).then_inc(s.split, 1)
                    continue
                for c in range(KC):
                    last = dve.scalar_tensor_tensor(
                        out=M.nT[1][:, c, tile_of(b)], in0=bank[b % 4][:, tile_of(c)],
                        scalar=feature_scale[:, c:c + 1], in1=f32(M.nT[0][:, c, tile_of(b)]),
                        op0=ALU.mult, op1=ALU.subtract)
                last.then_inc(s.split, 1)

        @block.tensor
        def _(pe):
            if not turn:
                return
            for b in range(NB):
                if normalize:
                    pe.wait_ge(s.normed, b + 1)
                if b >= 4:
                    pe.wait_ge(s.split, b - 3)
                for c in range(KC):
                    last = pe.transpose(bank[b % 4][:, tile_of(c)], xn[:, b, tile_of(c)], M.ident[:])
                last.then_inc(s.turned, 1)

        @block.scalar
        def _(act):
            if not turn:
                return
            if feature_scale is not None:
                act.wait_ge(s.scale_loaded, 16)
            for b in range(NB):
                act.wait_ge(s.turned, b + 1)
                if feature_scale is None:
                    act.activation(M.nT[0][:, :, tile_of(b)],
                                   bank[b % 4].rearrange("p (c t) -> p c t", c=KC),
                                   ACT.Copy).then_inc(s.hi_made, 1)
                    continue
                for c in range(KC):
                    last = act.activation(M.nT[0][:, c, tile_of(b)], bank[b % 4][:, tile_of(c)],
                                          ACT.Copy, scale=feature_scale[:, c:c + 1])
                last.then_inc(s.hi_made, 1)



def attn0_stage(nc, M, A):
    GROUPS, HD = 8, P
    UNITS = 2 * NB
    ALL = GROUPS * NB
    Q_STEPS, O_STEPS = range(1, 1 + KC), range(3, 3 + QUAD)
    ROOT = 1.0 / float(np.sqrt(HD))
    with ExitStack() as ctx:
        S = Scope(nc, M, ctx, "a0")
        raw_kv = S.sb("raw_kv", [P, KC, 2 * HD])
        raw_q = S.sb("raw_q", [P, KC, QUAD * HD])
        raw_o = S.sb("raw_o", [P, QUAD, D])
        w_kv = S.pair("w_kv", [P, KC, 2 * HD])
        w_q = S.pair("w_q", [P, 2, KC, QUAD * HD])
        w_o = S.pair("w_o", [P, 2, QUAD, D])
        norm_w = S.sb("norm_w", [P, 2])
        kq_w = S.sb("kq_w", [P, 1])
        mask = S.sb("mask", [P, P])
        squares = S.sb("squares", [P, P])
        k_meansq = S.sb("k_meansq", [P, 1])
        k_rstd = S.sb("k_rstd", [P, 1])
        q_meansq = S.sb("q_meansq", [P, QUAD])
        q_rstd = S.sb("q_rstd", [P, QUAD])
        k_n = S.sb("k_n", [P, HD])
        q_n = S.sb("q_n", [P, QUAD, HD])
        kT = S.pair("kT", [P, P])
        qT = S.pair("qT", [P, QUAD, P])
        v = S.pair("v", [P, 2, HD])
        probs = S.sb("probs", [P, QUAD, P])
        neg_max = S.sb("neg_max", [P, QUAD])
        sums = S.sb("sums", [P, QUAD])
        inv_sums = S.sb("inv_sums", [P, QUAD])
        pT = S.pair("pT", [P, QUAD * P])
        oT = S.pair("oT", [P, QUAD, P])
        B_Y, B_KV, B_Q, B_QT, B_S, B_PT, B_O, B_KT = M.bank
        s = Named()
        s.kv_loaded, s.q_loaded, s.o_loaded, s.small_loaded = S.sems("kv_loaded q_loaded o_loaded small_loaded")
        s.kq_ready, s.kv_hi, s.q_hi, s.o_hi = S.sems("kq_ready kv_hi q_hi o_hi")
        s.q_turned, s.k_turned, s.scored, s.p_turned, s.pv_made = S.sems("q_turned k_turned scored p_turned pv_made")
        s.k_squared, s.q_squared, s.k_pow, s.q_pow = S.sems("k_squared q_squared k_pow q_pow")
        s.v_hi, s.kT_hi, s.qT_hi, s.max_ready = S.sems("v_hi kT_hi qT_hi max_ready")
        s.exped, s.inverted, s.p_ready, s.pT_hi, s.oT_hi = S.sems("exped inverted p_ready pT_hi oT_hi")
        s.kv_split, s.q_split, s.o_split, s.v_split = S.sems("kv_split q_split o_split v_split", primed=True)
        s.k_normed, s.q_normed, s.kT_split, s.qT_split = S.sems("k_normed q_normed kT_split qT_split", primed=True)
        s.masked, s.pT_split, s.oT_split, s.y_added = S.sems("masked pT_split oT_split y_added", primed=True)
        s.kv_made, s.q_made, s.y_made = S.sems("kv_made q_made y_made", primed=True)
        block = S.block()

        def units_from(i, u):
            return ALL - (UNITS * i + u) if isinstance(i, int) else ALL

        def run(engine, step):
            with engine.Fori(0, GROUPS // 2 - 1) as i:
                for u in range(1, UNITS + 1):
                    step(i, u)
            for u in range(1, UNITS):
                step(GROUPS // 2 - 1, u)

        @block.sync
        def _(sp):
            sp.dma_start(norm_w[:, 0:1], A["L0_xattn_q_norm_w"]).then_inc(s.small_loaded, 16)
            sp.dma_start(norm_w[:, 1:2], A["L0_xattn_k_norm_w"]).then_inc(s.small_loaded, 16)
            sp.dma_start(mask[:], A["mask"]).then_inc(s.small_loaded, 16)
            with sp.Fori(0, GROUPS) as g:
                at = bass.ds(g, 1)
                sp.wait_ge(s.q_split, primed(g, KC, 0))
                sp.dma_start(raw_q[:], A["L0_xattn_Wq"][at].rearrange("g p c n -> (g p) c n")).then_inc(s.q_loaded, 16)
                sp.wait_ge(s.o_split, primed(g, QUAD, 0))
                sp.dma_start(raw_o[:], A["L0_xattn_Wo"][at].rearrange("g p c n -> (g p) c n")).then_inc(s.o_loaded, 16)
                sp.wait_ge(s.kv_split, primed(g, 1, 0))
                sp.dma_start(raw_kv[:], A["L0_xattn_Wkv"][at].rearrange("g p c n -> (g p) c n")).then_inc(s.kv_loaded, 16)

        @block.tensor
        def _(pe):
            def project_kv(i, u):
                if u % NB == 0:
                    pe.wait_ge(s.kv_split, primed(i, 2, u // NB + 1))
                pe.wait_ge(s.v_split, primed(i, UNITS, u))
                pe.wait_ge(s.k_normed, primed(i, UNITS, u))
                for c in range(KC):
                    last = mm3(pe, B_KV[:, 0:2 * HD], part(M.cT, slice(None), c, tile_of(u % NB)),
                               part(w_kv, slice(None), c), c == 0, c == KC - 1)
                last.then_inc(s.kv_made, 1)

            def project_q(i, u, chunks):
                if 0 in chunks:
                    pe.wait_ge(s.q_normed, primed(i, UNITS, u))
                for c in chunks:
                    if u % NB == 0:
                        pe.wait_ge(s.q_split, primed(i, 2 * KC, u // NB * KC + c + 1))
                    last = mm3(pe, B_Q[:], part(M.nT, slice(None), c, tile_of(u % NB)),
                               part(w_q, slice(None), u // NB % 2, c), c == 0, c == KC - 1)
                if KC - 1 in chunks:
                    last.then_inc(s.q_made, 1)

            def turn_kq(i, u):
                pe.wait_ge(s.q_normed, primed(i, UNITS, u + 1))
                pe.wait_ge(s.qT_split, primed(i, UNITS, u))
                for h in range(QUAD):
                    last = pe.transpose(B_QT[:, tile_of(h)], q_n[:, h, :], M.ident[:])
                last.then_inc(s.q_turned, 1)
                pe.wait_ge(s.k_normed, primed(i, UNITS, u + 1))
                pe.wait_ge(s.kT_split, primed(i, UNITS, u))
                pe.transpose(B_KT[:, 0:P], k_n[:], M.ident[:]).then_inc(s.k_turned, 1)

            def score(i, u):
                pe.wait_ge(s.kT_split, primed(i, UNITS, u + 1))
                pe.wait_ge(s.qT_split, primed(i, UNITS, u + 1))
                pe.wait_ge(s.masked, primed(i, UNITS, u))
                for h in range(QUAD):
                    last = mm3(pe, B_S[:, tile_of(h)], part(qT, slice(None), h), (kT[0][:], kT[1][:]), True, True)
                last.then_inc(s.scored, 1)

            def turn_p(i, u):
                pe.wait_ge(s.p_ready, nth(i, UNITS, u + 1))
                pe.wait_ge(s.pT_split, primed(i, UNITS, u))
                for h in range(QUAD):
                    last = pe.transpose(B_PT[:, tile_of(h)], probs[:, h, :], M.ident[:])
                last.then_inc(s.p_turned, 1)

            def weigh_v(i, u):
                pe.wait_ge(s.v_split, primed(i, UNITS, u + 1))
                pe.wait_ge(s.pT_split, primed(i, UNITS, u + 1))
                pe.wait_ge(s.oT_split, primed(i, UNITS, u))
                mm3(pe, B_O[:], part(v, slice(None), u % 2), (pT[0][:], pT[1][:]), True, True).then_inc(s.pv_made, 1)

            def project_out(i, u):
                if u % NB == 0:
                    pe.wait_ge(s.o_split, primed(i, 2 * QUAD, (u // NB + 1) * QUAD))
                pe.wait_ge(s.oT_split, primed(i, UNITS, u + 1))
                pe.wait_ge(s.y_added, primed(i, UNITS, u))
                for h in range(QUAD):
                    last = mm3(pe, B_Y[:], part(oT, slice(None), h), part(w_o, slice(None), u // NB % 2, h),
                               h == 0, h == QUAD - 1)
                last.then_inc(s.y_made, 1)

            def step(i, u, first=False):
                score(i, u)
                if units_from(i, u) > 1:
                    project_kv(i, u + 1)
                if not first:
                    project_out(i, u - 1)
                turn_p(i, u)
                if units_from(i, u) > 1:
                    turn_kq(i, u + 1)
                if units_from(i, u) > 2:
                    project_q(i, u + 2, (0, 1))
                weigh_v(i, u)
                if units_from(i, u) > 2:
                    project_q(i, u + 2, (2, 3))

            project_q(0, 0, (0, 1, 2, 3))
            project_kv(0, 0)
            turn_kq(0, 0)
            project_q(0, 1, (0, 1, 2, 3))
            step(0, 0, first=True)
            run(pe, step)
            project_out(GROUPS // 2 - 1, UNITS - 1)

        @block.scalar
        def _(act):
            def hi_q(i, k, c):
                act.wait_ge(s.q_loaded, nth(i, 32, 16 * (k + 1)))
                act.activation(w_q[0][:, k % 2, c], raw_q[:, c], ACT.Copy).then_inc(s.q_hi, 1)

            def hi_o(i, k, h):
                act.wait_ge(s.o_loaded, nth(i, 32, 16 * (k + 1)))
                act.activation(w_o[0][:, k % 2, h], raw_o[:, h], ACT.Copy).then_inc(s.o_hi, 1)

            def hi_kv(i, k):
                act.wait_ge(s.kv_loaded, nth(i, 32, 16 * (k + 1)))
                act.wait_ge(s.kv_made, primed(i, UNITS, NB * k))
                act.activation(w_kv[0][:], raw_kv[:], ACT.Copy).then_inc(s.kv_hi, 1)

            def read_q(i, u):
                act.wait_ge(s.q_made, primed(i, UNITS, u + 1))
                for h in range(QUAD):
                    if h:
                        act.wait_ge(s.q_squared, nth(i, UNITS * QUAD, QUAD * u + h))
                    act.activation(squares[:], B_Q[:, tile_of(h)], ACT.Square, scale=ROOT,
                                   accum_out=q_meansq[:, h:h + 1]).then_inc(s.q_squared, 1)

            def read_kv(i, u):
                act.wait_ge(s.kv_made, primed(i, UNITS, u + 1))
                act.wait_ge(s.q_squared, nth(i, UNITS * QUAD, QUAD * (u + 1)))
                act.activation(squares[:], B_KV[:, 0:HD], ACT.Square, scale=ROOT,
                               accum_out=k_meansq[:]).then_inc(s.k_squared, 1)
                act.activation(v[0][:, u % 2, :], B_KV[:, HD:2 * HD], ACT.Copy).then_inc(s.v_hi, 1)

            def read_turned(i, u):
                act.wait_ge(s.q_turned, nth(i, UNITS, u + 1))
                act.activation(qT[0][:], B_QT.rearrange("p (h t) -> p h t", h=QUAD), ACT.Copy).then_inc(s.qT_hi, 1)
                act.wait_ge(s.k_turned, nth(i, UNITS, u + 1))
                act.activation(kT[0][:], B_KT[:, 0:P], ACT.Copy, scale=kq_w[:]).then_inc(s.kT_hi, 1)

            def step(i, u, first=False):
                act.wait_ge(s.max_ready, nth(i, UNITS, u + 1))
                for h in range(QUAD):
                    act.activation(probs[:, h, :], probs[:, h, :], ACT.Exp, bias=neg_max[:, h:h + 1],
                                   accum_out=sums[:, h:h + 1]).then_inc(s.exped, 1)
                if units_from(i, u) > 1:
                    read_kv(i, u + 1)
                act.wait_ge(s.p_turned, nth(i, UNITS, u + 1))
                act.activation(pT[0][:], B_PT[:], ACT.Copy).then_inc(s.pT_hi, 1)
                if units_from(i, u) > 1:
                    read_turned(i, u + 1)
                act.wait_ge(s.pv_made, nth(i, UNITS, u + 1))
                act.activation(oT[0][:], B_O.rearrange("p (h t) -> p h t", h=QUAD), ACT.Copy).then_inc(s.oT_hi, 1)
                k, t = u // NB + 1, u % NB
                if units_from(i, u) > NB:
                    if t in Q_STEPS:
                        hi_q(i, k, t - Q_STEPS[0])
                    if t in O_STEPS:
                        hi_o(i, k, t - O_STEPS[0])
                    if t == NB - 2:
                        hi_kv(i, k)
                if units_from(i, u) > 2:
                    read_q(i, u + 2)

            for c in range(KC):
                hi_q(0, 0, c)
            hi_kv(0, 0)
            read_q(0, 0)
            read_kv(0, 0)
            for h in range(QUAD):
                hi_o(0, 0, h)
            act.wait_ge(s.kq_ready, 1)
            read_turned(0, 0)
            read_q(0, 1)
            step(0, 0)
            run(act, step)

        @block.gpsimd
        def _(pool):
            def q_factor(i, u):
                pool.wait_ge(s.q_squared, nth(i, UNITS * QUAD, QUAD * (u + 1)))
                pool.tensor_tensor(q_rstd[:], q_meansq[:], M.eps[:, 0:QUAD], ALU.add).then_inc(s.q_pow, 1)
                pool.wait_ge(s.q_pow, nth(i, 2 * UNITS, 2 * u + 1))
                pool.tensor_tensor(q_rstd[:], q_rstd[:], M.neg_half[:, 0:QUAD], ALU.pow).then_inc(s.q_pow, 1)

            def k_factor(i, u):
                pool.wait_ge(s.k_squared, nth(i, UNITS, u + 1))
                pool.tensor_tensor(k_rstd[:], k_meansq[:], M.eps[:, 0:1], ALU.add).then_inc(s.k_pow, 1)
                pool.wait_ge(s.k_pow, nth(i, 2 * UNITS, 2 * u + 1))
                pool.tensor_tensor(k_rstd[:], k_rstd[:], M.neg_half[:, 0:1], ALU.pow).then_inc(s.k_pow, 1)

            def step(i, u):
                if units_from(i, u) > 1:
                    k_factor(i, u + 1)
                if units_from(i, u) > 2:
                    q_factor(i, u + 2)

            q_factor(0, 0)
            k_factor(0, 0)
            q_factor(0, 1)
            step(0, 0)
            run(pool, step)

        @block.vector
        def _(dve):
            def lo_q(i, k, c):
                dve.wait_ge(s.q_hi, nth(i, 2 * KC, KC * k + c + 1))
                dve.tensor_tensor(w_q[1][:, k % 2, c], raw_q[:, c], f32(w_q[0][:, k % 2, c]),
                                  ALU.subtract).then_inc(s.q_split, 1)

            def lo_o(i, k, h):
                dve.wait_ge(s.o_hi, nth(i, 2 * QUAD, QUAD * k + h + 1))
                dve.tensor_tensor(w_o[1][:, k % 2, h], raw_o[:, h], f32(w_o[0][:, k % 2, h]),
                                  ALU.subtract).then_inc(s.o_split, 1)

            def lo_kv(i, k):
                dve.wait_ge(s.kv_hi, nth(i, 2, k + 1))
                dve.tensor_tensor(w_kv[1][:], raw_kv[:], f32(w_kv[0][:]), ALU.subtract).then_inc(s.kv_split, 1)

            def norm_q(i, u):
                dve.wait_ge(s.q_pow, nth(i, 2 * UNITS, 2 * u + 2))
                dve.tensor_tensor(q_n[:], B_Q.rearrange("p (h d) -> p h d", h=QUAD),
                                  q_rstd[:].unsqueeze(2).to_broadcast([P, QUAD, HD]), ALU.mult).then_inc(s.q_normed, 1)

            def read_kv(i, u):
                dve.wait_ge(s.v_hi, nth(i, UNITS, u + 1))
                dve.tensor_tensor(v[1][:, u % 2, :], B_KV[:, HD:2 * HD], f32(v[0][:, u % 2, :]),
                                  ALU.subtract).then_inc(s.v_split, 1)
                dve.wait_ge(s.k_pow, nth(i, 2 * UNITS, 2 * u + 2))
                dve.tensor_scalar(k_n[:], B_KV[:, 0:HD], k_rstd[:], None, ALU.mult).then_inc(s.k_normed, 1)

            def read_turned(i, u):
                dve.wait_ge(s.qT_hi, nth(i, UNITS, u + 1))
                dve.tensor_tensor(qT[1][:], B_QT.rearrange("p (h t) -> p h t", h=QUAD), f32(qT[0][:]),
                                  ALU.subtract).then_inc(s.qT_split, 1)
                dve.wait_ge(s.kT_hi, nth(i, UNITS, u + 1))
                dve.scalar_tensor_tensor(out=kT[1][:], in0=B_KT[:, 0:P], scalar=kq_w[:], in1=f32(kT[0][:]),
                                         op0=ALU.mult, op1=ALU.subtract).then_inc(s.kT_split, 1)

            def add_y(i, u):
                dve.wait_ge(s.y_made, primed(i, UNITS, u + 1))
                x = M.x[:, u % NB, :]
                dve.tensor_tensor(x, x, B_Y[:], ALU.add).then_inc(s.y_added, 1)

            def step(i, u, first=False):
                dve.wait_ge(s.scored, nth(i, UNITS, u + 1))
                dve.tensor_tensor(probs[:], B_S.rearrange("p (h k) -> p h k", h=QUAD),
                                  mask[:].unsqueeze(1).to_broadcast([P, QUAD, P]), ALU.add).then_inc(s.masked, 1)
                dve.wait_ge(s.masked, primed(i, UNITS, u + 1))
                dve.tensor_reduce(neg_max[:], probs[:], AX.X, ALU.max, negate=True).then_inc(s.max_ready, 1)
                if units_from(i, u) > 1:
                    norm_q(i, u + 1)
                dve.wait_ge(s.exped, nth(i, UNITS * QUAD, QUAD * (u + 1)))
                dve.reciprocal(inv_sums[:], sums[:]).then_inc(s.inverted, 1)
                dve.wait_ge(s.inverted, nth(i, UNITS, u + 1))
                dve.tensor_tensor(probs[:], probs[:], inv_sums[:].unsqueeze(2).to_broadcast([P, QUAD, P]),
                                  ALU.mult).then_inc(s.p_ready, 1)
                if units_from(i, u) > 1:
                    read_kv(i, u + 1)
                if not first:
                    add_y(i, u - 1)
                dve.wait_ge(s.pT_hi, nth(i, UNITS, u + 1))
                dve.tensor_tensor(pT[1][:], B_PT[:], f32(pT[0][:]), ALU.subtract).then_inc(s.pT_split, 1)
                if units_from(i, u) > 1:
                    read_turned(i, u + 1)
                dve.wait_ge(s.oT_hi, nth(i, UNITS, u + 1))
                dve.tensor_tensor(oT[1][:], B_O.rearrange("p (h t) -> p h t", h=QUAD), f32(oT[0][:]),
                                  ALU.subtract).then_inc(s.oT_split, 1)
                k, t = u // NB + 1, u % NB
                if units_from(i, u) > NB:
                    if t in Q_STEPS:
                        lo_q(i, k, t - Q_STEPS[0])
                    if t in O_STEPS:
                        lo_o(i, k, t - O_STEPS[0])
                    if t == NB - 2:
                        lo_kv(i, k)

            dve.wait_ge(s.small_loaded, 48)
            dve.scalar_tensor_tensor(out=kq_w[:], in0=norm_w[:, 0:1], scalar=ROOT, in1=norm_w[:, 1:2],
                                     op0=ALU.mult, op1=ALU.mult).then_inc(s.kq_ready, 1)
            for c in range(KC):
                lo_q(0, 0, c)
            lo_kv(0, 0)
            norm_q(0, 0)
            read_kv(0, 0)
            for h in range(QUAD):
                lo_o(0, 0, h)
            dve.wait_ge(s.kq_ready, 1)
            read_turned(0, 0)
            step(0, 0, first=True)
            run(dve, step)
            add_y(GROUPS // 2 - 1, UNITS - 1)



def ffn0_stage(nc, M, A):
    INNER = 1792
    CH = 2
    TURNS = INNER // (CH * P)
    UNITS = [(c, h) for h in range(2) for c in range(CH)]
    with ExitStack() as ctx:
        S = Scope(nc, M, ctx, "f0")
        raw_gu = S.sb("raw_gu", [P, KC, 2, CH * P])
        raw_d = S.sb("raw_d", [P, CH, D])
        w_gu = S.pair("w_gu", [P, KC, 2, CH * P])
        w_d = S.pair("w_d", [P, CH, D])
        hT = S.pair("hT", [P, CH, TOK])
        gated = S.sb("gated", [P, 2, HALF])
        prod = S.sb("prod", [P, 2, HALF])
        s = Named()
        s.gu_loaded, s.d_loaded, s.gu_hi, s.d_hi, s.g_made = S.sems("gu_loaded d_loaded gu_hi d_hi g_made")
        s.gated, s.h_hi, s.h_split = S.sems("gated h_hi h_split")
        s.gu_split, s.d_split, s.multiplied, s.y_added = S.sems("gu_split d_split multiplied y_added", primed=True)
        s.u_made, s.y_made = S.sems("u_made y_made", primed=True)
        G, U, Y = M.bank[0:2], M.bank[2:4], M.bank[4:8]
        NU = len(UNITS)
        block = S.block()

        @block.sync
        def _(sp):
            with sp.Fori(0, TURNS) as i:
                at = bass.ds(i, 1)
                sp.wait_ge(s.gu_split, primed(i, 1, 0))
                sp.dma_start(raw_gu[:], A["L0_ffn_Wgu"][at].rearrange("g p c w n -> (g p) c w n")).then_inc(s.gu_loaded, 16)
                sp.wait_ge(s.d_split, primed(i, 1, 0))
                sp.dma_start(raw_d[:], A["L0_ffn_Wd"][at].rearrange("g p c n -> (g p) c n")).then_inc(s.d_loaded, 16)

        @block.tensor
        def _(pe):
            with pe.Fori(0, TURNS) as i:
                pe.wait_ge(s.gu_split, primed(i, 1, 1))
                for u, (c, h) in enumerate(UNITS):
                    tokens = slice(h * HALF, (h + 1) * HALF)
                    if u >= 2:
                        pe.wait_ge(s.multiplied, primed(i, NU, u - 1))
                    else:
                        pe.wait_ge(s.multiplied, primed(i, NU, 0))
                    for w, (banks, made) in enumerate(((G, s.g_made), (U, s.u_made))):
                        for k in range(KC):
                            last = mm3(pe, banks[u % 2], part(w_gu, slice(None), k, w, tile_of(c)),
                                       part(M.nT, slice(None), k, tokens), k == 0, k == KC - 1)
                        last.then_inc(made, 1)
                pe.wait_ge(s.d_split, primed(i, 1, 1))
                for t in range(NB):
                    pe.wait_ge(s.h_split, nth(i, NU, CH if t < NB // 2 else NU))
                    pe.wait_ge(s.y_added, primed(i, NB, max(t - 3, 0)))
                    for c in range(CH):
                        last = mm3(pe, Y[t % 4], part(hT, slice(None), c, tile_of(t)), part(w_d, slice(None), c),
                                   c == 0, c == CH - 1)
                    last.then_inc(s.y_made, 1)

        @block.scalar
        def _(act):
            act.preload_act_table_set("silu_and_others")
            with act.Fori(0, TURNS) as i:
                act.wait_ge(s.gu_loaded, nth(i, 16, 16))
                act.wait_ge(s.u_made, primed(i, NU, 0))
                act.activation(w_gu[0][:], raw_gu[:], ACT.Copy).then_inc(s.gu_hi, 1)
                for u, (c, h) in enumerate(UNITS):
                    tokens = slice(h * HALF, (h + 1) * HALF)
                    act.wait_ge(s.g_made, nth(i, NU, u + 1))
                    act.activation(gated[:, u % 2, :], G[u % 2], ACT.Silu).then_inc(s.gated, 1)
                    if u == 0:
                        act.wait_ge(s.d_loaded, nth(i, 16, 16))
                        act.wait_ge(s.y_made, primed(i, NB, 0))
                        act.activation(w_d[0][:], raw_d[:], ACT.Copy).then_inc(s.d_hi, 1)
                    act.wait_ge(s.multiplied, primed(i, NU, u + 1))
                    act.activation(hT[0][:, c, tokens], prod[:, u % 2, :], ACT.Copy).then_inc(s.h_hi, 1)

        @block.gpsimd
        def _(pool):
            with pool.Fori(0, TURNS) as i:
                pool.wait_ge(s.d_hi, nth(i, 1, 1))
                pool.tensor_tensor(w_d[1][:], raw_d[:], f32(w_d[0][:]), ALU.subtract).then_inc(s.d_split, 1)

        @block.vector
        def _(dve):
            def add_y(i, t):
                dve.wait_ge(s.y_made, primed(i, NB, t + 1))
                dve.tensor_tensor(M.x[:, t, :], M.x[:, t, :], Y[t % 4], ALU.add).then_inc(s.y_added, 1)

            with dve.Fori(0, TURNS) as i:
                dve.wait_ge(s.gu_hi, nth(i, 1, 1))
                dve.tensor_tensor(w_gu[1][:], raw_gu[:], f32(w_gu[0][:]), ALU.subtract).then_inc(s.gu_split, 1)
                for u, (c, h) in enumerate(UNITS):
                    tokens = slice(h * HALF, (h + 1) * HALF)
                    dve.wait_ge(s.u_made, primed(i, NU, u + 1))
                    dve.wait_ge(s.gated, nth(i, NU, u + 1))
                    dve.tensor_tensor(prod[:, u % 2, :], gated[:, u % 2, :], U[u % 2], ALU.mult).then_inc(s.multiplied, 1)
                    dve.wait_ge(s.h_hi, nth(i, NU, u + 1))
                    dve.tensor_tensor(hT[1][:, c, tokens], prod[:, u % 2, :], f32(hT[0][:, c, tokens]),
                                      ALU.subtract).then_inc(s.h_split, 1)
                for t in range(NB):
                    add_y(i, t)



def attn1_stage(nc, M, A):
    HD = 16
    CHUNKS = D // P
    LAST = CHUNKS - 1
    HEADS = P // HD
    SCALE = HD ** -0.5
    with ExitStack() as ctx:
        S = Scope(nc, M, ctx, "a1")
        raw_v = S.sb("raw_v", [P, KC, P])
        w_v = S.pair("w_v", [P, KC, P])
        raw_qk = S.sb("raw_qk", [P, KC, 2, P])
        w_qk = S.pair("w_qk", [P, KC, 2, P])
        raw_o = S.sb("raw_o", [P, D])
        w_o = S.pair("w_o", [P, D])
        v = S.sb("v", [P, NB, P // HD, 2, HD], F32R)
        qT = S.pair("qT", [P, TOK])
        kM = S.pair("kM", [P, QUAD, TOK])
        k_raw = S.sb("k_raw", [P, HALF])
        head_mask = S.sb("head_mask", [P, QUAD])
        probs = S.sb("probs", [P, 2, HEADS, P])
        neg_max = S.sb("neg_max", [P, 2, HEADS])
        sums = S.sb("sums", [P, 2, HEADS])
        inv_sums = S.sb("inv_sums", [P, HEADS])
        pT = S.pair("pT", [P, HEADS, P])
        o_sum = S.sb("o_sum", [P, HEADS, HD])
        o_n = S.sb("o_n", [P, P])
        oT = S.pair("oT", [P, P])
        s = Named()
        s.v_loaded, s.mask_loaded, s.qk_loaded, s.o_loaded = S.sems("v_loaded mask_loaded qk_loaded o_loaded")
        s.v_hi, s.w_split, s.wk_hi, s.wq_hi, s.o_hi, s.v_made = S.sems("v_hi w_split wk_hi wq_hi o_hi v_made")
        s.v_val_hi, s.v_split, s.q_hi, s.k_hi, s.scored = S.sems("v_val_hi v_split q_hi k_hi scored")
        s.max_ready, s.p_turned, s.pT_hi, s.o_made = S.sems("max_ready p_turned pT_hi o_made")
        s.inverted, s.summed, s.o_normed, s.o_turned, s.oT_hi = S.sems("inverted summed o_normed o_turned oT_hi")
        s.wk_split, s.wq_split, s.o_split, s.exped = S.sems("wk_split wq_split o_split exped", primed=True)
        s.pT_split, s.oT_split, s.q_made, s.k_made = S.sems("pT_split oT_split q_made k_made", primed=True)
        s.q_split, s.k_split, s.y_made, s.y_added = S.sems("q_split k_split y_made y_added", primed=True)
        [s.k_copied] = S.sems("k_copied", primed=True)
        K_BANK, Q_BANK = M.bank[2], M.bank[3]
        PT, O, Y = M.psum[:, 4:6, :], M.bank[6], M.bank[7]
        scores = M.psum[:, 0:2, :].rearrange("p j (h k) -> p j h k", k=P)
        O_TURNED = O[:, 2 * P:3 * P]
        o_parts = O[:, 0:2 * P].rearrange("p (h w d) -> p h w d", w=2, d=HD)
        v_flat = v[:].rearrange("p b h w d -> p b (h w d)")
        block = S.block()

        def run(engine, step):
            with engine.Fori(0, LAST) as c:
                for b in range(1, NB + 1):
                    step(c, b)
            for b in range(1, NB):
                step(LAST, b)

        def steps_on(c, b):
            return b < NB - 1 or c is not LAST

        def piece_of(c, b):
            t, k = b % NB, b // NB
            if t in (1, 2):
                return 0, 2 * k + 1, t - 1
            if t == 0:
                return 1, 2 * k + 1, 1
            if c is LAST:
                return None
            return {3: (1, 2 * k + 2, 0), 4: (1, 2 * k + 2, 1), 5: (0, 2 * k + 2, 0), 6: (0, 2 * k + 2, 1),
                    7: (1, 2 * k + 3, 0)}[t]

        def k_masks_of(c, b):
            t, k = b % NB, b // NB
            if t in (0, 1):
                return 2 * k + 1, ((0, 1), (2, 3))[t]
            if t in (4, 5) and c is not LAST:
                return 2 * k + 2, ((0, 1), (2, 3))[t - 4]
            return None, ()

        @block.sync
        def _(sp):
            sp.dma_start(raw_v[:], A["L1_xattn_Wv"]).then_inc(s.v_loaded, 16)
            sp.dma_start(head_mask[:], A["head_mask"]).then_inc(s.mask_loaded, 16)
            with sp.Fori(0, CHUNKS) as c:
                at = bass.ds(c, 1)
                sp.wait_ge(s.wk_split, primed(c, 1, 0))
                sp.wait_ge(s.wq_split, primed(c, 1, 0))
                sp.dma_start(raw_qk[:], A["L1_xattn_Wqk"][at].rearrange("g p c w n -> (g p) c w n")).then_inc(s.qk_loaded, 16)
                sp.wait_ge(s.o_split, primed(c, 1, 0))
                sp.dma_start(raw_o[:], A["L1_xattn_Wo"][at].rearrange("g p n -> (g p) n")).then_inc(s.o_loaded, 16)

        @block.tensor
        def _(pe):
            def project(c, w, piece, halves):
                made, read, weights = ((s.q_made, s.q_split, s.wq_split), (s.k_made, s.k_copied, s.wk_split))[w]
                tokens = slice(piece % 2 * HALF, (piece % 2 + 1) * HALF)
                if 0 in halves:
                    pe.wait_ge(weights, primed(c, 1, piece // 2 + 1))
                    pe.wait_ge(read, primed(c, 2, piece))
                for half in halves:
                    for k in (2 * half, 2 * half + 1):
                        last = mm3(pe, (Q_BANK, K_BANK)[w], part(w_qk, slice(None), k, w),
                                   part((M.nT, M.cT)[w], slice(None), k, tokens), k == 0, k == KC - 1)
                if 1 in halves:
                    last.then_inc(made, 1)

            def score(c, b):
                if b % 4 == 0:
                    piece = b // 4
                    pe.wait_ge(s.q_split, primed(c, 2, piece + 1))
                    pe.wait_ge(s.k_split, primed(c, 2 * QUAD, QUAD * (piece + 1)))
                for j in range(2):
                    pe.wait_ge(s.exped, primed(c, NB * HEADS, HEADS * (b - 1) + QUAD * (j + 1) if b else 0))
                    rows = slice(64 * j, 64 * j + 64)
                    mm3(pe, M.bank[j], part(qT, rows, tile_of(b % NB)),
                        part(kM, rows, slice(None), tile_of(b % NB)), True, True).then_inc(s.scored, 1)

            def turn_p(c, b):
                for j in range(2):
                    pe.wait_ge(s.exped, primed(c, NB * HEADS, HEADS * b + QUAD * (j + 1)))
                    pe.wait_ge(s.pT_split, primed(c, 2 * NB, 2 * (b - 1) + j + 1 if b else 0))
                    for h in range(QUAD):
                        last = pe.transpose(PT[:, j, tile_of(h)], probs[:, b % 2, QUAD * j + h, :], M.ident[:])
                    last.then_inc(s.p_turned, 1)

            def weigh_v(c, b):
                pe.wait_ge(s.oT_split, primed(c, NB, b))
                for h in range(HEADS):
                    if h % QUAD == 0:
                        pe.wait_ge(s.pT_split, primed(c, 2 * NB, 2 * b + h // QUAD + 1))
                    first = (c + b // NB) * (4 * HD) + (h // QUAD) * (2 * HD)
                    pe.matmul(O[:, 2 * h * HD:2 * (h + 1) * HD], pT[0][:, h], v_flat[:, b % NB, bass.ds(first, 2 * HD)],
                              start=True, stop=False)
                    last = pe.matmul(O[:, 2 * h * HD:(2 * h + 1) * HD], pT[1][:, h], v_flat[:, b % NB, bass.ds(first, HD)],
                                     start=False, stop=True)
                last.then_inc(s.o_made, 1)

            def turn_o(c, b):
                pe.wait_ge(s.o_normed, nth(c, NB, b + 1))
                pe.transpose(O_TURNED, o_n[:], M.ident[:]).then_inc(s.o_turned, 1)

            def project_out(c, b):
                pe.wait_ge(s.oT_split, primed(c, NB, b + 1))
                pe.wait_ge(s.y_added, primed(c, NB, b))
                if b % NB == 0:
                    pe.wait_ge(s.o_split, primed(c, 1, b // NB + 1))
                mm3(pe, Y, (oT[0][:], oT[1][:]), (w_o[0][:], w_o[1][:]), True, True).then_inc(s.y_made, 1)

            def step(c, b, first=False):
                if steps_on(c, b):
                    score(c, b + 1)
                if not first:
                    turn_o(c, b - 1)
                turn_p(c, b)
                if not first and piece_of(c, b):
                    w, piece, half = piece_of(c, b)
                    project(c, w, piece, (half,))
                if not first:
                    project_out(c, b - 1)
                weigh_v(c, b)

            pe.wait_ge(s.w_split, 1)
            for b in range(NB):
                for k in range(KC):
                    last = mm3(pe, PT[:, b // 4, tile_of(b % 4)], part(M.cT, slice(None), k, tile_of(b)),
                               part(w_v, slice(None), k), k == 0, k == KC - 1)
                last.then_inc(s.v_made, 1)
            project(0, 1, 0, (0, 1))
            project(0, 0, 0, (0, 1))
            project(0, 1, 1, (0, 1))
            score(0, 0)
            pe.wait_ge(s.v_split, 2)
            step(0, 0, first=True)
            run(pe, step)
            turn_o(LAST, NB - 1)
            project_out(LAST, NB - 1)

        @block.scalar
        def _(act):
            def hi_w(c, w, chunk):
                act.wait_ge(s.qk_loaded, nth(c, 16, 16 * (chunk + 1)))
                act.wait_ge((s.q_made, s.k_made)[w], primed(c, 2, 2 * chunk))
                act.activation(w_qk[0][:, :, w], raw_qk[:, :, w], ACT.Copy).then_inc((s.wq_hi, s.wk_hi)[w], 1)

            def hi_o(c, chunk):
                act.wait_ge(s.o_loaded, nth(c, 16, 16 * (chunk + 1)))
                act.wait_ge(s.y_made, primed(c, NB, NB * chunk))
                act.activation(w_o[0][:], raw_o[:], ACT.Copy).then_inc(s.o_hi, 1)

            def hi_q(c, piece):
                tokens = slice(piece % 2 * HALF, (piece % 2 + 1) * HALF)
                act.wait_ge(s.q_made, primed(c, 2, piece + 1))
                act.activation(qT[0][:, tokens], Q_BANK, ACT.Copy, scale=SCALE).then_inc(s.q_hi, 1)

            def hi_k(c, piece, copies):
                if 0 in copies:
                    act.wait_ge(s.k_made, primed(c, 2, piece + 1))
                    act.wait_ge(s.k_split, primed(c, 2 * QUAD, QUAD * piece))
                    act.activation(k_raw[:], K_BANK, ACT.Copy).then_inc(s.k_copied, 1)
                    act.wait_ge(s.k_copied, primed(c, 2, piece + 1))
                for j in copies:
                    act.activation(kM[0][:, j, piece % 2 * HALF:(piece % 2 + 1) * HALF], k_raw[:], ACT.Copy,
                                   scale=head_mask[:, j:j + 1]).then_inc(s.k_hi, 1)

            def exps(c, b, j):
                act.wait_ge(s.max_ready, nth(c, 2 * NB, 2 * b + j + 1))
                for h in range(QUAD):
                    n = QUAD * j + h
                    act.activation(probs[:, b % 2, n, :], scores[:, j, h, :], ACT.Exp, bias=neg_max[:, b % 2, n:n + 1],
                                   accum_out=sums[:, b % 2, n:n + 1]).then_inc(s.exped, 1)

            def hi_oT(c, b):
                act.wait_ge(s.o_turned, nth(c, NB, b + 1))
                act.activation(oT[0][:], O_TURNED, ACT.Copy).then_inc(s.oT_hi, 1)

            def step(c, b, first=False):
                t = b % NB
                if steps_on(c, b):
                    exps(c, b + 1, 0)
                if not first:
                    hi_oT(c, b - 1)
                for j in range(2):
                    act.wait_ge(s.p_turned, nth(c, 2 * NB, 2 * b + j + 1))
                    act.activation(pT[0][:, QUAD * j:QUAD * (j + 1)], PT[:, j].rearrange("p (h q) -> p h q", q=P),
                                   ACT.Copy).then_inc(s.pT_hi, 1)
                if not first and (t == 2 or t == 6 and c is not LAST):
                    hi_q(c, piece_of(c, b)[1])
                if steps_on(c, b):
                    exps(c, b + 1, 1)
                hi_k(c, *k_masks_of(c, b))
                if t == 0:
                    hi_o(c, b // NB)
                if t in (1, 3) and c is not LAST:
                    hi_w(c, {1: 1, 3: 0}[t], b // NB + 1)

            act.wait_ge(s.v_loaded, 16)
            act.activation(w_v[0][:], raw_v[:], ACT.Copy).then_inc(s.v_hi, 1)
            hi_w(0, 1, 0)
            hi_w(0, 0, 0)
            for half in range(2):
                act.wait_ge(s.v_made, NB // 2 * (half + 1))
                act.activation(v[:, 4 * half:4 * half + 4, :, 0, :],
                               PT[:, half, :].rearrange("p (b h d) -> p b h d", b=4, d=HD), ACT.Copy).then_inc(s.v_val_hi, 1)
            act.wait_ge(s.mask_loaded, 16)
            hi_k(0, 0, range(QUAD))
            hi_q(0, 0)
            exps(0, 0, 0)
            exps(0, 0, 1)
            step(0, 0, first=True)
            run(act, step)
            hi_oT(LAST, NB - 1)

        @block.gpsimd
        def _(pool):
            def lo_w(c, w, chunk):
                pool.wait_ge((s.wq_hi, s.wk_hi)[w], nth(c, 1, chunk + 1))
                pool.tensor_tensor(w_qk[1][:, :, w], raw_qk[:, :, w], f32(w_qk[0][:, :, w]),
                                   ALU.subtract).then_inc((s.wq_split, s.wk_split)[w], 1)

            def step(c, b):
                t = b % NB
                if t == 0:
                    pool.wait_ge(s.o_hi, nth(c, 1, b // NB + 1))
                    pool.tensor_tensor(w_o[1][:], raw_o[:], f32(w_o[0][:]), ALU.subtract).then_inc(s.o_split, 1)
                if t in (1, 3) and c is not LAST:
                    lo_w(c, {1: 1, 3: 0}[t], b // NB + 1)

            lo_w(0, 1, 0)
            lo_w(0, 0, 0)
            step(0, 0)
            run(pool, step)

        @block.vector
        def _(dve):
            def lo_q(c, piece):
                tokens = slice(piece % 2 * HALF, (piece % 2 + 1) * HALF)
                dve.wait_ge(s.q_hi, nth(c, 2, piece + 1))
                dve.scalar_tensor_tensor(out=qT[1][:, tokens], in0=Q_BANK, scalar=SCALE, in1=f32(qT[0][:, tokens]),
                                         op0=ALU.mult, op1=ALU.subtract).then_inc(s.q_split, 1)

            def lo_k(c, piece, copies):
                for j in copies:
                    at = slice(piece % 2 * HALF, (piece % 2 + 1) * HALF)
                    dve.wait_ge(s.k_hi, nth(c, 2 * QUAD, QUAD * piece + j + 1))
                    dve.scalar_tensor_tensor(out=kM[1][:, j, at], in0=k_raw[:], scalar=head_mask[:, j:j + 1],
                                             in1=f32(kM[0][:, j, at]), op0=ALU.mult, op1=ALU.subtract).then_inc(s.k_split, 1)

            def row_max(c, b, j):
                dve.wait_ge(s.scored, nth(c, 2 * NB, 2 * b + j + 1))
                dve.tensor_reduce(neg_max[:, b % 2, QUAD * j:QUAD * (j + 1)], scores[:, j], AX.X, ALU.max,
                                  negate=True).then_inc(s.max_ready, 1)

            def lo_oT(c, b):
                dve.wait_ge(s.oT_hi, nth(c, NB, b + 1))
                dve.tensor_tensor(oT[1][:], O_TURNED, f32(oT[0][:]), ALU.subtract).then_inc(s.oT_split, 1)

            def add_y(c, b):
                x = M.x[:, b % NB, :]
                dve.wait_ge(s.y_made, primed(c, NB, b + 1))
                dve.tensor_tensor(x, x, Y, ALU.add).then_inc(s.y_added, 1)

            def step(c, b, first=False):
                t = b % NB
                if steps_on(c, b):
                    row_max(c, b + 1, 0)
                    row_max(c, b + 1, 1)
                if not first:
                    lo_oT(c, b - 1)
                for j in range(2):
                    dve.wait_ge(s.pT_hi, nth(c, 2 * NB, 2 * b + j + 1))
                    dve.tensor_tensor(pT[1][:, QUAD * j:QUAD * (j + 1)], PT[:, j].rearrange("p (h q) -> p h q", q=P),
                                      f32(pT[0][:, QUAD * j:QUAD * (j + 1)]), ALU.subtract).then_inc(s.pT_split, 1)
                if not first and (t == 2 or t == 6 and c is not LAST):
                    lo_q(c, piece_of(c, b)[1])
                if not first:
                    add_y(c, b - 1)
                dve.reciprocal(inv_sums[:], sums[:, b % 2, :]).then_inc(s.inverted, 1)
                dve.wait_ge(s.o_made, nth(c, NB, b + 1))
                dve.tensor_copy(o_sum[:], o_parts[:, :, 1, :]).then_inc(s.summed, 1)
                dve.wait_ge(s.summed, nth(c, 2 * NB, 2 * b + 1))
                dve.tensor_tensor(o_sum[:], o_parts[:, :, 0, :], o_sum[:], ALU.add).then_inc(s.summed, 1)
                dve.wait_ge(s.inverted, nth(c, NB, b + 1))
                dve.wait_ge(s.summed, nth(c, 2 * NB, 2 * b + 2))
                dve.tensor_tensor(o_n[:].rearrange("p (h d) -> p h d", d=HD), o_sum[:],
                                  inv_sums[:].unsqueeze(2).to_broadcast([P, HEADS, HD]), ALU.mult).then_inc(s.o_normed, 1)
                lo_k(c, *k_masks_of(c, b))

            dve.wait_ge(s.v_hi, 1)
            dve.tensor_tensor(w_v[1][:], raw_v[:], f32(w_v[0][:]), ALU.subtract).then_inc(s.w_split, 1)
            for half in range(2):
                dve.wait_ge(s.v_val_hi, half + 1)
                tiles = slice(4 * half, 4 * half + 4)
                dve.tensor_tensor(v[:, tiles, :, 1, :], PT[:, half, :].rearrange("p (b h d) -> p b h d", b=4, d=HD),
                                  f32(v[:, tiles, :, 0, :]), ALU.subtract).then_inc(s.v_split, 1)
            dve.wait_ge(s.mask_loaded, 16)
            lo_k(0, 0, range(QUAD))
            lo_q(0, 0)
            row_max(0, 0, 0)
            row_max(0, 0, 1)
            step(0, 0, first=True)
            run(dve, step)
            lo_oT(LAST, NB - 1)
            add_y(LAST, NB - 1)



def ffn1_stage(nc, M, A):
    E, R = 8, 16
    SCALING = 2.0
    MID = E * R
    with ExitStack() as ctx:
        S = Scope(nc, M, ctx, "f1")
        raw_mid = S.sb("raw_mid", [P, KC, MID + E])
        raw_base = S.sb("raw_base", [P, KC, D])
        raw_b = S.sb("raw_b", [P, D])
        w_mid = S.pair("w_mid", [P, KC, MID + E])
        w_base = S.pair("w_base", [P, KC, D])
        w_b = S.pair("w_b", [P, D])
        expert = S.sb("expert", [P, E])
        mid = S.sb("mid", [P, NB, MID + E])
        logits = mid[:, :, MID:MID + E]
        best = S.sb("best", [P, NB])
        second = S.sb("second", [P, NB])
        at_best = S.sb("at_best", [P, NB])
        hit = S.sb("hit", [P, NB, E])
        is_best = S.sb("is_best", [P, NB, E])
        is_second = S.sb("is_second", [P, NB, E])
        rest = S.sb("rest", [P, NB, E])
        weight = S.sb("weight", [P, NB, E])
        mid_w = S.sb("mid_w", [P, NB, MID])
        mT = S.pair("mT", [P, 2, P])
        s = Named()
        s.mid_loaded, s.base_loaded, s.b_loaded = S.sems("mid_loaded base_loaded b_loaded")
        s.expert_loaded, s.mid_hi, s.base_hi, s.b_hi = S.sems("expert_loaded mid_hi base_hi b_hi")
        s.mid_split, s.base_split, s.b_split, s.mid_made = S.sems("mid_split base_split b_split mid_made")
        s.mid_copied, s.routed, s.less_max, s.exped = S.sems("mid_copied routed less_max exped")
        s.mid_weighted, s.turned, s.mT_hi, s.mT_split, s.y_made = S.sems("mid_weighted turned mT_hi mT_split y_made")
        [s.y_added] = S.sems("y_added")
        block = S.block()
        Y = M.bank[4:8]

        def along_experts(ap):
            return ap.unsqueeze(2).to_broadcast([P, NB, E])

        @block.sync
        def _(sp):
            sp.dma_start(raw_mid[:], A["L1_ffn_mid"]).then_inc(s.mid_loaded, 16)
            sp.dma_start(raw_base[:], A["L1_ffn_base"]).then_inc(s.base_loaded, 16)
            sp.dma_start(raw_b[:], A["L1_ffn_lora_B"]).then_inc(s.b_loaded, 16)
            sp.dma_start(expert[:], A["expert"]).then_inc(s.expert_loaded, 16)

        @block.tensor
        def _(pe):
            pe.wait_ge(s.mid_split, 1)
            for b in range(NB):
                if b >= 2:
                    pe.wait_ge(s.mid_copied, b - 1)
                for k in range(KC):
                    last = mm3(pe, M.bank[b % 2][:, 0:MID + E], part(M.nT, slice(None), k, tile_of(b)),
                               part(w_mid, slice(None), k), k == 0, k == KC - 1)
                last.then_inc(s.mid_made, 1)
            pe.wait_ge(s.base_split, 1)

            def base(b):
                if b >= 4:
                    pe.wait_ge(s.y_added, b - 3)
                for k in range(KC):
                    mm3(pe, Y[b % 4], part(M.nT, slice(None), k, tile_of(b)), part(w_base, slice(None), k),
                        k == 0, False)

            for b in range(4):
                base(b)
            pe.wait_ge(s.b_split, 1)
            for b in range(NB):
                pe.wait_ge(s.mid_weighted, b + 1)
                if b >= 2:
                    pe.wait_ge(s.mT_split, b - 1)
                pe.transpose(M.bank[2 + b % 2][:, 0:P], mid_w[:, b, :], M.ident[:]).then_inc(s.turned, 1)
                pe.wait_ge(s.mT_split, b + 1)
                mm3(pe, Y[b % 4], part(mT, slice(None), b % 2), (w_b[0][:], w_b[1][:]), False, True).then_inc(s.y_made, 1)
                if b + 4 < NB:
                    base(b + 4)

        @block.scalar
        def _(act):
            act.wait_ge(s.mid_loaded, 16)
            act.activation(w_mid[0][:], raw_mid[:], ACT.Copy).then_inc(s.mid_hi, 1)
            act.wait_ge(s.base_loaded, 16)
            act.activation(w_base[0][:], raw_base[:], ACT.Copy).then_inc(s.base_hi, 1)
            act.wait_ge(s.b_loaded, 16)
            act.activation(w_b[0][:], raw_b[:], ACT.Copy).then_inc(s.b_hi, 1)
            for b in range(NB):
                act.wait_ge(s.mid_made, b + 1)
                act.activation(mid[:, b, :], M.bank[b % 2][:, 0:MID + E], ACT.Copy).then_inc(s.mid_copied, 1)
            act.wait_ge(s.less_max, 1)
            act.activation(weight[:], weight[:], ACT.Exp).then_inc(s.exped, 1)
            for b in range(NB):
                act.wait_ge(s.turned, b + 1)
                act.activation(mT[0][:, b % 2, :], M.bank[2 + b % 2][:, 0:P], ACT.Copy).then_inc(s.mT_hi, 1)

        @block.vector
        def _(dve):
            steps = [0]

            def step(ins):
                ins.then_inc(s.routed, 1)
                steps[0] += 1
                dve.wait_ge(s.routed, steps[0])

            for w, raw, hi, split in ((w_mid, raw_mid, s.mid_hi, s.mid_split), (w_base, raw_base, s.base_hi, s.base_split),
                                      (w_b, raw_b, s.b_hi, s.b_split)):
                dve.wait_ge(hi, 1)
                dve.tensor_tensor(w[1][:], raw[:], f32(w[0][:]), ALU.subtract).then_inc(split, 1)
            dve.wait_ge(s.expert_loaded, 16)
            dve.wait_ge(s.mid_copied, NB)
            numbers = expert[:].unsqueeze(1).to_broadcast([P, NB, E])
            step(dve.tensor_reduce(best[:], logits, AX.X, ALU.max))
            dve.tensor_tensor(weight[:], logits, along_experts(best[:]), ALU.subtract).then_inc(s.less_max, 1)

            def first_at(value, source, out):
                step(dve.tensor_tensor(hit[:], source, along_experts(value), ALU.is_equal))
                step(dve.tensor_tensor(hit[:], hit[:], numbers, ALU.mult))
                step(dve.tensor_reduce(at_best[:], hit[:], AX.X, ALU.min))
                step(dve.tensor_tensor(out, numbers, along_experts(at_best[:]), ALU.is_equal))

            first_at(best[:], logits, is_best[:])
            step(dve.scalar_tensor_tensor(out=rest[:], in0=is_best[:], scalar=-3.0e38, in1=logits,
                                          op0=ALU.mult, op1=ALU.add))
            step(dve.tensor_reduce(second[:], rest[:], AX.X, ALU.max))
            first_at(second[:], rest[:], is_second[:])
            step(dve.tensor_tensor(is_best[:], is_best[:], is_second[:], ALU.add))
            dve.wait_ge(s.exped, 1)
            step(dve.tensor_tensor(weight[:], weight[:], is_best[:], ALU.mult))
            step(dve.tensor_reduce(best[:], weight[:], AX.X, ALU.add))
            step(dve.reciprocal(second[:], best[:]))
            step(dve.scalar_tensor_tensor(out=weight[:], in0=weight[:], scalar=SCALING, in1=along_experts(second[:]),
                                          op0=ALU.mult, op1=ALU.mult))
            for b in range(NB):
                dve.tensor_tensor(mid_w[:, b, :].rearrange("p (e r) -> p e r", e=E),
                                  mid[:, b, 0:MID].rearrange("p (e r) -> p e r", e=E),
                                  weight[:, b, :].unsqueeze(2).to_broadcast([P, E, R]), ALU.mult).then_inc(s.mid_weighted, 1)
            for b in range(NB):
                dve.wait_ge(s.mT_hi, b + 1)
                dve.tensor_tensor(mT[1][:, b % 2, :], M.bank[2 + b % 2][:, 0:P], f32(mT[0][:, b % 2, :]),
                                  ALU.subtract).then_inc(s.mT_split, 1)
                dve.wait_ge(s.y_made, b + 1)
                dve.tensor_tensor(M.x[:, b, :], M.x[:, b, :], Y[b % 4], ALU.add).then_inc(s.y_added, 1)



def attn2_stage(nc, M, A):
    HD = P
    GROUPS = 4
    LAST = GROUPS - 1
    KEYS = 2 * P
    PAIR = 2 * P
    N = 2 * NB
    NQ = 2 * N
    AHEAD = 6
    SCALE = 1.0 / float(np.sqrt(HD))
    with ExitStack() as ctx:
        S = Scope(nc, M, ctx, "a2")
        raw_kv = S.sb("raw_kv", [P, KC, 2, HD])
        w_kv = S.pair("w_kv", [P, KC, 2, HD])
        raw_q = S.sb("raw_q", [P, KC, QUAD * HD])
        w_q = S.pair("w_q", [P, KC, QUAD * HD])
        raw_o = S.sb("raw_o", [P, QUAD, D])
        w_o = S.pair("w_o", [P, QUAD, D])
        kT = S.pair("kT", [P, NB, 2, P])
        v = S.pair("v", [P, NB, 2, HD])
        qT = S.pair("qT", [P, 2, QUAD, PAIR])
        probs = S.sb("probs", [P, QUAD, KEYS])
        neg_max = S.sb("neg_max", [P, QUAD])
        sums = S.sb("sums", [P, QUAD])
        inv_sums = S.sb("inv_sums", [P, QUAD])
        pT = S.pair("pT", [P, 2, QUAD * P])
        oT = S.pair("oT", [P, QUAD * P])
        s = Named()
        s.kv_loaded, s.q_loaded, s.o_loaded, s.kv_hi, s.wq_hi = S.sems("kv_loaded q_loaded o_loaded kv_hi wq_hi")
        s.wo_hi, s.kvp_hi, s.q_hi, s.scored, s.max_ready = S.sems("wo_hi kvp_hi q_hi scored max_ready")
        s.inverted, s.p_ready, s.p_turned, s.pT_hi, s.o_made = S.sems("inverted p_ready p_turned pT_hi o_made")
        [s.oT_hi] = S.sems("oT_hi")
        s.kv_split, s.wq_split, s.wo_split, s.q_split = S.sems("kv_split wq_split wo_split q_split", primed=True)
        s.exped, s.pT_split, s.oT_split, s.y_added = S.sems("exped pT_split oT_split y_added", primed=True)
        s.kvp_split, s.q_made, s.y_made, s.kvp_made = S.sems("kvp_split q_made y_made kvp_made", primed=True)
        PROJ = M.bank[0:2]
        SC, PT, O, Y = M.psum[:, 2:4, :], M.psum[:, 4:6, :], M.bank[6], M.bank[7]
        block = S.block()
        scores = SC.rearrange("p j (h k) -> p (j h) k", k=KEYS)
        PIECES = [(w, src, half) for w in range(2) for src in range(2) for half in range(2)]
        FIRST_SCORE = 5

        def query_pieces(g, n):
            return [j for j in (2 * n + AHEAD, 2 * n + AHEAD + 1) if j < NQ or g is not LAST]

        def run(engine, turn):
            with engine.Fori(0, LAST) as g:
                turn(g)
            turn(LAST)

        @block.sync
        def _(sp):
            with sp.Fori(0, GROUPS) as g:
                sp.wait_ge(s.kv_split, primed(g, 1, 0))
                sp.dma_start(raw_kv[:], A["L2_xattn_Wkv"][bass.ds(g, 1)].rearrange("g p c w n -> (g p) c w n")).then_inc(s.kv_loaded, 16)
                for quad in range(2):
                    at = bass.ds(g * 2 + quad, 1)
                    sp.wait_ge(s.wq_split, primed(g, 2 * QUAD, QUAD * quad))
                    sp.dma_start(raw_q[:], A["L2_xattn_Wq"][at].rearrange("g p c n -> (g p) c n")).then_inc(s.q_loaded, 16)
                    sp.wait_ge(s.wo_split, primed(g, 2 * QUAD, QUAD * quad))
                    sp.dma_start(raw_o[:], A["L2_xattn_Wo"][at].rearrange("g p c n -> (g p) c n")).then_inc(s.o_loaded, 16)

        @block.tensor
        def _(pe):
            def project_q(g, j):
                pair, h = j // QUAD, j % QUAD
                start = pair % 4 * PAIR
                if pair % 4 == 0:
                    pe.wait_ge(s.wq_split, primed(g, 2 * QUAD, pair // 4 * QUAD + h + 1))
                pe.wait_ge(s.q_split, primed(g, NQ, max(j - 1, 0)))
                for k in range(KC):
                    last = mm3(pe, PROJ[j % 2][:, 0:PAIR], part(w_q, slice(None), k, tile_of(h)),
                               part(M.nT, slice(None), k, slice(start, start + PAIR)), k == 0, k == KC - 1)
                last.then_inc(s.q_made, 1)

            def score(g, n):
                pe.wait_ge(s.q_split, primed(g, NQ, QUAD * (n // 2 + 1)))
                pe.wait_ge(s.exped, primed(g, N * QUAD, QUAD * n))
                for h in range(QUAD):
                    last = mm3(pe, scores[:, h, :], part(qT, slice(None), n // 2 % 2, h, tile_of(n % 2)),
                               part(kT, slice(None), n % NB), True, True)
                last.then_inc(s.scored, 1)

            def turn_p(g, n):
                pe.wait_ge(s.p_ready, nth(g, N, n + 1))
                pe.wait_ge(s.pT_split, primed(g, N, n))
                for j in range(2):
                    for h in range(QUAD):
                        last = pe.transpose(PT[:, j, tile_of(h)], probs[:, h, tile_of(j)], M.ident[:])
                last.then_inc(s.p_turned, 1)

            def weigh_v(g, n):
                pe.wait_ge(s.pT_split, primed(g, N, n + 1))
                pe.wait_ge(s.oT_split, primed(g, N, n))
                for j in range(2):
                    last = mm3(pe, O, part(v, slice(None), n % NB, j), part(pT, slice(None), j), j == 0, j == 1)
                last.then_inc(s.o_made, 1)

            def project_out(g, n):
                pe.wait_ge(s.oT_split, primed(g, N, n + 1))
                pe.wait_ge(s.y_added, primed(g, N, n))
                for h in range(QUAD):
                    if n % NB == 0:
                        pe.wait_ge(s.wo_split, primed(g, 2 * QUAD, n // NB * QUAD + h + 1))
                    last = mm3(pe, Y, part(oT, slice(None), tile_of(h)), part(w_o, slice(None), h), h == 0, h == QUAD - 1)
                last.then_inc(s.y_made, 1)

            def turn(g):
                pe.wait_ge(s.kv_split, primed(g, 1, 1))
                pe.wait_ge(s.q_split, primed(g, NQ, AHEAD))
                for n, (w, src, half) in enumerate(PIECES):
                    pe.wait_ge(s.kvp_split, primed(g, len(PIECES), max(n - 1, 0)))
                    source = (M.cT, M.nT)[src]
                    if w == 0:
                        for k in range(KC):
                            last = mm3(pe, PROJ[n % 2], part(w_kv, slice(None), k, 0),
                                       part(source, slice(None), k, slice(half * HALF, (half + 1) * HALF)),
                                       k == 0, k == KC - 1)
                    else:
                        for j in range(4):
                            for k in range(KC):
                                last = mm3(pe, PROJ[n % 2][:, tile_of(j)], part(source, slice(None), k, tile_of(half * 4 + j)),
                                           part(w_kv, slice(None), k, 1), k == 0, k == KC - 1)
                    last.then_inc(s.kvp_made, 1)
                    if n + 1 == FIRST_SCORE:
                        pe.wait_ge(s.kvp_split, primed(g, len(PIECES), 4))
                        score(g, 0)
                pe.wait_ge(s.kvp_split, primed(g, len(PIECES), len(PIECES)))
                for n in range(N):
                    turn_p(g, n)
                    for j in query_pieces(g, n)[0:1]:
                        project_q(g, j)
                    if n + 1 < N:
                        score(g, n + 1)
                    weigh_v(g, n)
                    for j in query_pieces(g, n)[1:2]:
                        project_q(g, j)
                    project_out(g, n)

            for j in range(AHEAD):
                project_q(0, j)
            run(pe, turn)

        @block.scalar
        def _(act):
            def hi_q(g, j):
                act.wait_ge(s.q_made, primed(g, NQ, j + 1))
                act.activation(qT[0][:, j // QUAD % 2, j % QUAD, :], PROJ[j % 2][:, 0:PAIR], ACT.Copy,
                               scale=SCALE).then_inc(s.q_hi, 1)

            def hi_wq(g, quad, h):
                act.wait_ge(s.q_loaded, nth(g, 32, 16 * (quad + 1)))
                if quad:
                    act.wait_ge(s.q_made, primed(g, NQ, QUAD * (4 * quad - 1) + h + 1))
                act.activation(w_q[0][:, :, tile_of(h)], raw_q[:, :, tile_of(h)], ACT.Copy).then_inc(s.wq_hi, 1)

            def hi_wo(g, quad, h):
                act.wait_ge(s.o_loaded, nth(g, 32, 16 * (quad + 1)))
                act.wait_ge(s.y_made, primed(g, N, NB * quad))
                act.activation(w_o[0][:, h, :], raw_o[:, h, :], ACT.Copy).then_inc(s.wo_hi, 1)

            def hi_kv(g, k):
                act.wait_ge(s.kv_loaded, nth(g, 16, 16 * (k + 1)))
                act.wait_ge(s.kvp_made, primed(g, len(PIECES), len(PIECES) * k))
                act.activation(w_kv[0][:], raw_kv[:], ACT.Copy).then_inc(s.kv_hi, 1)

            def exps(g, n):
                act.wait_ge(s.max_ready, nth(g, N, n + 1))
                for h in range(QUAD):
                    act.activation(probs[:, h, :], scores[:, h, :], ACT.Exp, bias=neg_max[:, h:h + 1],
                                   accum_out=sums[:, h:h + 1]).then_inc(s.exped, 1)

            def turn(g):
                for n, (w, src, half) in enumerate(PIECES):
                    act.wait_ge(s.kvp_made, primed(g, len(PIECES), n + 1))
                    dst = (kT, v)[w][0][:, half * 4:half * 4 + 4, src, :]
                    act.activation(dst, PROJ[n % 2].rearrange("p (b n) -> p b n", b=4), ACT.Copy).then_inc(s.kvp_hi, 1)
                    if n + 1 == FIRST_SCORE:
                        exps(g, 0)
                for n in range(N):
                    act.wait_ge(s.p_turned, nth(g, N, n + 1))
                    act.activation(pT[0][:], PT, ACT.Copy).then_inc(s.pT_hi, 1)
                    if n % NB == 0:
                        for h in range(QUAD):
                            hi_wo(g, n // NB, h)
                    if n % NB in (4, 5) and (n < NB or g is not LAST):
                        for h in range(2):
                            hi_wq(g, n // NB + 1, 2 * (n % NB - 4) + h)
                    for j in query_pieces(g, n)[0:1]:
                        hi_q(g, j)
                    act.wait_ge(s.o_made, nth(g, N, n + 1))
                    act.activation(oT[0][:], O, ACT.Copy).then_inc(s.oT_hi, 1)
                    if n + 1 < N:
                        exps(g, n + 1)
                    for j in query_pieces(g, n)[1:2]:
                        hi_q(g, j)
                    if n == NB + 1 and g is not LAST:
                        hi_kv(g, 1)

            for h in range(QUAD):
                hi_wq(0, 0, h)
            for j in range(2):
                hi_q(0, j)
            hi_kv(0, 0)
            for j in range(2, AHEAD):
                hi_q(0, j)
            run(act, turn)

        @block.gpsimd
        def _(pool):
            def lo_wq(g, quad, h):
                pool.wait_ge(s.wq_hi, nth(g, 2 * QUAD, QUAD * quad + h + 1))
                pool.tensor_tensor(w_q[1][:, :, tile_of(h)], raw_q[:, :, tile_of(h)], f32(w_q[0][:, :, tile_of(h)]),
                                   ALU.subtract).then_inc(s.wq_split, 1)

            def turn(g):
                for n in range(N):
                    if n % NB == 0:
                        for h in range(QUAD):
                            pool.wait_ge(s.wo_hi, nth(g, 2 * QUAD, QUAD * (n // NB) + h + 1))
                            pool.tensor_tensor(w_o[1][:, h, :], raw_o[:, h, :], f32(w_o[0][:, h, :]),
                                               ALU.subtract).then_inc(s.wo_split, 1)
                    if n % NB in (4, 5) and (n < NB or g is not LAST):
                        for h in range(2):
                            lo_wq(g, n // NB + 1, 2 * (n % NB - 4) + h)
                    if n == NB + 1 and g is not LAST:
                        pool.wait_ge(s.kv_hi, nth(g, 1, 2))
                        pool.tensor_tensor(w_kv[1][:], raw_kv[:], f32(w_kv[0][:]), ALU.subtract).then_inc(s.kv_split, 1)

            run(pool, turn)

        @block.vector
        def _(dve):
            def lo_q(g, j):
                dve.wait_ge(s.q_hi, nth(g, NQ, j + 1))
                slot, h = j // QUAD % 2, j % QUAD
                dve.scalar_tensor_tensor(out=qT[1][:, slot, h, :], in0=PROJ[j % 2][:, 0:PAIR], scalar=SCALE,
                                         in1=f32(qT[0][:, slot, h, :]), op0=ALU.mult, op1=ALU.subtract).then_inc(s.q_split, 1)

            def row_max(g, n):
                dve.wait_ge(s.scored, nth(g, N, n + 1))
                dve.tensor_reduce(neg_max[:], scores, AX.X, ALU.max, negate=True).then_inc(s.max_ready, 1)

            def normalize(g, n):
                dve.wait_ge(s.exped, primed(g, N * QUAD, QUAD * (n + 1)))
                dve.reciprocal(inv_sums[:], sums[:]).then_inc(s.inverted, 1)
                dve.wait_ge(s.inverted, nth(g, N, n + 1))
                dve.tensor_tensor(probs[:], probs[:], inv_sums[:].unsqueeze(2).to_broadcast([P, QUAD, KEYS]),
                                  ALU.mult).then_inc(s.p_ready, 1)

            def add_y(g, n):
                x = M.x[:, n % NB, :]
                dve.wait_ge(s.y_made, primed(g, N, n + 1))
                dve.tensor_tensor(x, x, Y, ALU.add).then_inc(s.y_added, 1)

            def turn(g):
                for n, (w, src, half) in enumerate(PIECES):
                    dve.wait_ge(s.kvp_hi, nth(g, len(PIECES), n + 1))
                    tiles = slice(half * 4, half * 4 + 4)
                    dve.tensor_tensor((kT, v)[w][1][:, tiles, src, :], PROJ[n % 2].rearrange("p (b n) -> p b n", b=4),
                                      f32((kT, v)[w][0][:, tiles, src, :]), ALU.subtract).then_inc(s.kvp_split, 1)
                    if n + 1 == FIRST_SCORE:
                        row_max(g, 0)
                        normalize(g, 0)
                for n in range(N):
                    if n:
                        add_y(g, n - 1)
                    dve.wait_ge(s.pT_hi, nth(g, N, n + 1))
                    dve.tensor_tensor(pT[1][:], PT, f32(pT[0][:]), ALU.subtract).then_inc(s.pT_split, 1)
                    for j in query_pieces(g, n)[0:1]:
                        lo_q(g, j)
                    if n + 1 < N:
                        row_max(g, n + 1)
                    dve.wait_ge(s.oT_hi, nth(g, N, n + 1))
                    dve.tensor_tensor(oT[1][:], O, f32(oT[0][:]), ALU.subtract).then_inc(s.oT_split, 1)
                    if n + 1 < N:
                        normalize(g, n + 1)
                    for j in query_pieces(g, n)[1:2]:
                        lo_q(g, j)
                add_y(g, N - 1)

            for h in range(QUAD):
                dve.wait_ge(s.wq_hi, h + 1)
                dve.tensor_tensor(w_q[1][:, :, tile_of(h)], raw_q[:, :, tile_of(h)], f32(w_q[0][:, :, tile_of(h)]),
                                  ALU.subtract).then_inc(s.wq_split, 1)
            for j in range(2):
                lo_q(0, j)
            dve.wait_ge(s.kv_hi, 1)
            dve.tensor_tensor(w_kv[1][:], raw_kv[:], f32(w_kv[0][:]), ALU.subtract).then_inc(s.kv_split, 1)
            for j in range(2, AHEAD):
                lo_q(0, j)
            run(dve, turn)



QMAX_ACT = 65535.0
I2 = 1376
C2 = -(-I2 // P)
BLOCK = 32


def quant_params(pool, s, T, peak, q, factor=None):
    def step(ins):
        T.steps += 1
        ins.then_inc(s.param_step, 1)
        pool.wait_ge(s.param_step, T.steps)

    step(pool.partition_all_reduce(T.peak[:], peak, P, bass.bass_isa.ReduceOp.max))
    step(pool.tensor_scalar(T.peak[:], T.peak[:], 0.0, None, ALU.max))
    if factor is not None:
        step(pool.tensor_scalar(T.peak[:], T.peak[:], factor, None, ALU.mult))
    step(pool.tensor_tensor(T.range[:], T.peak[:, 0:1], T.peak[:, 1:2], ALU.add))
    step(pool.tensor_scalar(q[:, 1:2], T.range[:], 1.0 / QMAX_ACT, 1e-12, ALU.mult, ALU.max))
    step(pool.tensor_tensor(q[:, 0:1], q[:, 1:2], T.const[:, 1:2], ALU.pow))
    step(pool.tensor_tensor(T.zero_point[:], T.peak[:, 1:2], q[:, 0:1], ALU.mult))
    step(pool.tensor_scalar(T.zero_point[:], T.zero_point[:], ROUND, -ROUND, ALU.add, ALU.add))
    step(pool.tensor_scalar(T.zero_point[:], T.zero_point[:], QMAX_ACT, -1.0, ALU.min, ALU.mult))
    step(pool.tensor_scalar(q[:, 2:3], T.zero_point[:], QMAX_ACT, None, ALU.add))


def round_up_part(act, out, in_, scale, T):
    return act.activation(out, in_, ACT.Identity, scale=scale, bias=T.const[:, 2:3])


def integer_part(dve, out, in_, limit):
    return dve.tensor_scalar(out, in_, -ROUND, limit, ALU.add, ALU.min)


def block_quant(dve, pool, s, W, raw, width, n):
    nb = width // BLOCK
    blocks = raw.rearrange("p (b k) -> p b k", k=BLOCK)
    wq = W.wq[:, 0:width].rearrange("p (b k) -> p b k", k=BLOCK)
    scale, inv = W.scale[:, 0:nb], W.inv[:, 0:nb]
    if dve is not None:
        dve.tensor_reduce(W.amax[:, 0:nb], blocks, AX.X, ALU.max, apply_absolute_value=True).then_inc(s.amax_ready, 1)
        dve.wait_ge(s.amax_ready, n(1))
        dve.tensor_scalar(scale, W.amax[:, 0:nb], 1.0 / 7.0, 1e-12, ALU.mult, ALU.max).then_inc(s.scale_ready, 1)
        dve.wait_ge(s.scale_ready, n(1))
        dve.reciprocal(inv, scale).then_inc(s.inverted, 1)
        dve.wait_ge(s.inverted, n(1))
        dve.tensor_tensor(wq, blocks, inv.unsqueeze(2).to_broadcast([P, nb, BLOCK]), ALU.mult).then_inc(s.scaled, 1)
        dve.wait_ge(s.scaled, n(1))
        dve.tensor_scalar(wq, wq, ROUND, -ROUND, ALU.add, ALU.add).then_inc(s.rounded, 1)
    if pool is not None:
        pool.wait_ge(s.rounded, n(1))
        pool.tensor_tensor(wq, wq, scale.unsqueeze(2).to_broadcast([P, nb, BLOCK]), ALU.mult).then_inc(s.wq_ready, 1)


def weight_buffers(S, width, raws):
    W = Named()
    W.raw = S.sb("raw", [P, raws, width])
    W.wq = S.sb("wq", [P, width])
    W.amax = S.sb("amax", [P, width // BLOCK])
    W.scale = S.sb("scale", [P, width // BLOCK])
    W.inv = S.sb("inv", [P, width // BLOCK])
    return W


def ffn2_down_weights(nc, M, A, w_d):
    with ExitStack() as ctx:
        S = Scope(nc, M, ctx, "f2w")
        s = Named()
        s.raw_loaded, s.amax_ready, s.scale_ready, s.inverted = S.sems("raw_loaded amax_ready scale_ready inverted")
        s.scaled, s.rounded, s.wq_ready, s.turned, s.w_hi = S.sems("scaled rounded wq_ready turned w_hi")
        [s.w_split] = S.sems("w_split")
        W = weight_buffers(S, C2 * P, 2)
        GROUPS = [range(j, min(j + 4, C2)) for j in range(0, C2, 4)]
        block = S.block()

        @block.sync
        def _(sp):
            for o in range(KC):
                if o >= 2:
                    sp.wait_ge(s.scaled, o - 1)
                sp.dma_start(W.raw[:, o % 2, :], A["L2_ffn_down"][o]).then_inc(s.raw_loaded, 16)
                sp.wait_ge(s.raw_loaded, 16 * (o + 1))

        @block.gpsimd
        def _(pool):
            for o in range(KC):
                block_quant(None, pool, s, W, W.raw[:, o % 2, :], C2 * P, lambda k, o=o: o + k)

        @block.vector
        def _(dve):
            for o in range(KC):
                dve.wait_ge(s.raw_loaded, 16 * (o + 1))
                if o:
                    dve.wait_ge(s.turned, len(GROUPS) * o)
                block_quant(dve, None, s, W, W.raw[:, o % 2, :], C2 * P, lambda k, o=o: o + k)
                for i, js in enumerate(GROUPS):
                    n = len(GROUPS) * o + i
                    dve.wait_ge(s.w_hi, n + 1)
                    dst = slice(js[0], js[-1] + 1)
                    dve.tensor_tensor(w_d[1][:, dst, tile_of(o)],
                                      M.bank[n % 3][:, 0:len(js) * P].rearrange("p (j o) -> p j o", o=P),
                                      f32(w_d[0][:, dst, tile_of(o)]), ALU.subtract).then_inc(s.w_split, 1)

        @block.tensor
        def _(pe):
            for o in range(KC):
                pe.wait_ge(s.wq_ready, o + 1)
                for i, js in enumerate(GROUPS):
                    n = len(GROUPS) * o + i
                    if n >= 3:
                        pe.wait_ge(s.w_split, n - 2)
                    for j in js:
                        last = pe.transpose(M.bank[n % 3][:, tile_of(j - js[0])], W.wq[:, tile_of(j)], M.ident[:])
                    last.then_inc(s.turned, 1)

        @block.scalar
        def _(act):
            for o in range(KC):
                for i, js in enumerate(GROUPS):
                    n = len(GROUPS) * o + i
                    act.wait_ge(s.turned, n + 1)
                    act.activation(w_d[0][:, js[0]:js[-1] + 1, tile_of(o)],
                                   M.bank[n % 3][:, 0:len(js) * P].rearrange("p (j o) -> p j o", o=P),
                                   ACT.Copy).then_inc(s.w_hi, 1)


def ffn2_quantise_input(nc, M, T, xn):
    with ExitStack() as ctx:
        S = Scope(nc, M, ctx, "f2q")
        s = Named()
        s.const_set, s.peak_ready, s.param_step = S.sems("const_set peak_ready param_step")
        s.params_ready, s.shifted = S.sems("params_ready shifted")
        peak = S.sb("peak", [P, 2])
        block = S.block()

        @block.gpsimd
        def _(pool):
            for i, value in enumerate((0.0, -1.0, ROUND)):
                pool.memset(T.const[:, i:i + 1], value).then_inc(s.const_set, 1)
            pool.wait_ge(s.const_set, 3)
            pool.wait_ge(s.peak_ready, 2)
            T.steps = 0
            quant_params(pool, s, T, peak[:], T.q_x)
            pool.memset(T.peak[:, 0:1], 0.0).then_inc(s.params_ready, 1)

        @block.vector
        def _(dve):
            dve.tensor_reduce(peak[:, 0:1], xn[:], AX.XY, ALU.max).then_inc(s.peak_ready, 1)
            dve.tensor_reduce(peak[:, 1:2], xn[:], AX.XY, ALU.min, negate=True).then_inc(s.peak_ready, 1)
            dve.wait_ge(s.params_ready, 1)
            for b in range(NB):
                dve.wait_ge(s.shifted, b + 1)
                integer_part(dve, xn[:, b, :], xn[:, b, :], T.q_x[:, 2:3])

        @block.scalar
        def _(act):
            act.wait_ge(s.params_ready, 1)
            for b in range(NB):
                round_up_part(act, xn[:, b, :], xn[:, b, :], T.q_x[:, 0:1], T).then_inc(s.shifted, 1)


def ffn2_gate_up(nc, M, A, T, hidden, peaks):
    with ExitStack() as ctx:
        S = Scope(nc, M, ctx, "f2g")
        s = Named()
        s.raw_loaded, s.w_hi, s.made, s.copied = S.sems("raw_loaded w_hi made copied")
        s.amax_ready, s.scale_ready, s.inverted = S.sems("amax_ready scale_ready inverted", primed=True)
        s.scaled, s.rounded, s.wq_ready, s.turned = S.sems("scaled rounded wq_ready turned", primed=True)
        s.w_split, s.peaked = S.sems("w_split peaked", primed=True)
        W = weight_buffers(S, D, 2)
        wT = S.pair("wT", [P, 2, KC, P])
        TURN = M.bank[0]
        OUT = [[M.bank[1], M.bank[2]], [M.bank[3], M.bank[4]]]
        LAST = 2 * C2
        block = S.block()

        @block.sync
        def _(sp):
            with sp.Fori(0, C2) as j:
                for w in range(2):
                    sp.wait_ge(s.scaled, primed(j, 2, 0))
                    sp.dma_start(W.raw[:, w, :], A["L2_ffn_gate_up"][bass.ds(j, 1), w].rearrange("g p n -> (g p) n")
                                 ).then_inc(s.raw_loaded, 16)

        @block.gpsimd
        def _(pool):
            with pool.Fori(0, C2) as j:
                for w in range(2):
                    block_quant(None, pool, s, W, W.raw[:, w, :], D, lambda k: primed(j, 2, w + k))

        @block.vector
        def _(dve):
            def weights(j, w):
                dve.wait_ge(s.raw_loaded, nth(j, 32, 32))
                dve.wait_ge(s.turned, primed(j, 2, w))
                block_quant(dve, None, s, W, W.raw[:, w, :], D, lambda k: primed(j, 2, w + k))
                dve.wait_ge(s.w_hi, nth(j, 2, w + 1))
                dve.tensor_tensor(wT[1][:, w], TURN.rearrange("p (c n) -> p c n", c=KC), f32(wT[0][:, w]),
                                  ALU.subtract).then_inc(s.w_split, 1)

            def peaks_of(j, w):
                for half in range(2):
                    dve.wait_ge(s.copied, nth(j, 4, 2 * w + half + 1))
                    col = peaks[:, w, :, bass.ds(j * 2 + half, 1)]
                    dve.tensor_reduce(col[:, 0, :], OUT[w][half], AX.X, ALU.max).then_inc(s.peaked, 1)
                    dve.tensor_reduce(col[:, 1, :], OUT[w][half], AX.X, ALU.min, negate=True).then_inc(s.peaked, 1)

            weights(0, 0)
            weights(0, 1)
            peaks_of(0, 0)
            with dve.Fori(1, C2) as j:
                weights(j, 0)
                peaks_of(j - 1, 1)
                weights(j, 1)
                peaks_of(j, 0)
            peaks_of(C2 - 1, 1)

        @block.tensor
        def _(pe):
            def turn(j, w):
                pe.wait_ge(s.wq_ready, primed(j, 2, w + 1))
                pe.wait_ge(s.w_split, primed(j, 2, w))
                for c in range(KC):
                    last = pe.transpose(TURN[:, tile_of(c)], W.wq[:, tile_of(c)], M.ident[:])
                last.then_inc(s.turned, 1)

            def product(j, w):
                pe.wait_ge(s.w_split, primed(j, 2, w + 1))
                for half in range(2):
                    pe.wait_ge(s.peaked, primed(j, 8, 0))
                    for c in range(KC):
                        last = mm3(pe, OUT[w][half], part(wT, slice(None), w, c),
                                   part(M.nT, slice(None), c, slice(half * HALF, (half + 1) * HALF)),
                                   c == 0, c == KC - 1)
                    last.then_inc(s.made, 1)

            turn(0, 0)
            turn(0, 1)
            product(0, 0)
            with pe.Fori(1, C2) as j:
                turn(j, 0)
                product(j - 1, 1)
                turn(j, 1)
                product(j, 0)
            product(C2 - 1, 1)

        @block.scalar
        def _(act):
            def hi(j, w):
                act.wait_ge(s.turned, primed(j, 2, w + 1))
                act.activation(wT[0][:, w], TURN.rearrange("p (c n) -> p c n", c=KC), ACT.Copy).then_inc(s.w_hi, 1)

            def copy_out(j, w):
                for half in range(2):
                    act.wait_ge(s.made, nth(j, 4, 2 * w + half + 1))
                    act.activation(hidden[w][:, bass.ds(j * TOK + half * HALF, HALF)], OUT[w][half], ACT.Copy,
                                   scale=T.q_x[:, 1:2]).then_inc(s.copied, 1)

            hi(0, 0)
            hi(0, 1)
            copy_out(0, 0)
            with act.Fori(1, C2) as j:
                hi(j, 0)
                copy_out(j - 1, 1)
                hi(j, 1)
                copy_out(j, 0)
            copy_out(C2 - 1, 1)


def ffn2_down(nc, M, T, hidden, peaks, w_d):
    with ExitStack() as ctx:
        S = Scope(nc, M, ctx, "f2d")
        s = Named()
        s.peak_ready, s.param_step, s.params_ready = S.sems("peak_ready param_step params_ready")
        s.u_shifted, s.u_int, s.g_shifted, s.g_int, s.sig_made = S.sems("u_shifted u_int g_shifted g_int sig_made")
        s.sig_shifted, s.sig_int, s.s_made, s.s_peaked = S.sems("sig_shifted sig_int s_made s_peaked")
        s.s_shifted, s.s_int, s.o_made, s.o_peaked, s.o_shifted = S.sems("s_shifted s_int o_made o_peaked o_shifted")
        s.o_int, s.o_hi, s.o_split, s.y_made, s.y_added = S.sems("o_int o_hi o_split y_made y_added")
        peak = S.sb("peak", [P, 2, 2])
        q = S.sb("q", [P, 4, 3])
        sg = S.sb("sg", [P, 1])
        so = S.sb("so", [P, 1])
        sig = S.sb("sig", [P, 2, TOK])
        o_hi_lo = M.nT
        gate, up = hidden
        q_g, q_u, q_s, q_o = (q[:, i] for i in range(4))
        Y = M.bank
        block = S.block()

        def at(t, j):
            return t[:, j * TOK:(j + 1) * TOK]

        @block.gpsimd
        def _(pool):
            T.steps = 0

            def params(n, w, q, factor):
                pool.wait_ge(s.peak_ready, n)
                quant_params(pool, s, T, peak[:, w], q, factor)

            params(2, 0, q_g, T.q_x[:, 1:2])
            pool.tensor_scalar(sg[:], q_g[:, 1:2], 2.0 ** -16, None, ALU.mult).then_inc(s.params_ready, 1)
            params(4, 1, q_u, T.q_x[:, 1:2])
            pool.memset(T.peak[:, 0:1], 0.0).then_inc(s.params_ready, 1)
            params(6, 0, q_s, None)
            pool.memset(T.peak[:, 0:1], 0.0).then_inc(s.params_ready, 1)
            params(8, 1, q_o, q_u[:, 1:2])
            pool.tensor_scalar(so[:], q_o[:, 0:1], q_u[:, 1:2], None, ALU.mult).then_inc(s.params_ready, 1)

        @block.scalar
        def _(act):
            act.wait_ge(s.params_ready, 1)
            for j in range(C2):
                round_up_part(act, at(gate, j), at(gate, j), q_g[:, 0:1], T).then_inc(s.g_shifted, 1)
            act.wait_ge(s.params_ready, 2)
            for j in range(C2):
                act.wait_ge(s.g_int, j + 1)
                if j >= 2:
                    act.wait_ge(s.s_made, j - 1)
                act.activation(sig[:, j % 2, :], at(gate, j), ACT.Sigmoid, scale=q_g[:, 1:2]).then_inc(s.sig_made, 1)
                act.wait_ge(s.sig_made, j + 1)
                act.activation(sig[:, j % 2, :], sig[:, j % 2, :], ACT.Identity, scale=65536.0,
                               bias=T.const[:, 2:3]).then_inc(s.sig_shifted, 1)
                round_up_part(act, at(up, j), at(up, j), q_u[:, 0:1], T).then_inc(s.u_shifted, 1)
            act.wait_ge(s.params_ready, 3)
            for j in range(C2):
                round_up_part(act, at(gate, j), at(gate, j), q_s[:, 0:1], T).then_inc(s.s_shifted, 1)
            act.wait_ge(s.params_ready, 4)
            for j in range(C2):
                round_up_part(act, at(gate, j), at(gate, j), so[:], T).then_inc(s.o_shifted, 1)
                act.wait_ge(s.o_int, j + 1)
                if j >= 4:
                    act.wait_ge(s.y_made, NB * (j - 3))
                act.activation(o_hi_lo[0][:, j % 4, :], at(gate, j), ACT.Copy).then_inc(s.o_hi, 1)

        @block.vector
        def _(dve):
            for n, (w, row) in enumerate(((0, 0), (0, 1), (1, 0), (1, 1))):
                dve.tensor_reduce(peak[:, w, row:row + 1], peaks[:, w, row, :], AX.X, ALU.max).then_inc(s.peak_ready, 1)
            for j in range(C2):
                dve.wait_ge(s.g_shifted, j + 1)
                integer_part(dve, at(gate, j), at(gate, j), q_g[:, 2:3]).then_inc(s.g_int, 1)
            for j in range(C2):
                dve.wait_ge(s.u_shifted, j + 1)
                integer_part(dve, at(up, j), at(up, j), q_u[:, 2:3]).then_inc(s.u_int, 1)
                dve.wait_ge(s.sig_shifted, j + 1)
                integer_part(dve, sig[:, j % 2, :], sig[:, j % 2, :], QMAX_ACT).then_inc(s.sig_int, 1)
                dve.wait_ge(s.sig_int, j + 1)
                dve.scalar_tensor_tensor(out=at(gate, j), in0=at(gate, j), scalar=sg[:], in1=sig[:, j % 2, :],
                                         op0=ALU.mult, op1=ALU.mult).then_inc(s.s_made, 1)
                dve.wait_ge(s.s_made, j + 1)
                dve.tensor_reduce(peaks[:, 0, 0, j:j + 1], at(gate, j), AX.X, ALU.max).then_inc(s.s_peaked, 1)
                dve.tensor_reduce(peaks[:, 0, 1, j:j + 1], at(gate, j), AX.X, ALU.min, negate=True).then_inc(s.s_peaked, 1)
            dve.wait_ge(s.s_peaked, 2 * C2)
            dve.wait_ge(s.params_ready, 1)
            for row in range(2):
                dve.tensor_reduce(peak[:, 0, row:row + 1], peaks[:, 0, row, 0:C2], AX.X, ALU.max).then_inc(s.peak_ready, 1)
            for j in range(C2):
                dve.wait_ge(s.s_shifted, j + 1)
                integer_part(dve, at(gate, j), at(gate, j), q_s[:, 2:3]).then_inc(s.s_int, 1)
                dve.wait_ge(s.s_int, j + 1)
                dve.wait_ge(s.u_int, j + 1)
                dve.scalar_tensor_tensor(out=at(gate, j), in0=at(gate, j), scalar=q_s[:, 1:2], in1=at(up, j),
                                         op0=ALU.mult, op1=ALU.mult).then_inc(s.o_made, 1)
                dve.wait_ge(s.o_made, j + 1)
                dve.tensor_reduce(peaks[:, 1, 0, j:j + 1], at(gate, j), AX.X, ALU.max).then_inc(s.o_peaked, 1)
                dve.tensor_reduce(peaks[:, 1, 1, j:j + 1], at(gate, j), AX.X, ALU.min, negate=True).then_inc(s.o_peaked, 1)
            dve.wait_ge(s.o_peaked, 2 * C2)
            for row in range(2):
                dve.tensor_reduce(peak[:, 1, row:row + 1], peaks[:, 1, row, 0:C2], AX.X, ALU.max).then_inc(s.peak_ready, 1)
            for j in range(C2):
                dve.wait_ge(s.o_shifted, j + 1)
                integer_part(dve, at(gate, j), at(gate, j), q_o[:, 2:3]).then_inc(s.o_int, 1)
                dve.wait_ge(s.o_hi, j + 1)
                dve.tensor_tensor(o_hi_lo[1][:, j % 4, :], at(gate, j), f32(o_hi_lo[0][:, j % 4, :]),
                                  ALU.subtract).then_inc(s.o_split, 1)
            for b in range(NB):
                dve.wait_ge(s.y_made, NB * (C2 - 1) + b + 1)
                dve.scalar_tensor_tensor(out=M.x[:, b, :], in0=Y[b], scalar=q_o[:, 1:2], in1=M.x[:, b, :],
                                         op0=ALU.mult, op1=ALU.add).then_inc(s.y_added, 1)

        @block.tensor
        def _(pe):
            for j in range(C2):
                pe.wait_ge(s.o_split, j + 1)
                for b in range(NB):
                    mm3(pe, Y[b], part(o_hi_lo, slice(None), j % 4, tile_of(b)), part(w_d, slice(None), j),
                        j == 0, j == C2 - 1).then_inc(s.y_made, 1)


def ffn2_stage(nc, M, A):
    with ExitStack() as ctx:
        S = Scope(nc, M, ctx, "f2")
        T = Named()
        T.q_x = S.sb("q_x", [P, 3])
        T.const = S.sb("const", [P, 3])
        T.peak = S.sb("peak", [P, 2])
        T.range = S.sb("range", [P, 1])
        T.zero_point = S.sb("zero_point", [P, 1])
        with ExitStack() as xn_ctx:
            xn = Scope(nc, M, xn_ctx, "f2x").sb("xn", [P, NB, D])
            norm_stage(nc, M, "n5", xn=xn, turn=False)
            ffn2_quantise_input(nc, M, T, xn)
            norm_stage(nc, M, "t5", xn=xn, normalize=False)
        w_d = S.pair("w_d", [P, C2, D])
        ffn2_down_weights(nc, M, A, w_d)
        hidden = [S.sb(name, [P, C2 * TOK]) for name in ("gate", "up")]
        peaks = S.sb("peaks", [P, 2, 2, 2 * C2])
        ffn2_gate_up(nc, M, A, T, hidden, peaks)
        ffn2_down(nc, M, T, hidden, peaks, w_d)



def attn3_stage(nc, M, A):
    SCALE = 1.0 / float(np.sqrt(D))
    with ExitStack() as ctx:
        S = Scope(nc, M, ctx, "a3")
        raw_w = S.sb("raw_w", [P, KC, D])
        w = S.pair("w", [P, KC, D])
        bias = S.sb("bias", [P, 2, KC])
        bias_q = S.sb("bias_q", [P, KC])
        biased = S.sb("biased", [P, 2, HALF])
        qT = S.pair("qT", [P, KC, TOK])
        kT = S.pair("kT", [P, KC, TOK])
        raw_f = S.sb("raw_f", [P, 2, D])
        feat = S.pair("feat", [P, 2, D])
        neg_max = S.sb("neg_max", [P, 2])
        sums = S.sb("sums", [P, 2])
        inv_sums = S.sb("inv_sums", [P, 2])
        probs = S.sb("probs", [P, 2, P])
        pT = S.pair("pT", [P, P])
        s = Named()
        s.bias_loaded, s.w_loaded, s.f_loaded, s.bias_ready = S.sems("bias_loaded w_loaded f_loaded bias_ready")
        s.w_hi, s.w_split, s.proj_made, s.biased, s.proj_hi = S.sems("w_hi w_split proj_made biased proj_hi")
        s.proj_split, s.f_hi, s.f_split, s.scored, s.max_ready = S.sems("proj_split f_hi f_split scored max_ready")
        s.exped, s.inverted, s.turned, s.pT_hi, s.pT_split = S.sems("exped inverted turned pT_hi pT_split")
        s.y_made, s.y_added = S.sems("y_made y_added")
        block = S.block()
        UNITS = [(i, c, half) for i in range(2) for c in range(KC) for half in range(2)]
        dst = (qT, kT)

        @block.sync
        def _(sp):
            sp.dma_start(bias[:], A["L3_xattn_bias"]).then_inc(s.bias_loaded, 16)
            for i in range(2):
                sp.wait_ge(s.w_split, i)
                sp.dma_start(raw_w[:], A["L3_xattn_Wqk"][i]).then_inc(s.w_loaded, 16)
            for b in range(NB):
                sp.wait_ge(s.f_split, max(b - 1, 0))
                sp.dma_start(raw_f[:, b % 2, :], A["ctx"][b]).then_inc(s.f_loaded, 16)
                sp.wait_ge(s.f_loaded, 16 * (b + 1))

        @block.tensor
        def _(pe):
            for n, (i, c, half) in enumerate(UNITS):
                pe.wait_ge(s.w_split, i + 1)
                if n >= 4:
                    pe.wait_ge(s.biased, n - 3)
                for k in range(KC):
                    last = mm3(pe, M.bank[n % 4], part(w, slice(None), k, tile_of(c)),
                               part((M.nT, M.cT)[i], slice(None), k, slice(half * HALF, (half + 1) * HALF)),
                               k == 0, k == KC - 1)
                last.then_inc(s.proj_made, 1)

            def score(b):
                if b == 0:
                    pe.wait_ge(s.proj_split, len(UNITS))
                if b >= 2:
                    pe.wait_ge(s.exped, b - 1)
                for k in range(KC):
                    last = mm3(pe, M.bank[b % 2][:, 0:P], part(qT, slice(None), k, tile_of(b)),
                               part(kT, slice(None), k, tile_of(b)), k == 0, k == KC - 1)
                last.then_inc(s.scored, 1)

            score(0)
            for b in range(NB):
                if b + 1 < NB:
                    score(b + 1)
                pe.wait_ge(s.exped, b + 1)
                pe.wait_ge(s.pT_split, b)
                pe.transpose(M.bank[4][:, 0:P], probs[:, b % 2, :], M.ident[:]).then_inc(s.turned, 1)
                pe.wait_ge(s.pT_split, b + 1)
                pe.wait_ge(s.f_split, b + 1)
                if b >= 2:
                    pe.wait_ge(s.y_added, b - 1)
                mm3(pe, M.bank[5 + b % 2], (pT[0][:], pT[1][:]), part(feat, slice(None), b % 2), True, True
                    ).then_inc(s.y_made, 1)

        @block.scalar
        def _(act):
            act.wait_ge(s.bias_ready, 1)
            for n, (i, c, half) in enumerate(UNITS):
                if n % 8 == 0:
                    act.wait_ge(s.w_loaded, 16 * (i + 1))
                    act.wait_ge(s.proj_made, n)
                    act.activation(w[0][:], raw_w[:], ACT.Copy).then_inc(s.w_hi, 1)
                act.wait_ge(s.proj_made, n + 1)
                if n >= 2:
                    act.wait_ge(s.proj_split, n - 1)
                act.activation(biased[:, n % 2, :], M.bank[n % 4], ACT.Identity, scale=1.0 if i else SCALE,
                               bias=(bias[:, 1, c:c + 1] if i else bias_q[:, c:c + 1])).then_inc(s.biased, 1)
                act.wait_ge(s.biased, n + 1)
                act.activation(dst[i][0][:, c, half * HALF:(half + 1) * HALF], biased[:, n % 2, :],
                               ACT.Copy).then_inc(s.proj_hi, 1)
            for b in range(NB + 1):
                if b < NB:
                    act.wait_ge(s.max_ready, b + 1)
                    if b >= 2:
                        act.wait_ge(s.turned, b - 1)
                    act.activation(probs[:, b % 2, :], M.bank[b % 2][:, 0:P], ACT.Exp, bias=neg_max[:, b % 2:b % 2 + 1],
                                   accum_out=sums[:, b % 2:b % 2 + 1]).then_inc(s.exped, 1)
                    act.wait_ge(s.f_loaded, 16 * (b + 1))
                    if b >= 2:
                        act.wait_ge(s.y_made, b - 1)
                    act.activation(feat[0][:, b % 2, :], raw_f[:, b % 2, :], ACT.Copy).then_inc(s.f_hi, 1)
                if b:
                    act.wait_ge(s.turned, b)
                    act.activation(pT[0][:], M.bank[4][:, 0:P], ACT.Copy).then_inc(s.pT_hi, 1)

        @block.vector
        def _(dve):
            dve.wait_ge(s.bias_loaded, 16)
            dve.tensor_scalar(bias_q[:], bias[:, 0, :], SCALE, None, ALU.mult).then_inc(s.bias_ready, 1)
            for n, (i, c, half) in enumerate(UNITS):
                if n % 8 == 0:
                    dve.wait_ge(s.w_hi, i + 1)
                    dve.tensor_tensor(w[1][:], raw_w[:], f32(w[0][:]), ALU.subtract).then_inc(s.w_split, 1)
                tokens = slice(half * HALF, (half + 1) * HALF)
                dve.wait_ge(s.proj_hi, n + 1)
                dve.tensor_tensor(dst[i][1][:, c, tokens], biased[:, n % 2, :], f32(dst[i][0][:, c, tokens]),
                                  ALU.subtract).then_inc(s.proj_split, 1)
            for b in range(NB + 1):
                if b < NB:
                    dve.wait_ge(s.scored, b + 1)
                    dve.tensor_reduce(neg_max[:, b % 2:b % 2 + 1], M.bank[b % 2][:, 0:P], AX.X, ALU.max,
                                      negate=True).then_inc(s.max_ready, 1)
                    dve.wait_ge(s.f_hi, b + 1)
                    dve.tensor_tensor(feat[1][:, b % 2, :], raw_f[:, b % 2, :], f32(feat[0][:, b % 2, :]),
                                      ALU.subtract).then_inc(s.f_split, 1)
                if b:
                    a = b - 1
                    dve.wait_ge(s.pT_hi, b)
                    dve.tensor_tensor(pT[1][:], M.bank[4][:, 0:P], f32(pT[0][:]), ALU.subtract).then_inc(s.pT_split, 1)
                    dve.wait_ge(s.exped, b)
                    dve.reciprocal(inv_sums[:, a % 2:a % 2 + 1], sums[:, a % 2:a % 2 + 1]).then_inc(s.inverted, 1)
                    dve.wait_ge(s.inverted, b)
                    dve.wait_ge(s.y_made, b)
                    dve.scalar_tensor_tensor(out=M.x[:, a, :], in0=M.bank[5 + a % 2], scalar=inv_sums[:, a % 2:a % 2 + 1],
                                             in1=M.x[:, a, :], op0=ALU.mult, op1=ALU.add).then_inc(s.y_added, 1)



def ffn3_stage(nc, M, A, xn, rms):
    NS = 4
    W = NS * NS + 2 * NS
    ITERS = 50
    with ExitStack() as ctx:
        S = Scope(nc, M, ctx, "f3")
        raw_w = S.sb("raw_w", [P, KC, W])
        w = S.pair("w", [P, KC, W])
        raw_b = S.sb("raw_b", [P, P])
        w_b = S.pair("w_b", [P, P])
        base = S.sb("base", [P, W])
        gate = S.sb("gate", [P, 1])
        keep = S.sb("keep", [P, 1])
        eye = S.sb("eye", [P, NS * NS])
        logits = S.sb("logits", [P, NB, W])
        L = S.sb("L", [P, NB, NS, NS])
        E = S.sb("E", [P, NB, NS, NS])
        peak = S.sb("peak", [P, NB, NS])
        total = S.sb("total", [P, NB, NS])
        H = S.sb("H", [P, NB, NS * NS])
        pp = S.sb("pp", [P, NB, 2, NS])
        pp_peak = S.sb("pp_peak", [P, NB, 2])
        x_pre = S.sb("x_pre", [P, NB, P])
        xT = S.pair("xT", [P, NB, P])
        s = Named()
        s.w_loaded, s.b_loaded, s.small_loaded, s.w_hi = S.sems("w_loaded b_loaded small_loaded w_hi")
        s.w_split, s.b_hi, s.b_split, s.logits_made, s.small = S.sems("w_split b_hi b_split logits_made small")
        s.pp_less, s.pp_exped, s.gated, s.less_max, s.exped = S.sems("pp_less pp_exped gated less_max exped")
        s.summed, s.logged, s.pre_step, s.x_pre_ready, s.turned = S.sems("summed logged pre_step x_pre_ready turned")
        s.xT_hi, s.xT_split, s.y_made, s.mixed, s.H_exped = S.sems("xT_hi xT_split y_made mixed H_exped")
        [s.stepped] = S.sems("stepped", primed=True)
        block = S.block()
        LOG, YB = M.bank[0], M.psum[:, 1:3, :].rearrange("p a (b n) -> p (a b) n", n=P)
        XT = M.psum[:, 3:5, :].rearrange("p a (b n) -> p (a b) n", n=P)

        @block.sync
        def _(sp):
            sp.dma_start(raw_w[:], A["L3_ffn_W"]).then_inc(s.w_loaded, 16)
            sp.dma_start(raw_b[:], A["L3_ffn_W_branch"]).then_inc(s.b_loaded, 16)
            for t, name in ((base, "L3_ffn_base"), (gate, "L3_ffn_gate"), (eye, "eye")):
                sp.dma_start(t[:], A[name]).then_inc(s.small_loaded, 16)

        @block.tensor
        def _(pe):
            pe.wait_ge(s.w_split, 1)
            for b in range(NB):
                for k in range(KC):
                    last = mm3(pe, LOG[:, b * W:(b + 1) * W], part(M.nT, slice(None), k, tile_of(b)),
                               part(w, slice(None), k), k == 0, k == KC - 1)
            last.then_inc(s.logits_made, 1)
            for b in range(NB):
                pe.wait_ge(s.x_pre_ready, b + 1)
                last = pe.transpose(XT[:, b, :], x_pre[:, b, :], M.ident[:])
            last.then_inc(s.turned, 1)
            pe.wait_ge(s.b_split, 1)
            pe.wait_ge(s.xT_split, 1)
            for b in range(NB):
                last = mm3(pe, YB[:, b, :], part(xT, slice(None), b), (w_b[0][:], w_b[1][:]), True, True)
            last.then_inc(s.y_made, 1)

        @block.scalar
        def _(act):
            act.wait_ge(s.w_loaded, 16)
            act.activation(w[0][:], raw_w[:], ACT.Copy).then_inc(s.w_hi, 1)
            act.wait_ge(s.b_loaded, 16)
            act.activation(w_b[0][:], raw_b[:], ACT.Copy).then_inc(s.b_hi, 1)
            act.wait_ge(s.small_loaded, 48)
            act.activation(gate[:], gate[:], ACT.Sigmoid).then_inc(s.gated, 1)
            act.wait_ge(s.pp_less, 1)
            act.activation(pp[:], pp[:], ACT.Exp).then_inc(s.pp_exped, 1)
            act.wait_ge(s.turned, 1)
            act.activation(xT[0][:], XT, ACT.Copy).then_inc(s.xT_hi, 1)
            act.preload_act_table_set("natural_log_exp_and_others")
            with act.Fori(0, ITERS) as i:
                for k in range(2):
                    act.wait_ge(s.less_max, nth(i, 2, k + 1))
                    act.activation(E[:], L[:], ACT.Exp).then_inc(s.exped, 1)
                    act.wait_ge(s.summed, nth(i, 2, k + 1))
                    act.activation(total[:], total[:], ACT.Ln).then_inc(s.logged, 1)
            act.wait_ge(s.stepped, primed(0, 0, 4 * ITERS))
            act.activation(E[:], L[:], ACT.Exp).then_inc(s.H_exped, 1)

        @block.vector
        def _(dve):
            steps = [0]

            def step(ins):
                ins.then_inc(s.small, 1)
                steps[0] += 1
                dve.wait_ge(s.small, steps[0])

            dve.wait_ge(s.w_hi, 1)
            dve.tensor_tensor(w[1][:], raw_w[:], f32(w[0][:]), ALU.subtract).then_inc(s.w_split, 1)
            dve.wait_ge(s.b_hi, 1)
            dve.tensor_tensor(w_b[1][:], raw_b[:], f32(w_b[0][:]), ALU.subtract).then_inc(s.b_split, 1)
            dve.wait_ge(s.small_loaded, 48)
            dve.wait_ge(s.gated, 1)
            step(dve.tensor_scalar(keep[:], gate[:], -1.0, 1.0, ALU.mult, ALU.add))
            step(dve.tensor_scalar(eye[:], eye[:], keep[:], None, ALU.mult))
            dve.wait_ge(s.logits_made, 1)
            step(dve.tensor_tensor(logits[:], LOG[:, 0:NB * W].rearrange("p (b n) -> p b n", n=W),
                                   rms[:].unsqueeze(2).to_broadcast([P, NB, W]), ALU.mult))
            step(dve.tensor_tensor(logits[:], logits[:], base[:].unsqueeze(1).to_broadcast([P, NB, W]), ALU.add))
            pre_post = logits[:, :, NS * NS:W].rearrange("p b (k n) -> p b k n", n=NS)
            step(dve.tensor_reduce(pp_peak[:], pre_post, AX.X, ALU.max))
            dve.tensor_tensor(pp[:], pre_post, pp_peak[:].unsqueeze(3).to_broadcast([P, NB, 2, NS]),
                              ALU.subtract).then_inc(s.pp_less, 1)
            step(dve.tensor_scalar(L[:].rearrange("p b i j -> p b (i j)"), logits[:, :, 0:NS * NS], 10.0, None, ALU.mult))
            dve.wait_ge(s.pp_exped, 1)
            step(dve.tensor_reduce(pp_peak[:], pp[:], AX.X, ALU.add))
            step(dve.reciprocal(pp_peak[:], pp_peak[:]))
            step(dve.tensor_tensor(pp[:], pp[:], pp_peak[:].unsqueeze(3).to_broadcast([P, NB, 2, NS]), ALU.mult))
            for n in range(NS):
                for b in range(NB):
                    stream = xn[:, b, tile_of(n)]
                    if n:
                        dve.wait_ge(s.pre_step, NB * (n - 1) + b + 1)
                        ins = dve.scalar_tensor_tensor(out=x_pre[:, b, :], in0=stream, scalar=pp[:, b, 0, n:n + 1],
                                                       in1=x_pre[:, b, :], op0=ALU.mult, op1=ALU.add)
                    else:
                        ins = dve.tensor_scalar(x_pre[:, b, :], stream, pp[:, b, 0, n:n + 1], None, ALU.mult)
                    ins.then_inc(s.pre_step if n < NS - 1 else s.x_pre_ready, 1)
            dve.wait_ge(s.xT_hi, 1)
            dve.tensor_tensor(xT[1][:], XT, f32(xT[0][:]), ALU.subtract).then_inc(s.xT_split, 1)
            dve.wait_ge(s.y_made, 1)
            for n in range(NS):
                for b in range(NB):
                    dve.scalar_tensor_tensor(out=M.x[:, b, tile_of(n)], in0=YB[:, b, :], scalar=pp[:, b, 1, n:n + 1],
                                             in1=M.x[:, b, tile_of(n)], op0=ALU.mult, op1=ALU.add).then_inc(s.mixed, 1)
            with dve.Fori(0, ITERS) as i:
                for k in range(2):
                    view = (lambda t: t[:]) if k == 0 else (lambda t: t[:].rearrange("p b i j -> p b j i"))
                    spread = (lambda t: t[:].unsqueeze(3).to_broadcast([P, NB, NS, NS]))
                    dve.wait_ge(s.stepped, primed(i, 4, 2 * k))
                    dve.tensor_reduce(peak[:], view(L), AX.X, ALU.max).then_inc(s.stepped, 1)
                    dve.wait_ge(s.stepped, primed(i, 4, 2 * k + 1))
                    dve.tensor_tensor(view(L), view(L), spread(peak), ALU.subtract).then_inc(s.less_max, 1)
                    dve.wait_ge(s.exped, nth(i, 2, k + 1))
                    dve.tensor_reduce(total[:], view(E), AX.X, ALU.add).then_inc(s.summed, 1)
                    dve.wait_ge(s.logged, nth(i, 2, k + 1))
                    dve.tensor_tensor(view(L), view(L), spread(total), ALU.subtract).then_inc(s.stepped, 1)
            dve.wait_ge(s.H_exped, 1)
            step(dve.tensor_scalar(H[:], E[:].rearrange("p b i j -> p b (i j)"), gate[:], None, ALU.mult))
            step(dve.tensor_tensor(H[:], H[:], eye[:].unsqueeze(1).to_broadcast([P, NB, NS * NS]), ALU.add))
            for j in range(NS):
                for n in range(NS):
                    for b in range(NB):
                        dve.wait_ge(s.mixed, NB * NS * j + NB * n + b + 1)
                        dve.scalar_tensor_tensor(out=M.x[:, b, tile_of(n)], in0=xn[:, b, tile_of(j)],
                                                 scalar=H[:, b, NS * n + j:NS * n + j + 1], in1=M.x[:, b, tile_of(n)],
                                                 op0=ALU.mult, op1=ALU.add).then_inc(s.mixed, 1)


def store_stage(nc, M, out):
    with ExitStack() as ctx:
        S = Scope(nc, M, ctx, "store")
        s = Named()
        [s.stored] = S.sems("stored")
        block = S.block()

        @block.sync
        def _(sp):
            sp.dma_start(out.rearrange("b p d -> p b d"), M.x[:]).then_inc(s.stored, 16)
            sp.wait_ge(s.stored, 16)


STAGES = ("attn0", "ffn0", "attn1", "ffn1", "attn2", "ffn2", "attn3", "ffn3")


def program(nc, A, out, stages=STAGES):
    with ExitStack() as ctx:
        M = Named()
        M.used_semaphores = []
        S = Scope(nc, M, ctx, "m")
        M.x = S.sb("x", [P, NB, D])
        M.nT = S.pair("nT", [P, KC, TOK])
        M.ident = S.sb("ident", [P, P])
        ln_w = S.sb("ln_w", [P, KC])
        M.neg_half = S.sb("neg_half", [P, 8])
        M.eps = S.sb("eps", [P, 8])
        psum = ctx.enter_context(nc.psum_tensor("banks", [P, 8, 512], F32))
        M.psum = psum
        M.bank = [psum[:, i, :] for i in range(8)]
        with ExitStack() as front:
            M.cT = Scope(nc, M, front, "c1").pair("cT", [P, KC, TOK])
            load_stage(nc, M, A, "load", x=A["x"])
            if "attn0" in stages:
                norm_stage(nc, M, "n0")
                attn0_stage(nc, M, A)
            if "ffn0" in stages:
                norm_stage(nc, M, "n1", rms_eps=LN_EPS, feature_scale=ln_w, load_scale=A["L0_ffn_ln_w"])
                ffn0_stage(nc, M, A)
                clear_semaphores(nc, M)
            if "attn1" in stages:
                norm_stage(nc, M, "n2")
                attn1_stage(nc, M, A)
            if "ffn1" in stages:
                norm_stage(nc, M, "n3")
                ffn1_stage(nc, M, A)
                clear_semaphores(nc, M)
            if "attn2" in stages:
                norm_stage(nc, M, "n4")
                attn2_stage(nc, M, A)
                clear_semaphores(nc, M)
        if "ffn2" in stages:
            ffn2_stage(nc, M, A)
            clear_semaphores(nc, M)
        if "attn3" in stages:
            with ExitStack() as back:
                M.cT = Scope(nc, M, back, "c2").pair("cT", [P, KC, TOK])
                load_stage(nc, M, A, "load2")
                norm_stage(nc, M, "n6")
                attn3_stage(nc, M, A)
                clear_semaphores(nc, M)
        if "ffn3" in stages:
            xn = S.sb("xn", [P, NB, D])
            rms = S.sb("rms", [P, NB])
            norm_stage(nc, M, "n7", rms_eps=RMS3_EPS, keep_rms=rms, xn=xn)
            ffn3_stage(nc, M, A, xn, rms)
        store_stage(nc, M, out)



def kc_major(w):
    return w.reshape(-1, P, w.shape[1]).transpose(1, 0, 2)


def column_blocks(w, n):
    k, m = w.shape
    return w.reshape(k // P, P, n, m // n).transpose(2, 1, 0, 3)


def row_blocks(w, n):
    k, m = w.shape
    return w.reshape(n, k // n // P, P, m).transpose(0, 2, 1, 3)


def lay_out(I):
    A = {"x": I["x"], "ctxT": I["ctx_4096"].reshape(TOK, D).T, "mask": I["mask_1x1xSxS2_ff0"].reshape(P, P)}
    A["L0_xattn_Wq"] = column_blocks(I["L0_xattn_Wq"].T, 8)
    A["L0_xattn_Wkv"] = np.concatenate([column_blocks(I["L0_xattn_Wk"].T, 8), column_blocks(I["L0_xattn_Wv"].T, 8)], axis=3)
    A["L0_xattn_Wo"] = row_blocks(I["L0_xattn_Wo"].T, 8)
    A["L0_xattn_q_norm_w"] = I["L0_xattn_q_norm_w"].reshape(P, 1)
    A["L0_xattn_k_norm_w"] = I["L0_xattn_k_norm_w"].reshape(P, 1)
    A["L0_ffn_ln_w"] = I["L0_ffn_ln_w"].reshape(KC, P).T
    A["L0_ffn_Wgu"] = np.stack([column_blocks(I["L0_ffn_gate_w"].T, 7), column_blocks(I["L0_ffn_up_w"].T, 7)], axis=3)
    A["L0_ffn_Wd"] = row_blocks(I["L0_ffn_down_w"].T, 7)
    A["L1_xattn_Wv"] = kc_major(I["L1_xattn_Wv"])
    k_repeated = np.repeat(I["L1_xattn_Wk"].reshape(D, 8, 1, 16), 4, axis=2).reshape(D, D)
    A["L1_xattn_Wqk"] = np.stack([column_blocks(I["L1_xattn_Wq"], 4), column_blocks(k_repeated, 4)], axis=3)
    A["L1_xattn_Wo"] = I["L1_xattn_Wo"].reshape(4, P, D)
    A["head_mask"] = (np.arange(P)[:, None] // 16 % 4 == np.arange(4)[None, :]).astype(np.float32)
    A["L1_ffn_mid"] = kc_major(np.concatenate([I["L1_ffn_lora_A"].transpose(1, 0, 2).reshape(D, P),
                                               I["L1_ffn_router_W"].T], axis=1))
    A["L1_ffn_base"] = kc_major(I["L1_ffn_base_W"].T)
    A["L1_ffn_lora_B"] = I["L1_ffn_lora_B"].reshape(P, D)
    A["expert"] = np.repeat(np.arange(-8, 0, dtype=np.float32)[None, :], P, axis=0)
    A["L2_xattn_Wkv"] = np.stack([column_blocks(I["L2_xattn_Wk"], 4), column_blocks(I["L2_xattn_Wv"], 4)], axis=3)
    A["L2_xattn_Wq"] = column_blocks(I["L2_xattn_Wq"], 8)
    A["L2_xattn_Wo"] = row_blocks(I["L2_xattn_Wo"], 8)
    padded = [np.pad(I["L2_ffn_w_gate"], ((0, C2 * P - I2), (0, 0))), np.pad(I["L2_ffn_w_up"], ((0, C2 * P - I2), (0, 0)))]
    A["L2_ffn_gate_up"] = np.stack([w.reshape(C2, P, D) for w in padded], axis=1)
    A["L2_ffn_down"] = np.pad(I["L2_ffn_w_down"], ((0, 0), (0, C2 * P - I2))).reshape(KC, P, C2 * P)
    A["ctx"] = I["ctx_4096"]
    A["L3_xattn_Wqk"] = np.stack([kc_major(I["L3_xattn_Wq"].T), kc_major(I["L3_xattn_Wk"].T)])
    A["L3_xattn_bias"] = np.stack([I["L3_xattn_bq"].reshape(KC, P).T, I["L3_xattn_bk"].reshape(KC, P).T], axis=1)
    A["L3_ffn_W"] = kc_major(np.concatenate([I["L3_ffn_W_res"], I["L3_ffn_W_pre"], I["L3_ffn_W_post"]]).T)
    A["L3_ffn_W_branch"] = I["L3_ffn_W_branch"]
    base = np.concatenate([I["L3_ffn_H_res_base"].reshape(-1), I["L3_ffn_H_pre_base"], I["L3_ffn_H_post_base"]])
    A["L3_ffn_base"] = np.repeat(base[None, :], P, axis=0)
    A["L3_ffn_gate"] = np.repeat(I["L3_ffn_gate"].reshape(1, 1), P, axis=0)
    A["eye"] = np.repeat(np.eye(4, dtype=np.float32).reshape(1, 16), P, axis=0)
    return {k: np.ascontiguousarray(v) for k, v in A.items()}


def kernel(**inputs):
    import concourse.bacc as bacc
    from concourse.bass_utils import run_bass_kernel_spmd

    nc = bacc.Bacc("TRN2", target_bir_lowering=False, num_devices=1)
    arrays = {f"in_{k}": v for k, v in lay_out({k: np.asarray(v) for k, v in inputs.items()}).items()}
    A = {k[3:]: nc.dram_tensor(k, v.shape, mybir.dt.from_np(v.dtype), kind="ExternalInput").ap()
         for k, v in arrays.items()}
    out = nc.dram_tensor("out_0", (NB, P, D), F32, kind="ExternalOutput").ap()
    program(nc, A, out)
    result = run_bass_kernel_spmd(nc, [arrays], core_ids=[0])
    return result.results[0]["out_0"]
```

```python
from contextlib import ExitStack

import numpy as np

import concourse.bass as bass
from concourse import mybir

F32 = mybir.dt.float32
F32R = mybir.dt.float32r
ALU = mybir.AluOpType
ACT = mybir.ActivationFunctionType
AX = mybir.AxisListType

P = 128
NB = 8
TOK = NB * P
D = 512
KC = D // P
HALF = TOK // 2
LN_EPS = 1e-5
RMS3_EPS = 1.1920929e-07
BIG_HEADS = 32
QUAD = 4
ROUND = 1.5 * 2.0 ** 23


def nth(turn, per_turn, n):
    return turn * per_turn + n


def primed(turn, per_turn, n):
    return turn * per_turn + n + 1


def f32(ap):
    return ap.bitcast(F32)


def mm3(pe, out, stationary, moving, first, last):
    (sh, sl), (mh, ml) = stationary, moving
    pe.matmul(out, sh, mh, start=first, stop=False)
    pe.matmul(out, sh, ml, start=False, stop=False)
    return pe.matmul(out, sl, mh, start=False, stop=last)


class Named:
    pass


class Scope:

    def __init__(self, nc, M, ctx, prefix):
        self.nc, self.M, self.ctx, self.prefix = nc, M, ctx, prefix
        self.primed = False

    def sb(self, name, shape, dtype=F32):
        return self.ctx.enter_context(self.nc.sbuf_tensor(f"{self.prefix}_{name}", shape, dtype))

    def pair(self, name, shape):
        return self.sb(name + "_hi", shape, F32R), self.sb(name + "_lo", shape, F32R)

    def sems(self, names, primed=False):
        sems = [self.nc.alloc_semaphore(name=f"{self.prefix}_{n}") for n in names.split()]
        self.M.used_semaphores.extend(sems)
        for sem in sems if primed else []:
            self.nc.gpsimd.sem_inc(sem, 1)
            self.primed = True
        return sems

    def block(self):
        if self.primed:
            self.nc.all_engine_barrier()
        return self.ctx.enter_context(self.nc.Block())


def clear_semaphores(nc, M):
    nc.clear_and_free_semaphores(list(M.used_semaphores))
    M.used_semaphores.clear()
    nc.all_engine_barrier()


def part(pair, *index):
    return pair[0][index], pair[1][index]


def tile_of(b):
    return slice(b * P, (b + 1) * P)



def load_stage(nc, M, x):
    with ExitStack() as ctx:
        S = Scope(nc, M, ctx, "load")
        s = Named()
        s.x_loaded, s.zeroed, s.made = S.sems("x_loaded zeroed made")
        block = S.block()

        @block.sync
        def _(sp):
            sp.dma_start(M.x[:], x.rearrange("b p d -> p b d")).then_inc(s.x_loaded, 16)

        @block.gpsimd
        def _(pool):
            pool.memset(M.ident[:], 0.0).then_inc(s.zeroed, 1)
            pool.memset(M.neg_half[:], -0.5).then_inc(s.zeroed, 1)
            pool.memset(M.eps[:], LN_EPS).then_inc(s.zeroed, 1)
            pool.wait_ge(s.zeroed, 3)
            pool.affine_select(out=M.ident[:], in_=M.ident[:], compare_op=ALU.not_equal, fill=1.0,
                               base=0, pattern=[[-1, P]], channel_multiplier=1).then_inc(s.made, 1)
            pool.wait_ge(s.made, 1)
            pool.wait_ge(s.x_loaded, 16)



def tile_stats(dve, M, b, added, value):
    dve.wait_ge(added, value)
    dve.bn_stats(M.stats[:, b, :], M.x[:, b, :])


def norm_stage(nc, M, name, rms_eps=None, feature_scale=None, load_scale=None, keep_rms=None, xn=None,
               normalize=True, turn=True, prefetch=None, context=None):
    with ExitStack() as ctx:
        S = Scope(nc, M, ctx, name)
        s = Named()
        s.stats, s.aggregated, s.pow_step, s.rstd_ready = S.sems("stats aggregated pow_step rstd_ready")
        s.normed, s.turned, s.hi_made, s.split, s.scale_loaded = S.sems("normed turned hi_made split scale_loaded")
        xn = xn if xn is not None else S.sb("xn", [P, NB, D])
        mv = S.sb("mv", [P, NB, 2])
        shifted = S.sb("shifted", [P, NB])
        rstd = S.sb("rstd", [P, NB])
        sq = S.sb("sq", [P, NB])
        rms = keep_rms if keep_rms is not None else S.sb("rms", [P, NB])
        both = S.sb("both", [P, NB])
        factor = both if rms_eps is not None and keep_rms is None else rstd
        bank = [M.bank[i] for i in range(4)]
        if context is not None:
            raw_ctx = S.sb("raw_ctx", [P, KC, TOK])
            s.ctx_loaded, s.ctx_hi = S.sems("ctx_loaded ctx_hi")
        block = S.block()

        @block.sync
        def _(sp):
            if context is not None:
                sp.dma_start(raw_ctx[:], context.rearrange("(c p) t -> p c t", p=P)).then_inc(s.ctx_loaded, 16)
            if feature_scale is not None:
                sp.dma_start(feature_scale[:], load_scale).then_inc(s.scale_loaded, 16)
            if prefetch is not None:
                prefetch(sp)

        @block.gpsimd
        def _(pool):
            steps = [0]

            def step(ins):
                ins.then_inc(s.pow_step, 1)
                steps[0] += 1
                pool.wait_ge(s.pow_step, steps[0])

            if not normalize:
                return
            pool.wait_ge(s.aggregated, NB)
            step(pool.tensor_scalar(shifted[:], mv[:, :, 1], LN_EPS, None, ALU.add))
            step(pool.tensor_tensor(rstd[:], shifted[:], M.neg_half[:, 0:NB], ALU.pow))
            if rms_eps is not None:
                step(pool.tensor_tensor(sq[:], rstd[:], rstd[:], ALU.mult))
                step(pool.tensor_tensor(sq[:], sq[:], mv[:, :, 1], ALU.mult))
                step(pool.tensor_scalar(sq[:], sq[:], rms_eps, None, ALU.add))
                step(pool.tensor_tensor(rms[:], sq[:], M.neg_half[:, 0:NB], ALU.pow))
            pool.tensor_tensor(both[:], rstd[:], rms[:] if rms_eps is not None else rstd[:],
                               ALU.mult).then_inc(s.rstd_ready, 1)

        @block.vector
        def _(dve):
            if normalize:
                if not M.stats_made:
                    for b in range(NB):
                        dve.bn_stats(M.stats[:, b, :], M.x[:, b, :]).then_inc(s.stats, 1)
                    dve.wait_ge(s.stats, NB)
                    M.stats_made = True
                for b in range(NB):
                    dve.bn_aggr(mv[:, b, :], M.stats[:, b, :]).then_inc(s.aggregated, 1)
                dve.wait_ge(s.aggregated, NB)
                dve.wait_ge(s.rstd_ready, 1)
                for b in range(NB):
                    dve.tensor_scalar(xn[:, b, :], M.x[:, b, :], mv[:, b, 0:1], factor[:, b:b + 1],
                                      ALU.subtract, ALU.mult).then_inc(s.normed, 1)
            if not turn:
                return
            if feature_scale is not None:
                dve.wait_ge(s.scale_loaded, 16)
            for b in range(NB):
                dve.wait_ge(s.hi_made, b + 1)
                if feature_scale is None:
                    dve.tensor_tensor(M.nT[1][:, :, tile_of(b)],
                                      bank[b % 4].rearrange("p (c t) -> p c t", c=KC),
                                      f32(M.nT[0][:, :, tile_of(b)]), ALU.subtract).then_inc(s.split, 1)
                    continue
                for c in range(KC):
                    last = dve.scalar_tensor_tensor(
                        out=M.nT[1][:, c, tile_of(b)], in0=bank[b % 4][:, tile_of(c)],
                        scalar=feature_scale[:, c:c + 1], in1=f32(M.nT[0][:, c, tile_of(b)]),
                        op0=ALU.mult, op1=ALU.subtract)
                last.then_inc(s.split, 1)
            if context is not None:
                for c in range(KC):
                    dve.wait_ge(s.ctx_hi, c + 1)
                    dve.tensor_tensor(M.cT[1][:, c, :], raw_ctx[:, c, :], f32(M.cT[0][:, c, :]), ALU.subtract)

        @block.tensor
        def _(pe):
            if not turn:
                return
            for b in range(NB):
                if normalize:
                    pe.wait_ge(s.normed, b + 1)
                if b >= 4:
                    pe.wait_ge(s.split, b - 3)
                for c in range(KC):
                    last = pe.transpose(bank[b % 4][:, tile_of(c)], xn[:, b, tile_of(c)], M.ident[:])
                last.then_inc(s.turned, 1)

        @block.scalar
        def _(act):
            if not turn:
                return
            if feature_scale is not None:
                act.wait_ge(s.scale_loaded, 16)
            for b in range(NB):
                act.wait_ge(s.turned, b + 1)
                if feature_scale is None:
                    act.activation(M.nT[0][:, :, tile_of(b)],
                                   bank[b % 4].rearrange("p (c t) -> p c t", c=KC),
                                   ACT.Copy).then_inc(s.hi_made, 1)
                    continue
                for c in range(KC):
                    last = act.activation(M.nT[0][:, c, tile_of(b)], bank[b % 4][:, tile_of(c)],
                                          ACT.Copy, scale=feature_scale[:, c:c + 1])
                last.then_inc(s.hi_made, 1)
            if context is not None:
                act.wait_ge(s.ctx_loaded, 16)
                for c in range(KC):
                    act.activation(M.cT[0][:, c, :], raw_ctx[:, c, :], ACT.Copy).then_inc(s.ctx_hi, 1)



def attn0_stage(nc, M, A):
    GROUPS, HD = 8, P
    UNITS = 2 * NB
    ALL = GROUPS * NB
    Q_STEPS, O_STEPS = range(1, 1 + KC), range(3, 3 + QUAD)
    ROOT = 1.0 / float(np.sqrt(HD))
    with ExitStack() as ctx:
        S = Scope(nc, M, ctx, "a0")
        raw_kv = S.sb("raw_kv", [P, KC, 2 * HD])
        raw_q = S.sb("raw_q", [P, KC, QUAD * HD])
        raw_o = S.sb("raw_o", [P, QUAD, D])
        norm_w = S.sb("norm_w", [P, 2])
        mask = S.sb("mask", [P, P])
        s = Named()
        s.kv_loaded, s.q_loaded, s.o_loaded, s.small_loaded = S.sems("kv_loaded q_loaded o_loaded small_loaded")

        def load_q(sp, g):
            sp.dma_start(raw_q[:], A["L0_xattn_Wq"][bass.ds(g, 1)].rearrange("g p c n -> (g p) c n")).then_inc(s.q_loaded, 16)

        def load_o(sp, g):
            sp.dma_start(raw_o[:], A["L0_xattn_Wo"][bass.ds(g, 1)].rearrange("g p c n -> (g p) c n")).then_inc(s.o_loaded, 16)

        def load_kv(sp, g):
            sp.dma_start(raw_kv[:], A["L0_xattn_Wkv"][bass.ds(g, 1)].rearrange("g p c n -> (g p) c n")).then_inc(s.kv_loaded, 16)

        def prefetch(sp):
            load_q(sp, 0)
            load_kv(sp, 0)
            sp.dma_start(norm_w[:, 0:1], A["L0_xattn_q_norm_w"]).then_inc(s.small_loaded, 16)
            sp.dma_start(norm_w[:, 1:2], A["L0_xattn_k_norm_w"]).then_inc(s.small_loaded, 16)
            sp.dma_start(mask[:], A["mask"]).then_inc(s.small_loaded, 16)
            load_o(sp, 0)

        norm_stage(nc, M, "n0", prefetch=prefetch, context=A["ctxT"])
        w_kv = S.pair("w_kv", [P, KC, 2 * HD])
        w_q = S.pair("w_q", [P, 2, KC, QUAD * HD])
        w_o = S.pair("w_o", [P, 2, QUAD, D])
        kq_w = S.sb("kq_w", [P, 1])
        squares = S.sb("squares", [P, P])
        k_meansq = S.sb("k_meansq", [P, 1])
        k_rstd = S.sb("k_rstd", [P, 1])
        q_meansq = S.sb("q_meansq", [P, QUAD])
        q_rstd = S.sb("q_rstd", [P, QUAD])
        k_n = S.sb("k_n", [P, HD])
        q_n = S.sb("q_n", [P, QUAD, HD])
        kT = S.pair("kT", [P, P])
        qT = S.pair("qT", [P, QUAD, P])
        v = S.pair("v", [P, 2, HD])
        probs = S.sb("probs", [P, QUAD, P])
        neg_max = S.sb("neg_max", [P, QUAD])
        sums = S.sb("sums", [P, QUAD])
        inv_sums = S.sb("inv_sums", [P, QUAD])
        pT = S.pair("pT", [P, QUAD * P])
        oT = S.pair("oT", [P, QUAD, P])
        B_Y, B_KV, B_Q, B_QT, B_S, B_PT, B_O, B_KT = M.bank
        s.kq_ready, s.kv_hi, s.q_hi, s.o_hi = S.sems("kq_ready kv_hi q_hi o_hi")
        s.q_turned, s.k_turned, s.scored, s.p_turned, s.pv_made = S.sems("q_turned k_turned scored p_turned pv_made")
        s.k_squared, s.q_squared, s.k_pow, s.q_pow = S.sems("k_squared q_squared k_pow q_pow")
        s.v_hi, s.kT_hi, s.qT_hi, s.max_ready = S.sems("v_hi kT_hi qT_hi max_ready")
        s.exped, s.inverted, s.p_ready, s.pT_hi, s.oT_hi = S.sems("exped inverted p_ready pT_hi oT_hi")
        s.kv_split, s.q_split, s.o_split, s.v_split = S.sems("kv_split q_split o_split v_split", primed=True)
        s.k_normed, s.q_normed, s.kT_split, s.qT_split = S.sems("k_normed q_normed kT_split qT_split", primed=True)
        s.masked, s.pT_split, s.oT_split, s.y_added = S.sems("masked pT_split oT_split y_added", primed=True)
        s.kv_made, s.q_made, s.y_made = S.sems("kv_made q_made y_made", primed=True)
        block = S.block()

        def units_from(i, u):
            return ALL - (UNITS * i + u) if isinstance(i, int) else ALL

        def run(engine, step):
            with engine.Fori(0, GROUPS // 2 - 1) as i:
                for u in range(1, UNITS + 1):
                    step(i, u)
            for u in range(1, UNITS):
                step(GROUPS // 2 - 1, u)

        @block.sync
        def _(sp):
            with sp.Fori(1, GROUPS) as g:
                sp.wait_ge(s.q_split, primed(g, KC, 0))
                load_q(sp, g)
                sp.wait_ge(s.o_split, primed(g, QUAD, 0))
                load_o(sp, g)
                sp.wait_ge(s.kv_split, primed(g, 1, 0))
                load_kv(sp, g)

        @block.tensor
        def _(pe):
            def project_kv(i, u):
                if u % NB == 0:
                    pe.wait_ge(s.kv_split, primed(i, 2, u // NB + 1))
                pe.wait_ge(s.v_split, primed(i, UNITS, u))
                pe.wait_ge(s.k_normed, primed(i, UNITS, u))
                for c in range(KC):
                    last = mm3(pe, B_KV[:, 0:2 * HD], part(M.cT, slice(None), c, tile_of(u % NB)),
                               part(w_kv, slice(None), c), c == 0, c == KC - 1)
                last.then_inc(s.kv_made, 1)

            def project_q(i, u, chunks):
                if 0 in chunks:
                    pe.wait_ge(s.q_normed, primed(i, UNITS, u))
                for c in chunks:
                    if u % NB == 0:
                        pe.wait_ge(s.q_split, primed(i, 2 * KC, u // NB * KC + c + 1))
                    last = mm3(pe, B_Q[:], part(M.nT, slice(None), c, tile_of(u % NB)),
                               part(w_q, slice(None), u // NB % 2, c), c == 0, c == KC - 1)
                if KC - 1 in chunks:
                    last.then_inc(s.q_made, 1)

            def turn_kq(i, u):
                pe.wait_ge(s.q_normed, primed(i, UNITS, u + 1))
                pe.wait_ge(s.qT_split, primed(i, UNITS, u))
                for h in range(QUAD):
                    last = pe.transpose(B_QT[:, tile_of(h)], q_n[:, h, :], M.ident[:])
                last.then_inc(s.q_turned, 1)
                pe.wait_ge(s.k_normed, primed(i, UNITS, u + 1))
                pe.wait_ge(s.kT_split, primed(i, UNITS, u))
                pe.transpose(B_KT[:, 0:P], k_n[:], M.ident[:]).then_inc(s.k_turned, 1)

            def score(i, u):
                pe.wait_ge(s.kT_split, primed(i, UNITS, u + 1))
                pe.wait_ge(s.qT_split, primed(i, UNITS, u + 1))
                pe.wait_ge(s.masked, primed(i, UNITS, u))
                for h in range(QUAD):
                    last = mm3(pe, B_S[:, tile_of(h)], part(qT, slice(None), h), (kT[0][:], kT[1][:]), True, True)
                last.then_inc(s.scored, 1)

            def turn_p(i, u):
                pe.wait_ge(s.p_ready, nth(i, UNITS, u + 1))
                pe.wait_ge(s.pT_split, primed(i, UNITS, u))
                for h in range(QUAD):
                    last = pe.transpose(B_PT[:, tile_of(h)], probs[:, h, :], M.ident[:])
                last.then_inc(s.p_turned, 1)

            def weigh_v(i, u):
                pe.wait_ge(s.v_split, primed(i, UNITS, u + 1))
                pe.wait_ge(s.pT_hi, nth(i, UNITS, u + 1))
                pe.wait_ge(s.oT_split, primed(i, UNITS, u))
                pe.matmul(B_O[:], v[0][:, u % 2], pT[0][:], start=True, stop=False)
                pe.matmul(B_O[:], v[1][:, u % 2], pT[0][:], start=False, stop=False)
                pe.wait_ge(s.pT_split, primed(i, UNITS, u + 1))
                pe.matmul(B_O[:], v[0][:, u % 2], pT[1][:], start=False, stop=True).then_inc(s.pv_made, 1)

            def project_out(i, u):
                if u % NB == 0:
                    pe.wait_ge(s.o_split, primed(i, 2 * QUAD, (u // NB + 1) * QUAD))
                pe.wait_ge(s.oT_split, primed(i, UNITS, u + 1))
                pe.wait_ge(s.y_added, primed(i, UNITS, u))
                for h in range(QUAD):
                    last = mm3(pe, B_Y[:], part(oT, slice(None), h), part(w_o, slice(None), u // NB % 2, h),
                               h == 0, h == QUAD - 1)
                last.then_inc(s.y_made, 1)

            def step(i, u, first=False):
                score(i, u)
                if units_from(i, u) > 1:
                    project_kv(i, u + 1)
                if not first:
                    project_out(i, u - 1)
                if units_from(i, u) > 2:
                    project_q(i, u + 2, (0,))
                turn_p(i, u)
                if units_from(i, u) > 1:
                    turn_kq(i, u + 1)
                if units_from(i, u) > 2:
                    project_q(i, u + 2, (1,))
                weigh_v(i, u)
                if units_from(i, u) > 2:
                    project_q(i, u + 2, (2, 3))

            project_q(0, 0, (0, 1, 2, 3))
            project_kv(0, 0)
            turn_kq(0, 0)
            project_q(0, 1, (0, 1, 2, 3))
            step(0, 0, first=True)
            run(pe, step)
            project_out(GROUPS // 2 - 1, UNITS - 1)

        @block.scalar
        def _(act):
            def hi_q(i, k, c):
                act.wait_ge(s.q_loaded, nth(i, 32, 16 * (k + 1)))
                act.activation(w_q[0][:, k % 2, c], raw_q[:, c], ACT.Copy).then_inc(s.q_hi, 1)

            def hi_o(i, k, h):
                act.wait_ge(s.o_loaded, nth(i, 32, 16 * (k + 1)))
                act.activation(w_o[0][:, k % 2, h], raw_o[:, h], ACT.Copy).then_inc(s.o_hi, 1)

            def hi_kv(i, k):
                act.wait_ge(s.kv_loaded, nth(i, 32, 16 * (k + 1)))
                act.wait_ge(s.kv_made, primed(i, UNITS, NB * k))
                act.activation(w_kv[0][:], raw_kv[:], ACT.Copy).then_inc(s.kv_hi, 1)

            def read_q(i, u):
                act.wait_ge(s.q_made, primed(i, UNITS, u + 1))
                for h in range(QUAD):
                    if h:
                        act.wait_ge(s.q_squared, nth(i, UNITS * QUAD, QUAD * u + h))
                    act.activation(squares[:], B_Q[:, tile_of(h)], ACT.Square, scale=ROOT,
                                   accum_out=q_meansq[:, h:h + 1]).then_inc(s.q_squared, 1)

            def read_kv(i, u):
                act.wait_ge(s.kv_made, primed(i, UNITS, u + 1))
                act.wait_ge(s.q_squared, nth(i, UNITS * QUAD, QUAD * (u + 1)))
                act.activation(squares[:], B_KV[:, 0:HD], ACT.Square, scale=ROOT,
                               accum_out=k_meansq[:]).then_inc(s.k_squared, 1)
                act.activation(v[0][:, u % 2, :], B_KV[:, HD:2 * HD], ACT.Copy).then_inc(s.v_hi, 1)

            def read_turned(i, u):
                act.wait_ge(s.q_turned, nth(i, UNITS, u + 1))
                act.activation(qT[0][:], B_QT.rearrange("p (h t) -> p h t", h=QUAD), ACT.Copy).then_inc(s.qT_hi, 1)
                act.wait_ge(s.k_turned, nth(i, UNITS, u + 1))
                act.activation(kT[0][:], B_KT[:, 0:P], ACT.Copy, scale=kq_w[:]).then_inc(s.kT_hi, 1)

            def step(i, u, first=False):
                act.wait_ge(s.max_ready, nth(i, UNITS, u + 1))
                for h in range(QUAD):
                    act.activation(probs[:, h, :], probs[:, h, :], ACT.Exp, bias=neg_max[:, h:h + 1],
                                   accum_out=sums[:, h:h + 1]).then_inc(s.exped, 1)
                if units_from(i, u) > 1:
                    read_kv(i, u + 1)
                act.wait_ge(s.p_turned, nth(i, UNITS, u + 1))
                act.activation(pT[0][:], B_PT[:], ACT.Copy).then_inc(s.pT_hi, 1)
                if units_from(i, u) > 1:
                    read_turned(i, u + 1)
                act.wait_ge(s.pv_made, nth(i, UNITS, u + 1))
                act.activation(oT[0][:], B_O.rearrange("p (h t) -> p h t", h=QUAD), ACT.Copy).then_inc(s.oT_hi, 1)
                k, t = u // NB + 1, u % NB
                if units_from(i, u) > NB:
                    if t in Q_STEPS:
                        hi_q(i, k, t - Q_STEPS[0])
                    if t in O_STEPS:
                        hi_o(i, k, t - O_STEPS[0])
                    if t == NB - 2:
                        hi_kv(i, k)
                if units_from(i, u) > 2:
                    read_q(i, u + 2)

            for c in range(KC):
                hi_q(0, 0, c)
            hi_kv(0, 0)
            read_q(0, 0)
            read_kv(0, 0)
            for h in range(QUAD):
                hi_o(0, 0, h)
            act.wait_ge(s.kq_ready, 1)
            read_turned(0, 0)
            read_q(0, 1)
            step(0, 0)
            run(act, step)

        @block.gpsimd
        def _(pool):
            def q_factor(i, u):
                pool.wait_ge(s.q_squared, nth(i, UNITS * QUAD, QUAD * (u + 1)))
                pool.tensor_tensor(q_rstd[:], q_meansq[:], M.eps[:, 0:QUAD], ALU.add).then_inc(s.q_pow, 1)
                pool.wait_ge(s.q_pow, nth(i, 2 * UNITS, 2 * u + 1))
                pool.tensor_tensor(q_rstd[:], q_rstd[:], M.neg_half[:, 0:QUAD], ALU.pow).then_inc(s.q_pow, 1)

            def k_factor(i, u):
                pool.wait_ge(s.k_squared, nth(i, UNITS, u + 1))
                pool.tensor_tensor(k_rstd[:], k_meansq[:], M.eps[:, 0:1], ALU.add).then_inc(s.k_pow, 1)
                pool.wait_ge(s.k_pow, nth(i, 2 * UNITS, 2 * u + 1))
                pool.tensor_tensor(k_rstd[:], k_rstd[:], M.neg_half[:, 0:1], ALU.pow).then_inc(s.k_pow, 1)

            def step(i, u):
                if units_from(i, u) > 1:
                    k_factor(i, u + 1)
                if units_from(i, u) > 2:
                    q_factor(i, u + 2)

            q_factor(0, 0)
            k_factor(0, 0)
            q_factor(0, 1)
            step(0, 0)
            run(pool, step)

        @block.vector
        def _(dve):
            def lo_q(i, k, c):
                dve.wait_ge(s.q_hi, nth(i, 2 * KC, KC * k + c + 1))
                dve.tensor_tensor(w_q[1][:, k % 2, c], raw_q[:, c], f32(w_q[0][:, k % 2, c]),
                                  ALU.subtract).then_inc(s.q_split, 1)

            def lo_o(i, k, h):
                dve.wait_ge(s.o_hi, nth(i, 2 * QUAD, QUAD * k + h + 1))
                dve.tensor_tensor(w_o[1][:, k % 2, h], raw_o[:, h], f32(w_o[0][:, k % 2, h]),
                                  ALU.subtract).then_inc(s.o_split, 1)

            def lo_kv(i, k):
                dve.wait_ge(s.kv_hi, nth(i, 2, k + 1))
                dve.tensor_tensor(w_kv[1][:], raw_kv[:], f32(w_kv[0][:]), ALU.subtract).then_inc(s.kv_split, 1)

            def norm_q(i, u):
                dve.wait_ge(s.q_pow, nth(i, 2 * UNITS, 2 * u + 2))
                dve.tensor_tensor(q_n[:], B_Q.rearrange("p (h d) -> p h d", h=QUAD),
                                  q_rstd[:].unsqueeze(2).to_broadcast([P, QUAD, HD]), ALU.mult).then_inc(s.q_normed, 1)

            def read_kv(i, u):
                dve.wait_ge(s.v_hi, nth(i, UNITS, u + 1))
                dve.tensor_tensor(v[1][:, u % 2, :], B_KV[:, HD:2 * HD], f32(v[0][:, u % 2, :]),
                                  ALU.subtract).then_inc(s.v_split, 1)
                dve.wait_ge(s.k_pow, nth(i, 2 * UNITS, 2 * u + 2))
                dve.tensor_scalar(k_n[:], B_KV[:, 0:HD], k_rstd[:], None, ALU.mult).then_inc(s.k_normed, 1)

            def read_turned(i, u):
                dve.wait_ge(s.qT_hi, nth(i, UNITS, u + 1))
                dve.tensor_tensor(qT[1][:], B_QT.rearrange("p (h t) -> p h t", h=QUAD), f32(qT[0][:]),
                                  ALU.subtract).then_inc(s.qT_split, 1)
                dve.wait_ge(s.kT_hi, nth(i, UNITS, u + 1))
                dve.scalar_tensor_tensor(out=kT[1][:], in0=B_KT[:, 0:P], scalar=kq_w[:], in1=f32(kT[0][:]),
                                         op0=ALU.mult, op1=ALU.subtract).then_inc(s.kT_split, 1)

            def add_y(i, u):
                dve.wait_ge(s.y_made, primed(i, UNITS, u + 1))
                x = M.x[:, u % NB, :]
                dve.tensor_tensor(x, x, B_Y[:], ALU.add).then_inc(s.y_added, 1)
                if units_from(i, u) <= NB:
                    tile_stats(dve, M, u % NB, s.y_added, primed(i, UNITS, u + 1))

            def step(i, u, first=False):
                dve.wait_ge(s.scored, nth(i, UNITS, u + 1))
                dve.tensor_tensor(probs[:], B_S.rearrange("p (h k) -> p h k", h=QUAD),
                                  mask[:].unsqueeze(1).to_broadcast([P, QUAD, P]), ALU.add).then_inc(s.masked, 1)
                dve.wait_ge(s.masked, primed(i, UNITS, u + 1))
                dve.tensor_reduce(neg_max[:], probs[:], AX.X, ALU.max, negate=True).then_inc(s.max_ready, 1)
                if units_from(i, u) > 1:
                    norm_q(i, u + 1)
                dve.wait_ge(s.exped, nth(i, UNITS * QUAD, QUAD * (u + 1)))
                dve.reciprocal(inv_sums[:], sums[:]).then_inc(s.inverted, 1)
                dve.wait_ge(s.inverted, nth(i, UNITS, u + 1))
                dve.tensor_tensor(probs[:], probs[:], inv_sums[:].unsqueeze(2).to_broadcast([P, QUAD, P]),
                                  ALU.mult).then_inc(s.p_ready, 1)
                if units_from(i, u) > 1:
                    read_kv(i, u + 1)
                if not first:
                    add_y(i, u - 1)
                dve.wait_ge(s.pT_hi, nth(i, UNITS, u + 1))
                dve.tensor_tensor(pT[1][:], B_PT[:], f32(pT[0][:]), ALU.subtract).then_inc(s.pT_split, 1)
                if units_from(i, u) > 1:
                    read_turned(i, u + 1)
                dve.wait_ge(s.oT_hi, nth(i, UNITS, u + 1))
                dve.tensor_tensor(oT[1][:], B_O.rearrange("p (h t) -> p h t", h=QUAD), f32(oT[0][:]),
                                  ALU.subtract).then_inc(s.oT_split, 1)
                k, t = u // NB + 1, u % NB
                if units_from(i, u) > NB:
                    if t in Q_STEPS:
                        lo_q(i, k, t - Q_STEPS[0])
                    if t in O_STEPS:
                        lo_o(i, k, t - O_STEPS[0])
                    if t == NB - 2:
                        lo_kv(i, k)

            dve.wait_ge(s.small_loaded, 48)
            dve.scalar_tensor_tensor(out=kq_w[:], in0=norm_w[:, 0:1], scalar=ROOT, in1=norm_w[:, 1:2],
                                     op0=ALU.mult, op1=ALU.mult).then_inc(s.kq_ready, 1)
            for c in range(KC):
                lo_q(0, 0, c)
            lo_kv(0, 0)
            norm_q(0, 0)
            read_kv(0, 0)
            for h in range(QUAD):
                lo_o(0, 0, h)
            dve.wait_ge(s.kq_ready, 1)
            read_turned(0, 0)
            step(0, 0, first=True)
            run(dve, step)
            add_y(GROUPS // 2 - 1, UNITS - 1)



def ffn0_stage(nc, M, A, ln_w):
    INNER = 1792
    CH = 2
    TURNS = INNER // (CH * P)
    LAST = TURNS - 1
    UNITS = [(c, h) for h in range(2) for c in range(CH)]
    with ExitStack() as ctx:
        S = Scope(nc, M, ctx, "f0")
        raw_gu = S.sb("raw_gu", [P, KC, 2, CH * P])
        raw_d = S.sb("raw_d", [P, CH, D])
        s = Named()
        s.gu_loaded, s.d_loaded = S.sems("gu_loaded d_loaded")

        def load_gu(sp, i):
            sp.dma_start(raw_gu[:], A["L0_ffn_Wgu"][bass.ds(i, 1)].rearrange("g p c w n -> (g p) c w n")
                         ).then_inc(s.gu_loaded, 16)

        def load_d(sp, i):
            sp.dma_start(raw_d[:], A["L0_ffn_Wd"][bass.ds(i, 1)].rearrange("g p c n -> (g p) c n")).then_inc(s.d_loaded, 16)

        def prefetch(sp):
            load_gu(sp, 0)
            load_d(sp, 0)

        norm_stage(nc, M, "n1", rms_eps=LN_EPS, feature_scale=ln_w, load_scale=A["L0_ffn_ln_w"], prefetch=prefetch)
        w_gu = S.pair("w_gu", [P, KC, 2, CH * P])
        w_d = S.pair("w_d", [P, CH, D])
        hT = S.pair("hT", [P, CH, TOK])
        gated = S.sb("gated", [P, 2, HALF])
        prod = S.sb("prod", [P, 2, HALF])
        s.gu_hi, s.d_hi, s.g_made = S.sems("gu_hi d_hi g_made")
        s.gated, s.h_hi, s.h_split = S.sems("gated h_hi h_split")
        s.gu_split, s.d_split, s.multiplied, s.y_added = S.sems("gu_split d_split multiplied y_added", primed=True)
        s.u_made, s.y_made = S.sems("u_made y_made", primed=True)
        G, U, Y = M.bank[0:2], M.bank[2:4], M.bank[4:8]
        NU = len(UNITS)
        block = S.block()

        def run(engine, turn):
            with engine.Fori(0, LAST) as i:
                turn(i)
            turn(LAST)

        @block.sync
        def _(sp):
            with sp.Fori(1, TURNS) as i:
                sp.wait_ge(s.gu_split, primed(i, 1, 0))
                load_gu(sp, i)
                sp.wait_ge(s.d_split, primed(i, 1, 0))
                load_d(sp, i)

        @block.tensor
        def _(pe):
            with pe.Fori(0, TURNS) as i:
                pe.wait_ge(s.gu_split, primed(i, 1, 1))
                for u, (c, h) in enumerate(UNITS):
                    tokens = slice(h * HALF, (h + 1) * HALF)
                    if u >= 2:
                        pe.wait_ge(s.multiplied, primed(i, NU, u - 1))
                    else:
                        pe.wait_ge(s.multiplied, primed(i, NU, 0))
                    for w, (banks, made) in enumerate(((G, s.g_made), (U, s.u_made))):
                        for k in range(KC):
                            last = mm3(pe, banks[u % 2], part(w_gu, slice(None), k, w, tile_of(c)),
                                       part(M.nT, slice(None), k, tokens), k == 0, k == KC - 1)
                        last.then_inc(made, 1)
                pe.wait_ge(s.d_split, primed(i, 1, 1))
                for t in range(NB):
                    pe.wait_ge(s.h_split, nth(i, NU, CH if t < NB // 2 else NU))
                    pe.wait_ge(s.y_added, primed(i, NB, max(t - 3, 0)))
                    for c in range(CH):
                        last = mm3(pe, Y[t % 4], part(hT, slice(None), c, tile_of(t)), part(w_d, slice(None), c),
                                   c == 0, c == CH - 1)
                    last.then_inc(s.y_made, 1)

        @block.scalar
        def _(act):
            def hi_gu(i, k):
                act.wait_ge(s.gu_loaded, nth(i, 16, 16 * (k + 1)))
                act.wait_ge(s.u_made, primed(i, NU, NU * k))
                act.activation(w_gu[0][:], raw_gu[:], ACT.Copy).then_inc(s.gu_hi, 1)

            def turn(i):
                for u, (c, h) in enumerate(UNITS):
                    tokens = slice(h * HALF, (h + 1) * HALF)
                    act.wait_ge(s.g_made, nth(i, NU, u + 1))
                    act.activation(gated[:, u % 2, :], G[u % 2], ACT.Silu).then_inc(s.gated, 1)
                    if u == 0:
                        act.wait_ge(s.d_loaded, nth(i, 16, 16))
                        act.wait_ge(s.y_made, primed(i, NB, 0))
                        act.activation(w_d[0][:], raw_d[:], ACT.Copy).then_inc(s.d_hi, 1)
                    act.wait_ge(s.multiplied, primed(i, NU, u + 1))
                    act.activation(hT[0][:, c, tokens], prod[:, u % 2, :], ACT.Copy).then_inc(s.h_hi, 1)
                if i is not LAST:
                    hi_gu(i, 1)

            act.preload_act_table_set("silu_and_others")
            hi_gu(0, 0)
            run(act, turn)

        @block.gpsimd
        def _(pool):
            with pool.Fori(0, TURNS) as i:
                pool.wait_ge(s.d_hi, nth(i, 1, 1))
                pool.tensor_tensor(w_d[1][:], raw_d[:], f32(w_d[0][:]), ALU.subtract).then_inc(s.d_split, 1)

        @block.vector
        def _(dve):
            def add_y(i, t):
                dve.wait_ge(s.y_made, primed(i, NB, t + 1))
                dve.tensor_tensor(M.x[:, t, :], M.x[:, t, :], Y[t % 4], ALU.add).then_inc(s.y_added, 1)
                if i is LAST:
                    tile_stats(dve, M, t, s.y_added, primed(i, NB, t + 1))

            def lo_gu(i, k):
                dve.wait_ge(s.gu_hi, nth(i, 1, k + 1))
                dve.tensor_tensor(w_gu[1][:], raw_gu[:], f32(w_gu[0][:]), ALU.subtract).then_inc(s.gu_split, 1)

            def turn(i):
                for u, (c, h) in enumerate(UNITS):
                    tokens = slice(h * HALF, (h + 1) * HALF)
                    dve.wait_ge(s.u_made, primed(i, NU, u + 1))
                    dve.wait_ge(s.gated, nth(i, NU, u + 1))
                    dve.tensor_tensor(prod[:, u % 2, :], gated[:, u % 2, :], U[u % 2], ALU.mult).then_inc(s.multiplied, 1)
                    dve.wait_ge(s.h_hi, nth(i, NU, u + 1))
                    dve.tensor_tensor(hT[1][:, c, tokens], prod[:, u % 2, :], f32(hT[0][:, c, tokens]),
                                      ALU.subtract).then_inc(s.h_split, 1)
                add_y(i, 0)
                add_y(i, 1)
                if i is not LAST:
                    lo_gu(i, 1)
                for t in range(2, NB):
                    add_y(i, t)

            lo_gu(0, 0)
            run(dve, turn)



def attn1_stage(nc, M, A):
    HD = 16
    CHUNKS = D // P
    LAST = CHUNKS - 1
    HEADS = P // HD
    SCALE = HD ** -0.5
    with ExitStack() as ctx:
        S = Scope(nc, M, ctx, "a1")
        raw_v = S.sb("raw_v", [P, KC, P])
        raw_qk = S.sb("raw_qk", [P, KC, 2, P])
        raw_o = S.sb("raw_o", [P, D])
        head_mask = S.sb("head_mask", [P, QUAD])
        s = Named()
        s.v_loaded, s.mask_loaded, s.qk_loaded, s.o_loaded = S.sems("v_loaded mask_loaded qk_loaded o_loaded")

        def load_qk(sp, c):
            sp.dma_start(raw_qk[:], A["L1_xattn_Wqk"][bass.ds(c, 1)].rearrange("g p c w n -> (g p) c w n")
                         ).then_inc(s.qk_loaded, 16)

        def load_o(sp, c):
            sp.dma_start(raw_o[:], A["L1_xattn_Wo"][bass.ds(c, 1)].rearrange("g p n -> (g p) n")).then_inc(s.o_loaded, 16)

        def prefetch(sp):
            sp.dma_start(raw_v[:], A["L1_xattn_Wv"]).then_inc(s.v_loaded, 16)
            load_qk(sp, 0)
            sp.dma_start(head_mask[:], A["head_mask"]).then_inc(s.mask_loaded, 16)
            load_o(sp, 0)

        norm_stage(nc, M, "n2", prefetch=prefetch)
        w_v = S.pair("w_v", [P, KC, P])
        w_qk = S.pair("w_qk", [P, KC, 2, P])
        w_o = S.pair("w_o", [P, D])
        v = S.sb("v", [P, NB, P // HD, 2, HD], F32R)
        qT = S.pair("qT", [P, TOK])
        kM = S.pair("kM", [P, QUAD, TOK])
        k_raw = S.sb("k_raw", [P, HALF])
        probs = S.sb("probs", [P, 2, HEADS, P])
        neg_max = S.sb("neg_max", [P, 2, HEADS])
        sums = S.sb("sums", [P, 2, HEADS])
        inv_sums = S.sb("inv_sums", [P, HEADS])
        pT = S.pair("pT", [P, HEADS, P])
        o_sum = S.sb("o_sum", [P, HEADS, HD])
        o_n = S.sb("o_n", [P, P])
        oT = S.pair("oT", [P, P])
        s.v_hi, s.w_split, s.wk_hi, s.wq_hi, s.o_hi, s.v_made = S.sems("v_hi w_split wk_hi wq_hi o_hi v_made")
        s.v_val_hi, s.v_split, s.q_hi, s.k_hi, s.scored = S.sems("v_val_hi v_split q_hi k_hi scored")
        s.max_ready, s.p_turned, s.pT_hi, s.o_made = S.sems("max_ready p_turned pT_hi o_made")
        s.inverted, s.summed, s.o_normed, s.o_turned, s.oT_hi = S.sems("inverted summed o_normed o_turned oT_hi")
        s.wk_split, s.wq_split, s.o_split, s.exped = S.sems("wk_split wq_split o_split exped", primed=True)
        s.pT_split, s.oT_split, s.q_made, s.k_made = S.sems("pT_split oT_split q_made k_made", primed=True)
        s.q_split, s.k_split, s.y_made, s.y_added = S.sems("q_split k_split y_made y_added", primed=True)
        [s.k_copied] = S.sems("k_copied", primed=True)
        K_BANK, Q_BANK = M.bank[2], M.bank[3]
        PT, O, Y = M.psum[:, 4:6, :], M.bank[6], M.bank[7]
        scores = M.psum[:, 0:2, :].rearrange("p j (h k) -> p j h k", k=P)
        O_TURNED = O[:, 2 * P:3 * P]
        o_parts = O[:, 0:2 * P].rearrange("p (h w d) -> p h w d", w=2, d=HD)
        v_flat = v[:].rearrange("p b h w d -> p b (h w d)")
        block = S.block()

        def run(engine, step):
            with engine.Fori(0, LAST) as c:
                for b in range(1, NB + 1):
                    step(c, b)
            for b in range(1, NB):
                step(LAST, b)

        def steps_on(c, b):
            return b < NB - 1 or c is not LAST

        def piece_of(c, b):
            t, k = b % NB, b // NB
            if t in (1, 2):
                return 0, 2 * k + 1, t - 1
            if t == 0:
                return 1, 2 * k + 1, 1
            if c is LAST:
                return None
            return {3: (1, 2 * k + 2, 0), 4: (1, 2 * k + 2, 1), 5: (0, 2 * k + 2, 0), 6: (0, 2 * k + 2, 1),
                    7: (1, 2 * k + 3, 0)}[t]

        def k_masks_of(c, b):
            t, k = b % NB, b // NB
            if t in (0, 1):
                return 2 * k + 1, ((0, 1), (2, 3))[t]
            if t in (4, 5) and c is not LAST:
                return 2 * k + 2, ((0, 1), (2, 3))[t - 4]
            return None, ()

        @block.sync
        def _(sp):
            with sp.Fori(1, CHUNKS) as c:
                sp.wait_ge(s.wk_split, primed(c, 1, 0))
                sp.wait_ge(s.wq_split, primed(c, 1, 0))
                load_qk(sp, c)
                sp.wait_ge(s.o_split, primed(c, 1, 0))
                load_o(sp, c)

        @block.tensor
        def _(pe):
            def project(c, w, piece, halves):
                made, read, weights = ((s.q_made, s.q_split, s.wq_split), (s.k_made, s.k_copied, s.wk_split))[w]
                tokens = slice(piece % 2 * HALF, (piece % 2 + 1) * HALF)
                if 0 in halves:
                    pe.wait_ge(weights, primed(c, 1, piece // 2 + 1))
                    pe.wait_ge(read, primed(c, 2, piece))
                for half in halves:
                    for k in (2 * half, 2 * half + 1):
                        last = mm3(pe, (Q_BANK, K_BANK)[w], part(w_qk, slice(None), k, w),
                                   part((M.nT, M.cT)[w], slice(None), k, tokens), k == 0, k == KC - 1)
                if 1 in halves:
                    last.then_inc(made, 1)

            def score(c, b):
                if b % 4 == 0:
                    piece = b // 4
                    pe.wait_ge(s.q_split, primed(c, 2, piece + 1))
                    pe.wait_ge(s.k_split, primed(c, 2 * QUAD, QUAD * (piece + 1)))
                for j in range(2):
                    pe.wait_ge(s.exped, primed(c, NB * HEADS, HEADS * (b - 1) + QUAD * (j + 1) if b else 0))
                    rows = slice(64 * j, 64 * j + 64)
                    mm3(pe, M.bank[j], part(qT, rows, tile_of(b % NB)),
                        part(kM, rows, slice(None), tile_of(b % NB)), True, True).then_inc(s.scored, 1)

            def turn_p(c, b):
                for j in range(2):
                    pe.wait_ge(s.exped, primed(c, NB * HEADS, HEADS * b + QUAD * (j + 1)))
                    pe.wait_ge(s.pT_split, primed(c, 2 * NB, 2 * (b - 1) + j + 1 if b else 0))
                    for h in range(QUAD):
                        last = pe.transpose(PT[:, j, tile_of(h)], probs[:, b % 2, QUAD * j + h, :], M.ident[:])
                    last.then_inc(s.p_turned, 1)

            def weigh_v(c, b):
                pe.wait_ge(s.oT_split, primed(c, NB, b))
                for h in range(HEADS):
                    if h % QUAD == 0:
                        pe.wait_ge(s.pT_split, primed(c, 2 * NB, 2 * b + h // QUAD + 1))
                    first = (c + b // NB) * (4 * HD) + (h // QUAD) * (2 * HD)
                    pe.matmul(O[:, 2 * h * HD:2 * (h + 1) * HD], pT[0][:, h], v_flat[:, b % NB, bass.ds(first, 2 * HD)],
                              start=True, stop=False)
                    last = pe.matmul(O[:, 2 * h * HD:(2 * h + 1) * HD], pT[1][:, h], v_flat[:, b % NB, bass.ds(first, HD)],
                                     start=False, stop=True)
                last.then_inc(s.o_made, 1)

            def turn_o(c, b):
                pe.wait_ge(s.o_normed, nth(c, NB, b + 1))
                pe.transpose(O_TURNED, o_n[:], M.ident[:]).then_inc(s.o_turned, 1)

            def project_out(c, b):
                pe.wait_ge(s.oT_split, primed(c, NB, b + 1))
                pe.wait_ge(s.y_added, primed(c, NB, b))
                if b % NB == 0:
                    pe.wait_ge(s.o_split, primed(c, 1, b // NB + 1))
                mm3(pe, Y, (oT[0][:], oT[1][:]), (w_o[0][:], w_o[1][:]), True, True).then_inc(s.y_made, 1)

            def step(c, b, first=False):
                if steps_on(c, b):
                    score(c, b + 1)
                if not first:
                    turn_o(c, b - 1)
                turn_p(c, b)
                if not first and piece_of(c, b):
                    w, piece, half = piece_of(c, b)
                    project(c, w, piece, (half,))
                if not first:
                    project_out(c, b - 1)
                weigh_v(c, b)

            pe.wait_ge(s.w_split, 1)
            for b in range(NB):
                for k in range(KC):
                    last = mm3(pe, PT[:, b // 4, tile_of(b % 4)], part(M.cT, slice(None), k, tile_of(b)),
                               part(w_v, slice(None), k), k == 0, k == KC - 1)
                last.then_inc(s.v_made, 1)
            project(0, 1, 0, (0, 1))
            project(0, 0, 0, (0, 1))
            project(0, 1, 1, (0, 1))
            score(0, 0)
            pe.wait_ge(s.v_split, 2)
            step(0, 0, first=True)
            run(pe, step)
            turn_o(LAST, NB - 1)
            project_out(LAST, NB - 1)

        @block.scalar
        def _(act):
            def hi_w(c, w, chunk):
                act.wait_ge(s.qk_loaded, nth(c, 16, 16 * (chunk + 1)))
                act.wait_ge((s.q_made, s.k_made)[w], primed(c, 2, 2 * chunk))
                act.activation(w_qk[0][:, :, w], raw_qk[:, :, w], ACT.Copy).then_inc((s.wq_hi, s.wk_hi)[w], 1)

            def hi_o(c, chunk):
                act.wait_ge(s.o_loaded, nth(c, 16, 16 * (chunk + 1)))
                act.wait_ge(s.y_made, primed(c, NB, NB * chunk))
                act.activation(w_o[0][:], raw_o[:], ACT.Copy).then_inc(s.o_hi, 1)

            def hi_q(c, piece):
                tokens = slice(piece % 2 * HALF, (piece % 2 + 1) * HALF)
                act.wait_ge(s.q_made, primed(c, 2, piece + 1))
                act.activation(qT[0][:, tokens], Q_BANK, ACT.Copy, scale=SCALE).then_inc(s.q_hi, 1)

            def hi_k(c, piece, copies):
                if 0 in copies:
                    act.wait_ge(s.k_made, primed(c, 2, piece + 1))
                    act.wait_ge(s.k_split, primed(c, 2 * QUAD, QUAD * piece))
                    act.activation(k_raw[:], K_BANK, ACT.Copy).then_inc(s.k_copied, 1)
                    act.wait_ge(s.k_copied, primed(c, 2, piece + 1))
                for j in copies:
                    act.activation(kM[0][:, j, piece % 2 * HALF:(piece % 2 + 1) * HALF], k_raw[:], ACT.Copy,
                                   scale=head_mask[:, j:j + 1]).then_inc(s.k_hi, 1)

            def exps(c, b, j):
                act.wait_ge(s.max_ready, nth(c, 2 * NB, 2 * b + j + 1))
                for h in range(QUAD):
                    n = QUAD * j + h
                    act.activation(probs[:, b % 2, n, :], scores[:, j, h, :], ACT.Exp, bias=neg_max[:, b % 2, n:n + 1],
                                   accum_out=sums[:, b % 2, n:n + 1]).then_inc(s.exped, 1)

            def hi_oT(c, b):
                act.wait_ge(s.o_turned, nth(c, NB, b + 1))
                act.activation(oT[0][:], O_TURNED, ACT.Copy).then_inc(s.oT_hi, 1)

            def step(c, b, first=False):
                t = b % NB
                if not first:
                    hi_oT(c, b - 1)
                if steps_on(c, b):
                    exps(c, b + 1, 0)
                for j in range(2):
                    act.wait_ge(s.p_turned, nth(c, 2 * NB, 2 * b + j + 1))
                    act.activation(pT[0][:, QUAD * j:QUAD * (j + 1)], PT[:, j].rearrange("p (h q) -> p h q", q=P),
                                   ACT.Copy).then_inc(s.pT_hi, 1)
                if not first and (t == 2 or t == 6 and c is not LAST):
                    hi_q(c, piece_of(c, b)[1])
                hi_k(c, *k_masks_of(c, b))
                if steps_on(c, b):
                    exps(c, b + 1, 1)
                if t == 0:
                    hi_o(c, b // NB)
                if t in (1, 3) and c is not LAST:
                    hi_w(c, {1: 1, 3: 0}[t], b // NB + 1)

            act.wait_ge(s.v_loaded, 16)
            act.activation(w_v[0][:], raw_v[:], ACT.Copy).then_inc(s.v_hi, 1)
            hi_w(0, 1, 0)
            hi_w(0, 0, 0)
            for half in range(2):
                act.wait_ge(s.v_made, NB // 2 * (half + 1))
                act.activation(v[:, 4 * half:4 * half + 4, :, 0, :],
                               PT[:, half, :].rearrange("p (b h d) -> p b h d", b=4, d=HD), ACT.Copy).then_inc(s.v_val_hi, 1)
            act.wait_ge(s.mask_loaded, 16)
            hi_k(0, 0, range(QUAD))
            hi_q(0, 0)
            exps(0, 0, 0)
            exps(0, 0, 1)
            step(0, 0, first=True)
            run(act, step)
            hi_oT(LAST, NB - 1)

        @block.gpsimd
        def _(pool):
            def lo_w(c, w, chunk):
                pool.wait_ge((s.wq_hi, s.wk_hi)[w], nth(c, 1, chunk + 1))
                pool.tensor_tensor(w_qk[1][:, :, w], raw_qk[:, :, w], f32(w_qk[0][:, :, w]),
                                   ALU.subtract).then_inc((s.wq_split, s.wk_split)[w], 1)

            def step(c, b):
                t = b % NB
                if t == 0:
                    pool.wait_ge(s.o_hi, nth(c, 1, b // NB + 1))
                    pool.tensor_tensor(w_o[1][:], raw_o[:], f32(w_o[0][:]), ALU.subtract).then_inc(s.o_split, 1)
                if t in (1, 3) and c is not LAST:
                    lo_w(c, {1: 1, 3: 0}[t], b // NB + 1)

            lo_w(0, 1, 0)
            lo_w(0, 0, 0)
            step(0, 0)
            run(pool, step)

        @block.vector
        def _(dve):
            def lo_q(c, piece):
                tokens = slice(piece % 2 * HALF, (piece % 2 + 1) * HALF)
                dve.wait_ge(s.q_hi, nth(c, 2, piece + 1))
                dve.scalar_tensor_tensor(out=qT[1][:, tokens], in0=Q_BANK, scalar=SCALE, in1=f32(qT[0][:, tokens]),
                                         op0=ALU.mult, op1=ALU.subtract).then_inc(s.q_split, 1)

            def lo_k(c, piece, copies):
                for j in copies:
                    at = slice(piece % 2 * HALF, (piece % 2 + 1) * HALF)
                    dve.wait_ge(s.k_hi, nth(c, 2 * QUAD, QUAD * piece + j + 1))
                    dve.scalar_tensor_tensor(out=kM[1][:, j, at], in0=k_raw[:], scalar=head_mask[:, j:j + 1],
                                             in1=f32(kM[0][:, j, at]), op0=ALU.mult, op1=ALU.subtract).then_inc(s.k_split, 1)

            def row_max(c, b, j):
                dve.wait_ge(s.scored, nth(c, 2 * NB, 2 * b + j + 1))
                dve.tensor_reduce(neg_max[:, b % 2, QUAD * j:QUAD * (j + 1)], scores[:, j], AX.X, ALU.max,
                                  negate=True).then_inc(s.max_ready, 1)

            def lo_oT(c, b):
                dve.wait_ge(s.oT_hi, nth(c, NB, b + 1))
                dve.tensor_tensor(oT[1][:], O_TURNED, f32(oT[0][:]), ALU.subtract).then_inc(s.oT_split, 1)

            def add_y(c, b):
                x = M.x[:, b % NB, :]
                dve.wait_ge(s.y_made, primed(c, NB, b + 1))
                dve.tensor_tensor(x, x, Y, ALU.add).then_inc(s.y_added, 1)
                if c is LAST:
                    tile_stats(dve, M, b, s.y_added, primed(c, NB, b + 1))

            def step(c, b, first=False):
                t = b % NB
                if steps_on(c, b):
                    row_max(c, b + 1, 0)
                    row_max(c, b + 1, 1)
                if not first:
                    lo_oT(c, b - 1)
                for j in range(2):
                    dve.wait_ge(s.pT_hi, nth(c, 2 * NB, 2 * b + j + 1))
                    dve.tensor_tensor(pT[1][:, QUAD * j:QUAD * (j + 1)], PT[:, j].rearrange("p (h q) -> p h q", q=P),
                                      f32(pT[0][:, QUAD * j:QUAD * (j + 1)]), ALU.subtract).then_inc(s.pT_split, 1)
                if not first and (t == 2 or t == 6 and c is not LAST):
                    lo_q(c, piece_of(c, b)[1])
                if not first:
                    add_y(c, b - 1)
                dve.reciprocal(inv_sums[:], sums[:, b % 2, :]).then_inc(s.inverted, 1)
                lo_k(c, *k_masks_of(c, b))
                dve.wait_ge(s.o_made, nth(c, NB, b + 1))
                dve.tensor_copy(o_sum[:], o_parts[:, :, 1, :]).then_inc(s.summed, 1)
                dve.wait_ge(s.summed, nth(c, 2 * NB, 2 * b + 1))
                dve.tensor_tensor(o_sum[:], o_parts[:, :, 0, :], o_sum[:], ALU.add).then_inc(s.summed, 1)
                dve.wait_ge(s.inverted, nth(c, NB, b + 1))
                dve.wait_ge(s.summed, nth(c, 2 * NB, 2 * b + 2))
                dve.tensor_tensor(o_n[:].rearrange("p (h d) -> p h d", d=HD), o_sum[:],
                                  inv_sums[:].unsqueeze(2).to_broadcast([P, HEADS, HD]), ALU.mult).then_inc(s.o_normed, 1)

            dve.wait_ge(s.v_hi, 1)
            dve.tensor_tensor(w_v[1][:], raw_v[:], f32(w_v[0][:]), ALU.subtract).then_inc(s.w_split, 1)
            for half in range(2):
                dve.wait_ge(s.v_val_hi, half + 1)
                tiles = slice(4 * half, 4 * half + 4)
                dve.tensor_tensor(v[:, tiles, :, 1, :], PT[:, half, :].rearrange("p (b h d) -> p b h d", b=4, d=HD),
                                  f32(v[:, tiles, :, 0, :]), ALU.subtract).then_inc(s.v_split, 1)
            dve.wait_ge(s.mask_loaded, 16)
            lo_k(0, 0, range(QUAD))
            lo_q(0, 0)
            row_max(0, 0, 0)
            row_max(0, 0, 1)
            step(0, 0, first=True)
            run(dve, step)
            lo_oT(LAST, NB - 1)
            add_y(LAST, NB - 1)



def ffn1_stage(nc, M, A):
    E, R = 8, 16
    SCALING = 2.0
    MID = E * R
    with ExitStack() as ctx:
        S = Scope(nc, M, ctx, "f1")
        raw_mid = S.sb("raw_mid", [P, KC, MID + E])
        raw_base = S.sb("raw_base", [P, KC, D])
        raw_b = S.sb("raw_b", [P, D])
        expert = S.sb("expert", [P, E])
        s = Named()
        s.mid_loaded, s.base_loaded, s.b_loaded = S.sems("mid_loaded base_loaded b_loaded")
        [s.expert_loaded] = S.sems("expert_loaded")

        def prefetch(sp):
            sp.dma_start(raw_mid[:], A["L1_ffn_mid"]).then_inc(s.mid_loaded, 16)
            sp.dma_start(raw_base[:], A["L1_ffn_base"]).then_inc(s.base_loaded, 16)
            sp.dma_start(raw_b[:], A["L1_ffn_lora_B"]).then_inc(s.b_loaded, 16)
            sp.dma_start(expert[:], A["expert"]).then_inc(s.expert_loaded, 16)

        norm_stage(nc, M, "n3", prefetch=prefetch)
        w_mid = S.pair("w_mid", [P, KC, MID + E])
        w_base = S.pair("w_base", [P, KC, D])
        w_b = S.pair("w_b", [P, D])
        mid = S.sb("mid", [P, NB, MID + E])
        logits = mid[:, :, MID:MID + E]
        best = S.sb("best", [P, NB])
        second = S.sb("second", [P, NB])
        at_best = S.sb("at_best", [P, NB])
        hit = S.sb("hit", [P, NB, E])
        is_best = S.sb("is_best", [P, NB, E])
        is_second = S.sb("is_second", [P, NB, E])
        rest = S.sb("rest", [P, NB, E])
        weight = S.sb("weight", [P, NB, E])
        mid_w = S.sb("mid_w", [P, NB, MID])
        mT = S.pair("mT", [P, 2, P])
        s.mid_hi, s.base_hi, s.b_hi = S.sems("mid_hi base_hi b_hi")
        s.mid_split, s.base_split, s.b_split, s.mid_made = S.sems("mid_split base_split b_split mid_made")
        s.mid_copied, s.routed, s.less_max, s.exped = S.sems("mid_copied routed less_max exped")
        s.mid_weighted, s.turned, s.mT_hi, s.mT_split, s.y_made = S.sems("mid_weighted turned mT_hi mT_split y_made")
        [s.y_added] = S.sems("y_added")
        block = S.block()
        Y = M.bank[4:8] + M.bank[0:2]

        def along_experts(ap):
            return ap.unsqueeze(2).to_broadcast([P, NB, E])

        @block.tensor
        def _(pe):
            pe.wait_ge(s.mid_split, 1)
            for b in range(NB):
                if b >= 2:
                    pe.wait_ge(s.mid_copied, b - 1)
                for k in range(KC):
                    last = mm3(pe, M.bank[b % 2][:, 0:MID + E], part(M.nT, slice(None), k, tile_of(b)),
                               part(w_mid, slice(None), k), k == 0, k == KC - 1)
                last.then_inc(s.mid_made, 1)
            pe.wait_ge(s.base_split, 1)

            def base(b):
                if b == 4:
                    pe.wait_ge(s.mid_copied, NB)
                if b >= len(Y):
                    pe.wait_ge(s.y_added, b - len(Y) + 1)
                for k in range(KC):
                    mm3(pe, Y[b % len(Y)], part(M.nT, slice(None), k, tile_of(b)), part(w_base, slice(None), k),
                        k == 0, False)

            def turn(b):
                pe.wait_ge(s.mid_weighted, b + 1)
                if b >= 2:
                    pe.wait_ge(s.mT_split, b - 1)
                pe.transpose(M.bank[2 + b % 2][:, 0:P], mid_w[:, b, :], M.ident[:]).then_inc(s.turned, 1)

            for b in range(4):
                base(b)
            pe.wait_ge(s.b_split, 1)
            turn(0)
            for b in range(NB):
                if b + 4 < NB:
                    base(b + 4)
                if b + 1 < NB:
                    turn(b + 1)
                pe.wait_ge(s.mT_split, b + 1)
                mm3(pe, Y[b % len(Y)], part(mT, slice(None), b % 2), (w_b[0][:], w_b[1][:]), False, True).then_inc(s.y_made, 1)

        @block.scalar
        def _(act):
            act.wait_ge(s.mid_loaded, 16)
            act.activation(w_mid[0][:], raw_mid[:], ACT.Copy).then_inc(s.mid_hi, 1)
            act.wait_ge(s.base_loaded, 16)
            act.activation(w_base[0][:], raw_base[:], ACT.Copy).then_inc(s.base_hi, 1)
            act.wait_ge(s.b_loaded, 16)
            act.activation(w_b[0][:], raw_b[:], ACT.Copy).then_inc(s.b_hi, 1)
            for b in range(NB):
                act.wait_ge(s.mid_made, b + 1)
                act.activation(mid[:, b, :], M.bank[b % 2][:, 0:MID + E], ACT.Copy).then_inc(s.mid_copied, 1)
            act.wait_ge(s.less_max, 1)
            act.activation(weight[:], weight[:], ACT.Exp).then_inc(s.exped, 1)
            for b in range(NB):
                act.wait_ge(s.turned, b + 1)
                act.activation(mT[0][:, b % 2, :], M.bank[2 + b % 2][:, 0:P], ACT.Copy).then_inc(s.mT_hi, 1)

        @block.vector
        def _(dve):
            steps = [0]

            def step(ins):
                ins.then_inc(s.routed, 1)
                steps[0] += 1
                dve.wait_ge(s.routed, steps[0])

            for w, raw, hi, split in ((w_mid, raw_mid, s.mid_hi, s.mid_split), (w_base, raw_base, s.base_hi, s.base_split),
                                      (w_b, raw_b, s.b_hi, s.b_split)):
                dve.wait_ge(hi, 1)
                dve.tensor_tensor(w[1][:], raw[:], f32(w[0][:]), ALU.subtract).then_inc(split, 1)
            dve.wait_ge(s.expert_loaded, 16)
            dve.wait_ge(s.mid_copied, NB)
            numbers = expert[:].unsqueeze(1).to_broadcast([P, NB, E])
            step(dve.tensor_reduce(best[:], logits, AX.X, ALU.max))
            dve.tensor_tensor(weight[:], logits, along_experts(best[:]), ALU.subtract).then_inc(s.less_max, 1)

            def first_at(value, source, out):
                step(dve.tensor_tensor(hit[:], source, along_experts(value), ALU.is_equal))
                step(dve.tensor_tensor(hit[:], hit[:], numbers, ALU.mult))
                step(dve.tensor_reduce(at_best[:], hit[:], AX.X, ALU.min))
                step(dve.tensor_tensor(out, numbers, along_experts(at_best[:]), ALU.is_equal))

            first_at(best[:], logits, is_best[:])
            step(dve.scalar_tensor_tensor(out=rest[:], in0=is_best[:], scalar=-3.0e38, in1=logits,
                                          op0=ALU.mult, op1=ALU.add))
            step(dve.tensor_reduce(second[:], rest[:], AX.X, ALU.max))
            first_at(second[:], rest[:], is_second[:])
            step(dve.tensor_tensor(is_best[:], is_best[:], is_second[:], ALU.add))
            dve.wait_ge(s.exped, 1)
            step(dve.tensor_tensor(weight[:], weight[:], is_best[:], ALU.mult))
            step(dve.tensor_reduce(best[:], weight[:], AX.X, ALU.add))
            step(dve.reciprocal(second[:], best[:]))
            step(dve.scalar_tensor_tensor(out=weight[:], in0=weight[:], scalar=SCALING, in1=along_experts(second[:]),
                                          op0=ALU.mult, op1=ALU.mult))
            for b in range(NB):
                dve.tensor_tensor(mid_w[:, b, :].rearrange("p (e r) -> p e r", e=E),
                                  mid[:, b, 0:MID].rearrange("p (e r) -> p e r", e=E),
                                  weight[:, b, :].unsqueeze(2).to_broadcast([P, E, R]), ALU.mult).then_inc(s.mid_weighted, 1)
            def lo(b):
                dve.wait_ge(s.mT_hi, b + 1)
                dve.tensor_tensor(mT[1][:, b % 2, :], M.bank[2 + b % 2][:, 0:P], f32(mT[0][:, b % 2, :]),
                                  ALU.subtract).then_inc(s.mT_split, 1)

            lo(0)
            for b in range(NB):
                if b + 1 < NB:
                    lo(b + 1)
                dve.wait_ge(s.y_made, b + 1)
                dve.tensor_tensor(M.x[:, b, :], M.x[:, b, :], Y[b % len(Y)], ALU.add).then_inc(s.y_added, 1)
                tile_stats(dve, M, b, s.y_added, b + 1)



def attn2_stage(nc, M, A):
    HD = P
    GROUPS = 4
    LAST = GROUPS - 1
    KEYS = 2 * P
    PAIR = 2 * P
    N = 2 * NB
    NQ = 2 * N
    AHEAD = 6
    SCALE = 1.0 / float(np.sqrt(HD))
    with ExitStack() as ctx:
        S = Scope(nc, M, ctx, "a2")
        raw_kv = S.sb("raw_kv", [P, KC, 2, HD])
        raw_q = S.sb("raw_q", [P, KC, QUAD * HD])
        raw_o = S.sb("raw_o", [P, QUAD, D])
        s = Named()
        s.kv_loaded, s.q_loaded, s.o_loaded = S.sems("kv_loaded q_loaded o_loaded")

        def load_kv(sp, g):
            sp.dma_start(raw_kv[:], A["L2_xattn_Wkv"][bass.ds(g, 1)].rearrange("g p c w n -> (g p) c w n")
                         ).then_inc(s.kv_loaded, 16)

        def load_q(sp, quad):
            sp.dma_start(raw_q[:], A["L2_xattn_Wq"][bass.ds(quad, 1)].rearrange("g p c n -> (g p) c n")
                         ).then_inc(s.q_loaded, 16)

        def load_o(sp, quad):
            sp.dma_start(raw_o[:], A["L2_xattn_Wo"][bass.ds(quad, 1)].rearrange("g p c n -> (g p) c n")
                         ).then_inc(s.o_loaded, 16)

        def prefetch(sp):
            load_q(sp, 0)
            load_kv(sp, 0)
            load_o(sp, 0)

        norm_stage(nc, M, "n4", prefetch=prefetch)
        w_kv = S.pair("w_kv", [P, KC, 2, HD])
        w_q = S.pair("w_q", [P, KC, QUAD * HD])
        w_o = S.pair("w_o", [P, QUAD, D])
        kT = S.pair("kT", [P, NB, 2, P])
        v = S.pair("v", [P, NB, 2, HD])
        qT = S.pair("qT", [P, 2, QUAD, PAIR])
        probs = S.sb("probs", [P, QUAD, KEYS])
        neg_max = S.sb("neg_max", [P, QUAD])
        sums = S.sb("sums", [P, QUAD])
        inv_sums = S.sb("inv_sums", [P, QUAD])
        pT = S.pair("pT", [P, 2, QUAD * P])
        vT = raw_kv[:].rearrange("p c w n -> p (c w n)").rearrange("p (j n) -> p j n", j=2)
        oT = S.pair("oT", [P, QUAD * P])
        s.kv_hi, s.wq_hi = S.sems("kv_hi wq_hi")
        s.wo_hi, s.kvp_hi, s.q_hi, s.scored, s.max_ready = S.sems("wo_hi kvp_hi q_hi scored max_ready")
        s.inverted, s.p_ready, s.p_turned, s.pT_hi, s.o_made = S.sems("inverted p_ready p_turned pT_hi o_made")
        s.oT_hi, s.vT_copied, s.v_turned = S.sems("oT_hi vT_copied v_turned")
        s.kv_split, s.wq_split, s.wo_split, s.q_split = S.sems("kv_split wq_split wo_split q_split", primed=True)
        s.exped, s.pT_split, s.oT_split, s.y_added = S.sems("exped pT_split oT_split y_added", primed=True)
        s.kvp_split, s.q_made, s.y_made, s.kvp_made = S.sems("kvp_split q_made y_made kvp_made", primed=True)
        PROJ = M.bank[0:2]
        SC, PT, O, Y = M.psum[:, 2:4, :], M.psum[:, 4:6, :], M.bank[6], M.bank[7]
        block = S.block()
        scores = SC.rearrange("p j (h k) -> p (j h) k", k=KEYS)
        PIECES = [(w, src, half) for w in range(2) for src in range(2) for half in range(2)]
        NV = len(PIECES) // 2
        FIRST_SCORE = 5
        TURNED_V = (O, Y)

        def query_pieces(g, n):
            return [j for j in (2 * n + AHEAD, 2 * n + AHEAD + 1) if j < NQ or g is not LAST]

        def run(engine, turn):
            with engine.Fori(0, LAST) as g:
                turn(g)
            turn(LAST)

        @block.sync
        def _(sp):
            def loads(g):
                for quad in range(2):
                    if quad == 0 and isinstance(g, int):
                        continue
                    if quad == 0:
                        sp.wait_ge(s.kv_split, primed(g, 1, 0))
                        sp.wait_ge(s.kvp_split, primed(g, len(PIECES), 0))
                        load_kv(sp, g)
                    sp.wait_ge(s.wq_split, primed(g, 2 * QUAD, QUAD * quad))
                    load_q(sp, g * 2 + quad)
                    sp.wait_ge(s.wo_split, primed(g, 2 * QUAD, QUAD * quad))
                    load_o(sp, g * 2 + quad)

            loads(0)
            with sp.Fori(1, GROUPS) as g:
                loads(g)

        @block.tensor
        def _(pe):
            def project_q(g, j):
                pair, h = j // QUAD, j % QUAD
                start = pair % 4 * PAIR
                if pair % 4 == 0:
                    pe.wait_ge(s.wq_split, primed(g, 2 * QUAD, pair // 4 * QUAD + h + 1))
                pe.wait_ge(s.q_split, primed(g, NQ, max(j - 1, 0)))
                for k in range(KC):
                    last = mm3(pe, PROJ[j % 2][:, 0:PAIR], part(w_q, slice(None), k, tile_of(h)),
                               part(M.nT, slice(None), k, slice(start, start + PAIR)), k == 0, k == KC - 1)
                last.then_inc(s.q_made, 1)

            def score(g, n):
                pe.wait_ge(s.q_split, primed(g, NQ, QUAD * (n // 2 + 1)))
                pe.wait_ge(s.exped, primed(g, N * QUAD, QUAD * n))
                for h in range(QUAD):
                    last = mm3(pe, scores[:, h, :], part(qT, slice(None), n // 2 % 2, h, tile_of(n % 2)),
                               part(kT, slice(None), n % NB), True, True)
                last.then_inc(s.scored, 1)

            def turn_p(g, n):
                pe.wait_ge(s.p_ready, nth(g, N, n + 1))
                pe.wait_ge(s.pT_split, primed(g, N, n))
                for j in range(2):
                    for h in range(QUAD):
                        last = pe.transpose(PT[:, j, tile_of(h)], probs[:, h, tile_of(j)], M.ident[:])
                last.then_inc(s.p_turned, 1)

            def weigh_v(g, n):
                pe.wait_ge(s.pT_split, primed(g, N, n + 1))
                pe.wait_ge(s.oT_split, primed(g, N, n))
                if n == 0:
                    pe.wait_ge(s.kvp_split, primed(g, len(PIECES), len(PIECES)))
                for j in range(2):
                    last = mm3(pe, O, part(v, slice(None), n % NB, j), part(pT, slice(None), j), j == 0, j == 1)
                last.then_inc(s.o_made, 1)

            def project_out(g, n):
                pe.wait_ge(s.oT_hi, nth(g, N, n + 1))
                pe.wait_ge(s.y_added, primed(g, N, n))
                for h in range(QUAD):
                    if n % NB == 0:
                        pe.wait_ge(s.wo_split, primed(g, 2 * QUAD, n // NB * QUAD + h + 1))
                    pe.matmul(Y, oT[0][:, tile_of(h)], w_o[0][:, h], start=h == 0, stop=False)
                    pe.matmul(Y, oT[0][:, tile_of(h)], w_o[1][:, h], start=False, stop=False)
                pe.wait_ge(s.oT_split, primed(g, N, n + 1))
                for h in range(QUAD):
                    last = pe.matmul(Y, oT[1][:, tile_of(h)], w_o[0][:, h], start=False, stop=h == QUAD - 1)
                last.then_inc(s.y_made, 1)

            def turn_v(g, m):
                pe.wait_ge(s.vT_copied, nth(g, NV, m + 1))
                if m >= 2:
                    pe.wait_ge(s.kvp_split, primed(g, len(PIECES), NV + m - 1))
                elif m == 0:
                    pe.wait_ge(s.oT_split, primed(g, N, 0))
                else:
                    pe.wait_ge(s.y_added, primed(g, N, 0))
                for j in range(4):
                    last = pe.transpose(TURNED_V[m % 2][:, tile_of(j)], vT[:, m % 2, tile_of(j)], M.ident[:])
                last.then_inc(s.v_turned, 1)

            def turn(g):
                pe.wait_ge(s.kv_split, primed(g, 1, 1))
                pe.wait_ge(s.q_split, primed(g, NQ, AHEAD))
                for n, (w, src, half) in enumerate(PIECES):
                    if n < NV + 2:
                        pe.wait_ge(s.kvp_split, primed(g, len(PIECES), max(n - 1, 0)))
                    else:
                        pe.wait_ge(s.vT_copied, nth(g, NV, n - NV - 1))
                    source = (M.cT, M.nT)[src]
                    for k in range(KC):
                        last = mm3(pe, PROJ[n % 2], part(w_kv, slice(None), k, w),
                                   part(source, slice(None), k, slice(half * HALF, (half + 1) * HALF)),
                                   k == 0, k == KC - 1)
                    last.then_inc(s.kvp_made, 1)
                    if n + 1 == FIRST_SCORE:
                        pe.wait_ge(s.kvp_split, primed(g, len(PIECES), NV))
                        score(g, 0)
                    if n > NV:
                        turn_v(g, n - NV - 1)
                turn_v(g, NV - 1)
                for n in range(N):
                    turn_p(g, n)
                    for j in query_pieces(g, n)[0:1]:
                        project_q(g, j)
                    if n + 1 < N:
                        score(g, n + 1)
                    weigh_v(g, n)
                    for j in query_pieces(g, n)[1:2]:
                        project_q(g, j)
                    project_out(g, n)

            for j in range(AHEAD):
                project_q(0, j)
            run(pe, turn)

        @block.scalar
        def _(act):
            def hi_q(g, j):
                act.wait_ge(s.q_made, primed(g, NQ, j + 1))
                act.activation(qT[0][:, j // QUAD % 2, j % QUAD, :], PROJ[j % 2][:, 0:PAIR], ACT.Copy,
                               scale=SCALE).then_inc(s.q_hi, 1)

            def hi_wq(g, quad, h):
                act.wait_ge(s.q_loaded, nth(g, 32, 16 * (quad + 1)))
                if quad:
                    act.wait_ge(s.q_made, primed(g, NQ, QUAD * (4 * quad - 1) + h + 1))
                act.activation(w_q[0][:, :, tile_of(h)], raw_q[:, :, tile_of(h)], ACT.Copy).then_inc(s.wq_hi, 1)

            def hi_wo(g, quad, h):
                act.wait_ge(s.o_loaded, nth(g, 32, 16 * (quad + 1)))
                act.wait_ge(s.y_made, primed(g, N, NB * quad))
                act.activation(w_o[0][:, h, :], raw_o[:, h, :], ACT.Copy).then_inc(s.wo_hi, 1)

            def hi_kv(g, k):
                act.wait_ge(s.kv_loaded, nth(g, 16, 16 * (k + 1)))
                act.wait_ge(s.kvp_made, primed(g, len(PIECES), len(PIECES) * k))
                act.activation(w_kv[0][:], raw_kv[:], ACT.Copy).then_inc(s.kv_hi, 1)

            def exps(g, n):
                act.wait_ge(s.max_ready, nth(g, N, n + 1))
                for h in range(QUAD):
                    act.activation(probs[:, h, :], scores[:, h, :], ACT.Exp, bias=neg_max[:, h:h + 1],
                                   accum_out=sums[:, h:h + 1]).then_inc(s.exped, 1)

            def hi_kv_piece(n, bank):
                w, src, half = PIECES[n]
                act.activation((kT, v)[w][0][:, half * 4:half * 4 + 4, src, :],
                               bank.rearrange("p (b n) -> p b n", b=4), ACT.Copy).then_inc(s.kvp_hi, 1)

            def hi_v(g, m):
                act.wait_ge(s.v_turned, nth(g, NV, m + 1))
                hi_kv_piece(NV + m, TURNED_V[m % 2])

            def turn(g):
                for n in range(NV):
                    act.wait_ge(s.kvp_made, primed(g, len(PIECES), n + 1))
                    hi_kv_piece(n, PROJ[n % 2])
                for n in range(NV, len(PIECES)):
                    act.wait_ge(s.kvp_made, primed(g, len(PIECES), n + 1))
                    if n >= NV + 2:
                        act.wait_ge(s.v_turned, nth(g, NV, n - NV - 1))
                    act.activation(vT[:, n % 2, :], PROJ[n % 2], ACT.Copy).then_inc(s.vT_copied, 1)
                    if n + 1 == FIRST_SCORE:
                        exps(g, 0)
                    else:
                        hi_v(g, n - NV - 1)
                hi_v(g, NV - 1)
                for n in range(N):
                    act.wait_ge(s.p_turned, nth(g, N, n + 1))
                    act.activation(pT[0][:], PT, ACT.Copy).then_inc(s.pT_hi, 1)
                    if n % NB == 0:
                        for h in range(QUAD):
                            hi_wo(g, n // NB, h)
                    if n % NB in (4, 5) and (n < NB or g is not LAST):
                        for h in range(2):
                            hi_wq(g, n // NB + 1, 2 * (n % NB - 4) + h)
                    for j in query_pieces(g, n)[0:1]:
                        hi_q(g, j)
                    act.wait_ge(s.o_made, nth(g, N, n + 1))
                    act.activation(oT[0][:], O, ACT.Copy).then_inc(s.oT_hi, 1)
                    if n + 1 < N:
                        exps(g, n + 1)
                    for j in query_pieces(g, n)[1:2]:
                        hi_q(g, j)
                    if n == NB + 1 and g is not LAST:
                        hi_kv(g, 1)

            for h in range(QUAD):
                hi_wq(0, 0, h)
            for j in range(2):
                hi_q(0, j)
            hi_kv(0, 0)
            for j in range(2, AHEAD):
                hi_q(0, j)
            run(act, turn)

        @block.gpsimd
        def _(pool):
            def lo_wq(g, quad, h):
                pool.wait_ge(s.wq_hi, nth(g, 2 * QUAD, QUAD * quad + h + 1))
                pool.tensor_tensor(w_q[1][:, :, tile_of(h)], raw_q[:, :, tile_of(h)], f32(w_q[0][:, :, tile_of(h)]),
                                   ALU.subtract).then_inc(s.wq_split, 1)

            def turn(g):
                for n in range(N):
                    if n % NB == 0:
                        for h in range(QUAD):
                            pool.wait_ge(s.wo_hi, nth(g, 2 * QUAD, QUAD * (n // NB) + h + 1))
                            pool.tensor_tensor(w_o[1][:, h, :], raw_o[:, h, :], f32(w_o[0][:, h, :]),
                                               ALU.subtract).then_inc(s.wo_split, 1)
                    if n % NB in (4, 5) and (n < NB or g is not LAST):
                        for h in range(2):
                            lo_wq(g, n // NB + 1, 2 * (n % NB - 4) + h)
                    if n == NB + 1 and g is not LAST:
                        pool.wait_ge(s.kv_hi, nth(g, 1, 2))
                        pool.tensor_tensor(w_kv[1][:], raw_kv[:], f32(w_kv[0][:]), ALU.subtract).then_inc(s.kv_split, 1)

            run(pool, turn)

        @block.vector
        def _(dve):
            def lo_q(g, j):
                dve.wait_ge(s.q_hi, nth(g, NQ, j + 1))
                slot, h = j // QUAD % 2, j % QUAD
                dve.scalar_tensor_tensor(out=qT[1][:, slot, h, :], in0=PROJ[j % 2][:, 0:PAIR], scalar=SCALE,
                                         in1=f32(qT[0][:, slot, h, :]), op0=ALU.mult, op1=ALU.subtract).then_inc(s.q_split, 1)

            def row_max(g, n):
                dve.wait_ge(s.scored, nth(g, N, n + 1))
                dve.tensor_reduce(neg_max[:], scores, AX.X, ALU.max, negate=True).then_inc(s.max_ready, 1)

            def normalize(g, n):
                dve.wait_ge(s.exped, primed(g, N * QUAD, QUAD * (n + 1)))
                dve.reciprocal(inv_sums[:], sums[:]).then_inc(s.inverted, 1)
                dve.wait_ge(s.inverted, nth(g, N, n + 1))
                dve.tensor_tensor(probs[:], probs[:], inv_sums[:].unsqueeze(2).to_broadcast([P, QUAD, KEYS]),
                                  ALU.mult).then_inc(s.p_ready, 1)

            def add_y(g, n):
                x = M.x[:, n % NB, :]
                dve.wait_ge(s.y_made, primed(g, N, n + 1))
                dve.tensor_tensor(x, x, Y, ALU.add).then_inc(s.y_added, 1)
                if g is LAST and n >= NB:
                    tile_stats(dve, M, n % NB, s.y_added, primed(g, N, n + 1))

            def turn(g):
                for n, (w, src, half) in enumerate(PIECES):
                    if n == NV:
                        row_max(g, 0)
                        normalize(g, 0)
                    dve.wait_ge(s.kvp_hi, nth(g, len(PIECES), n + 1))
                    tiles = slice(half * 4, half * 4 + 4)
                    bank = TURNED_V[n % 2] if w else PROJ[n % 2]
                    dve.tensor_tensor((kT, v)[w][1][:, tiles, src, :], bank.rearrange("p (b n) -> p b n", b=4),
                                      f32((kT, v)[w][0][:, tiles, src, :]), ALU.subtract).then_inc(s.kvp_split, 1)
                for n in range(N):
                    if n:
                        add_y(g, n - 1)
                    dve.wait_ge(s.pT_hi, nth(g, N, n + 1))
                    dve.tensor_tensor(pT[1][:], PT, f32(pT[0][:]), ALU.subtract).then_inc(s.pT_split, 1)
                    for j in query_pieces(g, n)[0:1]:
                        lo_q(g, j)
                    if n + 1 < N:
                        row_max(g, n + 1)
                    dve.wait_ge(s.oT_hi, nth(g, N, n + 1))
                    dve.tensor_tensor(oT[1][:], O, f32(oT[0][:]), ALU.subtract).then_inc(s.oT_split, 1)
                    if n + 1 < N:
                        normalize(g, n + 1)
                    for j in query_pieces(g, n)[1:2]:
                        lo_q(g, j)
                add_y(g, N - 1)

            for h in range(QUAD):
                dve.wait_ge(s.wq_hi, h + 1)
                dve.tensor_tensor(w_q[1][:, :, tile_of(h)], raw_q[:, :, tile_of(h)], f32(w_q[0][:, :, tile_of(h)]),
                                  ALU.subtract).then_inc(s.wq_split, 1)
            for j in range(2):
                lo_q(0, j)
            dve.wait_ge(s.kv_hi, 1)
            dve.tensor_tensor(w_kv[1][:], raw_kv[:], f32(w_kv[0][:]), ALU.subtract).then_inc(s.kv_split, 1)
            for j in range(2, AHEAD):
                lo_q(0, j)
            run(dve, turn)



QMAX_ACT = 65535.0
I2 = 1376
C2 = -(-I2 // P)
BLOCK = 32


def quant_params(pool, s, T, peak, q, factor=None):
    def step(ins):
        T.steps += 1
        ins.then_inc(s.param_step, 1)
        pool.wait_ge(s.param_step, T.steps)

    step(pool.partition_all_reduce(T.peak[:], peak, P, bass.bass_isa.ReduceOp.max))
    step(pool.tensor_scalar(T.peak[:], T.peak[:], 0.0, None, ALU.max))
    if factor is not None:
        step(pool.tensor_scalar(T.peak[:], T.peak[:], factor, None, ALU.mult))
    step(pool.tensor_tensor(T.range[:], T.peak[:, 0:1], T.peak[:, 1:2], ALU.add))
    step(pool.tensor_scalar(q[:, 1:2], T.range[:], 1.0 / QMAX_ACT, 1e-12, ALU.mult, ALU.max))
    step(pool.tensor_tensor(q[:, 0:1], q[:, 1:2], T.const[:, 1:2], ALU.pow))
    step(pool.tensor_tensor(T.zero_point[:], T.peak[:, 1:2], q[:, 0:1], ALU.mult))
    step(pool.tensor_scalar(T.zero_point[:], T.zero_point[:], ROUND, -ROUND, ALU.add, ALU.add))
    step(pool.tensor_scalar(T.zero_point[:], T.zero_point[:], QMAX_ACT, -1.0, ALU.min, ALU.mult))
    step(pool.tensor_scalar(q[:, 2:3], T.zero_point[:], QMAX_ACT, None, ALU.add))


def round_up_part(act, out, in_, scale, T):
    return act.activation(out, in_, ACT.Identity, scale=scale, bias=T.const[:, 2:3])


def integer_part(dve, out, in_, limit):
    return dve.tensor_scalar(out, in_, -ROUND, limit, ALU.add, ALU.min)


def block_quant(dve, pool, s, W, slot, raw, width, n):
    nb = width // BLOCK
    blocks = raw.rearrange("p (b k) -> p b k", k=BLOCK)
    wq = W.wq[:, slot, 0:width].rearrange("p (b k) -> p b k", k=BLOCK)
    scale, inv = W.scale[:, slot, 0:nb], W.inv[:, 0:nb]
    if dve is not None:
        dve.tensor_reduce(W.amax[:, 0:nb], blocks, AX.X, ALU.max, apply_absolute_value=True).then_inc(s.amax_ready, 1)
        dve.wait_ge(s.amax_ready, n(1))
        dve.tensor_scalar(scale, W.amax[:, 0:nb], 1.0 / 7.0, 1e-12, ALU.mult, ALU.max).then_inc(s.scale_ready, 1)
        dve.wait_ge(s.scale_ready, n(1))
        dve.reciprocal(inv, scale).then_inc(s.inverted, 1)
        dve.wait_ge(s.inverted, n(1))
        dve.tensor_tensor(wq, blocks, inv.unsqueeze(2).to_broadcast([P, nb, BLOCK]), ALU.mult).then_inc(s.scaled, 1)
        dve.wait_ge(s.scaled, n(1))
        dve.tensor_scalar(wq, wq, ROUND, -ROUND, ALU.add, ALU.add).then_inc(s.rounded, 1)
    if pool is not None:
        pool.wait_ge(s.rounded, n(1))
        pool.tensor_tensor(wq, wq, scale.unsqueeze(2).to_broadcast([P, nb, BLOCK]), ALU.mult).then_inc(s.wq_ready, 1)


def weight_buffers(S, width, raws):
    W = Named()
    W.raw = S.sb("raw", [P, raws, width])
    W.wq = S.sb("wq", [P, 2, width])
    W.amax = S.sb("amax", [P, width // BLOCK])
    W.scale = S.sb("scale", [P, 2, width // BLOCK])
    W.inv = S.sb("inv", [P, width // BLOCK])
    return W


def ffn2_down_weights(nc, M, A, w_d):
    with ExitStack() as ctx:
        S = Scope(nc, M, ctx, "f2w")
        s = Named()
        s.raw_loaded, s.amax_ready, s.scale_ready, s.inverted = S.sems("raw_loaded amax_ready scale_ready inverted")
        s.scaled, s.rounded, s.wq_ready, s.turned, s.w_hi = S.sems("scaled rounded wq_ready turned w_hi")
        [s.w_split] = S.sems("w_split")
        W = weight_buffers(S, C2 * P, 2)
        GROUPS = [range(j, min(j + 4, C2)) for j in range(0, C2, 4)]
        block = S.block()

        @block.sync
        def _(sp):
            for o in range(KC):
                if o >= 2:
                    sp.wait_ge(s.scaled, o - 1)
                sp.dma_start(W.raw[:, o % 2, :], A["L2_ffn_down"][o]).then_inc(s.raw_loaded, 16)
                sp.wait_ge(s.raw_loaded, 16 * (o + 1))

        @block.gpsimd
        def _(pool):
            for o in range(KC):
                block_quant(None, pool, s, W, o % 2, W.raw[:, o % 2, :], C2 * P, lambda k, o=o: o + k)

        @block.vector
        def _(dve):
            def quantise(o):
                dve.wait_ge(s.raw_loaded, 16 * (o + 1))
                if o >= 2:
                    dve.wait_ge(s.turned, len(GROUPS) * (o - 1))
                block_quant(dve, None, s, W, o % 2, W.raw[:, o % 2, :], C2 * P, lambda k: o + k)

            quantise(0)
            for o in range(KC):
                if o + 1 < KC:
                    quantise(o + 1)
                for i, js in enumerate(GROUPS):
                    n = len(GROUPS) * o + i
                    dve.wait_ge(s.w_hi, n + 1)
                    dst = slice(js[0], js[-1] + 1)
                    dve.tensor_tensor(w_d[1][:, dst, tile_of(o)],
                                      M.bank[n % 3][:, 0:len(js) * P].rearrange("p (j o) -> p j o", o=P),
                                      f32(w_d[0][:, dst, tile_of(o)]), ALU.subtract).then_inc(s.w_split, 1)

        @block.tensor
        def _(pe):
            for o in range(KC):
                pe.wait_ge(s.wq_ready, o + 1)
                for i, js in enumerate(GROUPS):
                    n = len(GROUPS) * o + i
                    if n >= 3:
                        pe.wait_ge(s.w_split, n - 2)
                    for j in js:
                        last = pe.transpose(M.bank[n % 3][:, tile_of(j - js[0])], W.wq[:, o % 2, tile_of(j)], M.ident[:])
                    last.then_inc(s.turned, 1)

        @block.scalar
        def _(act):
            for o in range(KC):
                for i, js in enumerate(GROUPS):
                    n = len(GROUPS) * o + i
                    act.wait_ge(s.turned, n + 1)
                    act.activation(w_d[0][:, js[0]:js[-1] + 1, tile_of(o)],
                                   M.bank[n % 3][:, 0:len(js) * P].rearrange("p (j o) -> p j o", o=P),
                                   ACT.Copy).then_inc(s.w_hi, 1)


def ffn2_quantise_input(nc, M, T, xn):
    with ExitStack() as ctx:
        S = Scope(nc, M, ctx, "f2q")
        s = Named()
        s.const_set, s.peak_ready, s.param_step = S.sems("const_set peak_ready param_step")
        s.params_ready, s.shifted = S.sems("params_ready shifted")
        peak = S.sb("peak", [P, 2])
        block = S.block()

        @block.gpsimd
        def _(pool):
            for i, value in enumerate((0.0, -1.0, ROUND, -ROUND)):
                pool.memset(T.const[:, i:i + 1], value).then_inc(s.const_set, 1)
            pool.wait_ge(s.const_set, 4)
            pool.wait_ge(s.peak_ready, 2)
            T.steps = 0
            quant_params(pool, s, T, peak[:], T.q_x)
            pool.memset(T.peak[:, 0:1], 0.0).then_inc(s.params_ready, 1)

        @block.vector
        def _(dve):
            dve.tensor_reduce(peak[:, 0:1], xn[:], AX.XY, ALU.max).then_inc(s.peak_ready, 1)
            dve.tensor_reduce(peak[:, 1:2], xn[:], AX.XY, ALU.min, negate=True).then_inc(s.peak_ready, 1)
            dve.wait_ge(s.params_ready, 1)
            for b in range(NB):
                dve.wait_ge(s.shifted, b + 1)
                integer_part(dve, xn[:, b, :], xn[:, b, :], T.q_x[:, 2:3])

        @block.scalar
        def _(act):
            act.wait_ge(s.params_ready, 1)
            for b in range(NB):
                round_up_part(act, xn[:, b, :], xn[:, b, :], T.q_x[:, 0:1], T).then_inc(s.shifted, 1)


def ffn2_gate_up(nc, M, A, T, hidden, peaks):
    with ExitStack() as ctx:
        S = Scope(nc, M, ctx, "f2g")
        s = Named()
        s.made, s.copied, s.w_hi = S.sems("made copied w_hi")
        s.loaded = S.sems("gate_loaded up_loaded")
        s.amax_ready, s.scale_ready, s.inverted = S.sems("amax_ready scale_ready inverted", primed=True)
        s.scaled, s.rounded, s.wq_ready = S.sems("scaled rounded wq_ready", primed=True)
        s.turned, s.w_split = S.sems("turned w_split", primed=True)
        s.peaked = S.sems("gate_peaked up_peaked", primed=True)
        W = weight_buffers(S, D, 2)
        wT = S.pair("wT", [P, 2, KC, P])
        TURN = M.bank[0]
        OUT = [[M.bank[1], M.bank[2]], [M.bank[3], M.bank[4]]]
        LAST = C2 - 1
        block = S.block()

        def run(engine, step):
            with engine.Fori(0, LAST) as j:
                step(j, 0)
                step(j, 1)
            step(LAST, 0)
            step(LAST, 1)

        def units_on(j, u, n):
            return j is not LAST or u + n < 2

        @block.sync
        def _(sp):
            with sp.Fori(0, C2) as j:
                for w in range(2):
                    sp.wait_ge(s.scaled, primed(j, 2, max(w - 1, 0)))
                    sp.dma_start(W.raw[:, w, :], A["L2_ffn_gate_up"][bass.ds(j, 1), w].rearrange("g p n -> (g p) n")
                                 ).then_inc(s.loaded[w], 16)

        @block.gpsimd
        def _(pool):
            def quantise(j, u):
                block_quant(None, pool, s, W, u % 2, W.raw[:, u % 2, :], D, lambda k: primed(j, 2, u + k))

            quantise(0, 0)
            quantise(0, 1)
            run(pool, lambda j, u: quantise(j, u + 2) if units_on(j, u, 2) else None)

        @block.vector
        def _(dve):
            def quantise(j, u):
                dve.wait_ge(s.loaded[u % 2], nth(j, 16, 16 * (u // 2 + 1)))
                dve.wait_ge(s.turned, primed(j, 2, max(u - 1, 0)))
                block_quant(dve, None, s, W, u % 2, W.raw[:, u % 2, :], D, lambda k: primed(j, 2, u + k))

            def lo(j, u):
                dve.wait_ge(s.w_hi, nth(j, 2, u + 1))
                dve.tensor_tensor(wT[1][:, u % 2], TURN.rearrange("p (c n) -> p c n", c=KC), f32(wT[0][:, u % 2]),
                                  ALU.subtract).then_inc(s.w_split, 1)

            def peaks_of(j, u):
                for half in range(2):
                    dve.wait_ge(s.copied, nth(j, 4, 2 * u + half + 1))
                    col = peaks[:, u, :, bass.ds(j * 2 + half, 1)]
                    dve.tensor_reduce(col[:, 0, :], OUT[u][half], AX.X, ALU.max).then_inc(s.peaked[u], 1)
                    dve.tensor_reduce(col[:, 1, :], OUT[u][half], AX.X, ALU.min, negate=True).then_inc(s.peaked[u], 1)

            def step(j, u):
                if units_on(j, u, 2):
                    quantise(j, u + 2)
                if units_on(j, u, 1):
                    lo(j, u + 1)
                peaks_of(j, u)

            quantise(0, 0)
            quantise(0, 1)
            lo(0, 0)
            run(dve, step)

        @block.tensor
        def _(pe):
            def turn(j, u):
                pe.wait_ge(s.wq_ready, primed(j, 2, u + 1))
                pe.wait_ge(s.w_split, primed(j, 2, u))
                for c in range(KC):
                    last = pe.transpose(TURN[:, tile_of(c)], W.wq[:, u % 2, tile_of(c)], M.ident[:])
                last.then_inc(s.turned, 1)

            def product(j, u):
                pe.wait_ge(s.w_split, primed(j, 2, u + 1))
                pe.wait_ge(s.peaked[u], primed(j, 4, 0))
                for half in range(2):
                    for c in range(KC):
                        last = mm3(pe, OUT[u][half], part(wT, slice(None), u, c),
                                   part(M.nT, slice(None), c, slice(half * HALF, (half + 1) * HALF)),
                                   c == 0, c == KC - 1)
                    last.then_inc(s.made, 1)

            def step(j, u):
                if units_on(j, u, 1):
                    turn(j, u + 1)
                product(j, u)

            turn(0, 0)
            run(pe, step)

        @block.scalar
        def _(act):
            def hi(j, u):
                act.wait_ge(s.turned, primed(j, 2, u + 1))
                act.activation(wT[0][:, u % 2], TURN.rearrange("p (c n) -> p c n", c=KC), ACT.Copy).then_inc(s.w_hi, 1)

            def copy_out(j, u):
                for half in range(2):
                    act.wait_ge(s.made, nth(j, 4, 2 * u + half + 1))
                    act.activation(hidden[u][:, bass.ds(j * TOK + half * HALF, HALF)], OUT[u][half], ACT.Copy,
                                   scale=T.q_x[:, 1:2]).then_inc(s.copied, 1)

            def step(j, u):
                if units_on(j, u, 1):
                    hi(j, u + 1)
                copy_out(j, u)

            hi(0, 0)
            run(act, step)


def ffn2_down(nc, M, T, hidden, peaks, w_d):
    with ExitStack() as ctx:
        S = Scope(nc, M, ctx, "f2d")
        s = Named()
        s.peak_ready, s.param_step, s.params_ready = S.sems("peak_ready param_step params_ready")
        s.u_shifted, s.u_int, s.g_shifted, s.g_int, s.sig_made = S.sems("u_shifted u_int g_shifted g_int sig_made")
        s.sig_shifted, s.sig_int, s.s_made, s.s_peaked = S.sems("sig_shifted sig_int s_made s_peaked")
        s.s_shifted, s.o_made, s.o_peaked, s.o_shifted = S.sems("s_shifted o_made o_peaked o_shifted")
        s.o_int, s.o_hi, s.o_split, s.y_made, s.y_added = S.sems("o_int o_hi o_split y_made y_added")
        s.unit_made, s.s_rounded = S.sems("unit_made s_rounded")
        peak = S.sb("peak", [P, 2, 2])
        q = S.sb("q", [P, 4, 3])
        sg = S.sb("sg", [P, 1])
        unit = S.sb("unit", [P, 1])
        so = S.sb("so", [P, 1])
        sig = S.sb("sig", [P, 2, TOK])
        o_hi_lo = M.nT
        gate, up = hidden
        q_g, q_u, q_s, q_o = (q[:, i] for i in range(4))
        Y = M.bank
        AHEAD = 2
        block = S.block()

        def at(t, j):
            return t[:, j * TOK:(j + 1) * TOK]

        @block.gpsimd
        def _(pool):
            T.steps = 0

            def params(n, w, q, factor):
                pool.wait_ge(s.peak_ready, n)
                quant_params(pool, s, T, peak[:, w], q, factor)

            params(2, 0, q_g, T.q_x[:, 1:2])
            pool.tensor_scalar(sg[:], q_g[:, 1:2], 2.0 ** -16, None, ALU.mult).then_inc(s.params_ready, 1)
            params(4, 1, q_u, T.q_x[:, 1:2])
            pool.memset(T.peak[:, 0:1], 0.0).then_inc(s.params_ready, 1)
            for j in range(C2):
                pool.wait_ge(s.u_shifted, j + 1)
                integer_part(pool, at(up, j), at(up, j), q_u[:, 2:3]).then_inc(s.u_int, 1)
            params(6, 0, q_s, None)
            pool.memset(T.peak[:, 0:1], 0.0).then_inc(s.params_ready, 1)
            pool.tensor_tensor(unit[:], q_s[:, 1:2], q_u[:, 1:2], ALU.mult).then_inc(s.unit_made, 1)
            pool.wait_ge(s.unit_made, 1)
            params(8, 1, q_o, unit[:])
            pool.tensor_scalar(so[:], q_o[:, 0:1], unit[:], None, ALU.mult).then_inc(s.params_ready, 1)

        @block.scalar
        def _(act):
            act.preload_act_table_set("sigmoid_and_others")
            def shift_gate(j):
                round_up_part(act, at(gate, j), at(gate, j), q_g[:, 0:1], T).then_inc(s.g_shifted, 1)

            act.wait_ge(s.params_ready, 1)
            for j in range(AHEAD):
                shift_gate(j)
            act.wait_ge(s.params_ready, 2)
            for j in range(C2):
                if j + AHEAD < C2:
                    shift_gate(j + AHEAD)
                act.wait_ge(s.g_int, j + 1)
                if j >= 2:
                    act.wait_ge(s.s_made, j - 1)
                act.activation(sig[:, j % 2, :], at(gate, j), ACT.Sigmoid, scale=q_g[:, 1:2]).then_inc(s.sig_made, 1)
                act.wait_ge(s.sig_made, j + 1)
                act.activation(sig[:, j % 2, :], sig[:, j % 2, :], ACT.Identity, scale=65536.0,
                               bias=T.const[:, 2:3]).then_inc(s.sig_shifted, 1)
                round_up_part(act, at(up, j), at(up, j), q_u[:, 0:1], T).then_inc(s.u_shifted, 1)
            act.wait_ge(s.params_ready, 3)
            for j in range(C2 + 1):
                if j < C2:
                    round_up_part(act, at(gate, j), at(gate, j), q_s[:, 0:1], T).then_inc(s.s_shifted, 1)
                if j:
                    act.wait_ge(s.s_shifted, j)
                    act.activation(at(gate, j - 1), at(gate, j - 1), ACT.Identity,
                                   bias=T.const[:, 3:4]).then_inc(s.s_rounded, 1)
            act.wait_ge(s.params_ready, 4)
            for j in range(C2):
                round_up_part(act, at(gate, j), at(gate, j), so[:], T).then_inc(s.o_shifted, 1)
                act.wait_ge(s.o_int, j + 1)
                if j >= 4:
                    act.wait_ge(s.y_made, NB * (j - 3))
                act.activation(o_hi_lo[0][:, j % 4, :], at(gate, j), ACT.Copy).then_inc(s.o_hi, 1)

        @block.vector
        def _(dve):
            for n, (w, row) in enumerate(((0, 0), (0, 1), (1, 0), (1, 1))):
                dve.tensor_reduce(peak[:, w, row:row + 1], peaks[:, w, row, :], AX.X, ALU.max).then_inc(s.peak_ready, 1)
            def gate_int(j):
                dve.wait_ge(s.g_shifted, j + 1)
                integer_part(dve, at(gate, j), at(gate, j), q_g[:, 2:3]).then_inc(s.g_int, 1)

            for j in range(AHEAD):
                gate_int(j)
            for j in range(C2):
                if j + AHEAD < C2:
                    gate_int(j + AHEAD)
                dve.wait_ge(s.sig_shifted, j + 1)
                integer_part(dve, sig[:, j % 2, :], sig[:, j % 2, :], QMAX_ACT).then_inc(s.sig_int, 1)
                dve.wait_ge(s.sig_int, j + 1)
                dve.scalar_tensor_tensor(out=at(gate, j), in0=at(gate, j), scalar=sg[:], in1=sig[:, j % 2, :],
                                         op0=ALU.mult, op1=ALU.mult).then_inc(s.s_made, 1)
                dve.wait_ge(s.s_made, j + 1)
                dve.tensor_reduce(peaks[:, 0, 0, j:j + 1], at(gate, j), AX.X, ALU.max).then_inc(s.s_peaked, 1)
                dve.tensor_reduce(peaks[:, 0, 1, j:j + 1], at(gate, j), AX.X, ALU.min, negate=True).then_inc(s.s_peaked, 1)
            dve.wait_ge(s.s_peaked, 2 * C2)
            dve.wait_ge(s.params_ready, 1)
            for row in range(2):
                dve.tensor_reduce(peak[:, 0, row:row + 1], peaks[:, 0, row, 0:C2], AX.X, ALU.max).then_inc(s.peak_ready, 1)
            for j in range(C2):
                dve.wait_ge(s.s_rounded, j + 1)
                dve.wait_ge(s.u_int, j + 1)
                dve.scalar_tensor_tensor(out=at(gate, j), in0=at(gate, j), scalar=q_s[:, 2:3], in1=at(up, j),
                                         op0=ALU.min, op1=ALU.mult).then_inc(s.o_made, 1)
                dve.wait_ge(s.o_made, j + 1)
                dve.tensor_reduce(peaks[:, 1, 0, j:j + 1], at(gate, j), AX.X, ALU.max).then_inc(s.o_peaked, 1)
                dve.tensor_reduce(peaks[:, 1, 1, j:j + 1], at(gate, j), AX.X, ALU.min, negate=True).then_inc(s.o_peaked, 1)
            dve.wait_ge(s.o_peaked, 2 * C2)
            for row in range(2):
                dve.tensor_reduce(peak[:, 1, row:row + 1], peaks[:, 1, row, 0:C2], AX.X, ALU.max).then_inc(s.peak_ready, 1)
            for j in range(C2):
                dve.wait_ge(s.o_shifted, j + 1)
                integer_part(dve, at(gate, j), at(gate, j), q_o[:, 2:3]).then_inc(s.o_int, 1)
                dve.wait_ge(s.o_hi, j + 1)
                dve.tensor_tensor(o_hi_lo[1][:, j % 4, :], at(gate, j), f32(o_hi_lo[0][:, j % 4, :]),
                                  ALU.subtract).then_inc(s.o_split, 1)
            for b in range(NB):
                dve.wait_ge(s.y_made, NB * (C2 - 1) + b + 1)
                dve.scalar_tensor_tensor(out=M.x[:, b, :], in0=Y[b], scalar=q_o[:, 1:2], in1=M.x[:, b, :],
                                         op0=ALU.mult, op1=ALU.add).then_inc(s.y_added, 1)
                tile_stats(dve, M, b, s.y_added, b + 1)

        @block.tensor
        def _(pe):
            for j in range(C2):
                pe.wait_ge(s.o_split, j + 1)
                for b in range(NB):
                    mm3(pe, Y[b], part(o_hi_lo, slice(None), j % 4, tile_of(b)), part(w_d, slice(None), j),
                        j == 0, j == C2 - 1).then_inc(s.y_made, 1)


def ffn2_stage(nc, M, A):
    with ExitStack() as ctx:
        S = Scope(nc, M, ctx, "f2")
        T = Named()
        T.q_x = S.sb("q_x", [P, 3])
        T.const = S.sb("const", [P, 4])
        T.peak = S.sb("peak", [P, 2])
        T.range = S.sb("range", [P, 1])
        T.zero_point = S.sb("zero_point", [P, 1])
        with ExitStack() as xn_ctx:
            xn = Scope(nc, M, xn_ctx, "f2x").sb("xn", [P, NB, D])
            norm_stage(nc, M, "n5", xn=xn, turn=False)
            ffn2_quantise_input(nc, M, T, xn)
            norm_stage(nc, M, "t5", xn=xn, normalize=False)
        w_d = S.pair("w_d", [P, C2, D])
        ffn2_down_weights(nc, M, A, w_d)
        hidden = [S.sb(name, [P, C2 * TOK]) for name in ("gate", "up")]
        peaks = S.sb("peaks", [P, 2, 2, 2 * C2])
        ffn2_gate_up(nc, M, A, T, hidden, peaks)
        ffn2_down(nc, M, T, hidden, peaks, w_d)



def attn3_stage(nc, M, A):
    SCALE = 1.0 / float(np.sqrt(D))
    with ExitStack() as ctx:
        S = Scope(nc, M, ctx, "a3")
        raw_w = S.sb("raw_w", [P, 2, KC, D])
        bias = S.sb("bias", [P, 2, KC])
        kT = S.pair("kT", [P, KC, TOK])
        raw_ctx = S.sb("raw_ctx", [P, 2, TOK])
        s = Named()
        s.bias_loaded, s.wq_loaded, s.wk_loaded = S.sems("bias_loaded wq_loaded wk_loaded")
        s.ctx_loaded = S.sems("even_ctx_loaded odd_ctx_loaded")

        def load_ctx(sp, c):
            sp.dma_start(raw_ctx[:, c % 2, :], A["ctxT"][c * P:(c + 1) * P, :]).then_inc(s.ctx_loaded[c % 2], 16)

        def prefetch(sp):
            sp.dma_start(bias[:], A["L3_xattn_bias"]).then_inc(s.bias_loaded, 16)
            for i, loaded in enumerate((s.wq_loaded, s.wk_loaded)):
                sp.dma_start(raw_w[:, i], A["L3_xattn_Wqk"][i]).then_inc(loaded, 16)
            load_ctx(sp, 0)
            load_ctx(sp, 1)

        norm_stage(nc, M, "n6", prefetch=prefetch)
        w = S.pair("w", [P, 2, KC, D])
        bias_q = S.sb("bias_q", [P, KC])
        biased = S.sb("biased", [P, 2, HALF])
        qT = S.pair("qT", [P, KC, TOK])
        raw_f = raw_w[:, 0, 0:2]
        feat = w[0][:, 0, 0:2], w[1][:, 0, 0:2]
        neg_max = S.sb("neg_max", [P, 2])
        sums = S.sb("sums", [P, 2])
        inv_sums = S.sb("inv_sums", [P, 2])
        probs = biased[:, :, 0:P]
        pT = S.pair("pT", [P, 2, P])
        s.f_loaded, s.bias_ready, s.ctx_hi, s.ctx_split = S.sems("f_loaded bias_ready ctx_hi ctx_split")
        s.w_hi, s.w_split, s.proj_made, s.biased, s.proj_hi = S.sems("w_hi w_split proj_made biased proj_hi")
        s.proj_split, s.f_hi, s.f_split, s.scored, s.max_ready = S.sems("proj_split f_hi f_split scored max_ready")
        s.exped, s.inverted, s.turned, s.pT_hi, s.pT_split = S.sems("exped inverted turned pT_hi pT_split")
        s.y_made, s.y_added = S.sems("y_made y_added")
        block = S.block()
        UNITS = [(i, c, half) for i in range(2) for c in range(KC) for half in range(2)]
        dst = (qT, kT)
        SCORES, PT, Y = M.bank[0:2], M.bank[2:4], M.bank[4:6]

        @block.sync
        def _(sp):
            for c in range(2, KC):
                sp.wait_ge(s.ctx_split, c - 1)
                load_ctx(sp, c)
            for b in range(NB):
                if b == 0:
                    sp.wait_ge(s.w_split, 1)
                if b >= 2:
                    sp.wait_ge(s.f_split, b - 1)
                sp.dma_start(raw_f[:, b % 2, :], A["ctx"][b]).then_inc(s.f_loaded, 16)
                sp.wait_ge(s.f_loaded, 16 * (b + 1))

        @block.tensor
        def _(pe):
            for n, (i, c, half) in enumerate(UNITS):
                pe.wait_ge(s.w_split, i + 1)
                if i:
                    pe.wait_ge(s.ctx_split, KC)
                if n >= 4:
                    pe.wait_ge(s.biased, n - 3)
                for k in range(KC):
                    last = mm3(pe, M.bank[n % 4], part(w, slice(None), i, k, tile_of(c)),
                               part((M.nT, M.cT)[i], slice(None), k, slice(half * HALF, (half + 1) * HALF)),
                               k == 0, k == KC - 1)
                last.then_inc(s.proj_made, 1)

            def score(b):
                if b >= 2:
                    pe.wait_ge(s.exped, b - 1)
                for k in range(KC):
                    last = mm3(pe, SCORES[b % 2][:, 0:P], part(qT, slice(None), k, tile_of(b)),
                               part(kT, slice(None), k, tile_of(b)), k == 0, k == KC - 1)
                last.then_inc(s.scored, 1)

            def turn_p(b):
                pe.wait_ge(s.exped, b + 1)
                if b >= 2:
                    pe.wait_ge(s.pT_split, b - 1)
                pe.transpose(PT[b % 2][:, 0:P], probs[:, b % 2, :], M.ident[:]).then_inc(s.turned, 1)

            pe.wait_ge(s.proj_split, len(UNITS))
            score(0)
            score(1)
            turn_p(0)
            for b in range(NB):
                if b + 2 < NB:
                    score(b + 2)
                if b + 1 < NB:
                    turn_p(b + 1)
                pe.wait_ge(s.pT_split, b + 1)
                pe.wait_ge(s.f_split, b + 1)
                if b >= 2:
                    pe.wait_ge(s.y_added, b - 1)
                mm3(pe, Y[b % 2], part(pT, slice(None), b % 2), part(feat, slice(None), b % 2), True, True
                    ).then_inc(s.y_made, 1)

        @block.scalar
        def _(act):
            def hi_w(i):
                act.wait_ge((s.wq_loaded, s.wk_loaded)[i], 16)
                act.activation(w[0][:, i], raw_w[:, i], ACT.Copy).then_inc(s.w_hi, 1)

            def exps(b):
                act.wait_ge(s.max_ready, b + 1)
                if b >= 2:
                    act.wait_ge(s.turned, b - 1)
                    act.wait_ge(s.inverted, b - 1)
                act.activation(probs[:, b % 2, :], SCORES[b % 2][:, 0:P], ACT.Exp, bias=neg_max[:, b % 2:b % 2 + 1],
                               accum_out=sums[:, b % 2:b % 2 + 1]).then_inc(s.exped, 1)

            def hi_f(b):
                act.wait_ge(s.f_loaded, 16 * (b + 1))
                if b >= 2:
                    act.wait_ge(s.y_made, b - 1)
                act.activation(feat[0][:, b % 2, :], raw_f[:, b % 2, :], ACT.Copy).then_inc(s.f_hi, 1)

            def hi_p(b):
                act.wait_ge(s.turned, b + 1)
                act.activation(pT[0][:, b % 2, :], PT[b % 2][:, 0:P], ACT.Copy).then_inc(s.pT_hi, 1)

            hi_w(0)
            act.wait_ge(s.bias_ready, 1)
            for n, (i, c, half) in enumerate(UNITS):
                act.wait_ge(s.proj_made, n + 1)
                if n >= 2:
                    act.wait_ge(s.proj_split, n - 1)
                act.activation(biased[:, n % 2, :], M.bank[n % 4], ACT.Identity, scale=1.0 if i else SCALE,
                               bias=(bias[:, 1, c:c + 1] if i else bias_q[:, c:c + 1])).then_inc(s.biased, 1)
                act.wait_ge(s.biased, n + 1)
                act.activation(dst[i][0][:, c, half * HALF:(half + 1) * HALF], biased[:, n % 2, :],
                               ACT.Copy).then_inc(s.proj_hi, 1)
                if n < KC:
                    act.wait_ge(s.ctx_loaded[n % 2], 16 * (n // 2 + 1))
                    act.activation(M.cT[0][:, n, :], raw_ctx[:, n % 2, :], ACT.Copy).then_inc(s.ctx_hi, 1)
                elif n == KC:
                    hi_w(1)
            exps(0)
            hi_f(0)
            exps(1)
            hi_p(0)
            for b in range(NB - 1):
                if b + 2 < NB:
                    exps(b + 2)
                hi_f(b + 1)
                hi_p(b + 1)

        @block.vector
        def _(dve):
            def lo_w(i):
                dve.wait_ge(s.w_hi, i + 1)
                dve.tensor_tensor(w[1][:, i], raw_w[:, i], f32(w[0][:, i]), ALU.subtract).then_inc(s.w_split, 1)

            def row_max(b):
                dve.wait_ge(s.scored, b + 1)
                dve.tensor_reduce(neg_max[:, b % 2:b % 2 + 1], SCORES[b % 2][:, 0:P], AX.X, ALU.max,
                                  negate=True).then_inc(s.max_ready, 1)

            def invert(b):
                dve.wait_ge(s.exped, b + 1)
                dve.reciprocal(inv_sums[:, b % 2:b % 2 + 1], sums[:, b % 2:b % 2 + 1]).then_inc(s.inverted, 1)

            def lo_f(b):
                dve.wait_ge(s.f_hi, b + 1)
                dve.tensor_tensor(feat[1][:, b % 2, :], raw_f[:, b % 2, :], f32(feat[0][:, b % 2, :]),
                                  ALU.subtract).then_inc(s.f_split, 1)

            def lo_p(b):
                dve.wait_ge(s.pT_hi, b + 1)
                dve.tensor_tensor(pT[1][:, b % 2, :], PT[b % 2][:, 0:P], f32(pT[0][:, b % 2, :]),
                                  ALU.subtract).then_inc(s.pT_split, 1)

            dve.wait_ge(s.bias_loaded, 16)
            dve.tensor_scalar(bias_q[:], bias[:, 0, :], SCALE, None, ALU.mult).then_inc(s.bias_ready, 1)
            lo_w(0)
            for n, (i, c, half) in enumerate(UNITS):
                tokens = slice(half * HALF, (half + 1) * HALF)
                dve.wait_ge(s.proj_hi, n + 1)
                dve.tensor_tensor(dst[i][1][:, c, tokens], biased[:, n % 2, :], f32(dst[i][0][:, c, tokens]),
                                  ALU.subtract).then_inc(s.proj_split, 1)
                if n < KC:
                    dve.wait_ge(s.ctx_hi, n + 1)
                    dve.tensor_tensor(M.cT[1][:, n, :], raw_ctx[:, n % 2, :], f32(M.cT[0][:, n, :]),
                                      ALU.subtract).then_inc(s.ctx_split, 1)
                elif n == KC:
                    lo_w(1)
            row_max(0)
            lo_f(0)
            row_max(1)
            invert(0)
            lo_p(0)
            for b in range(NB):
                if b + 2 < NB:
                    row_max(b + 2)
                if b + 1 < NB:
                    invert(b + 1)
                    lo_f(b + 1)
                    lo_p(b + 1)
                dve.wait_ge(s.inverted, b + 1)
                dve.wait_ge(s.y_made, b + 1)
                dve.scalar_tensor_tensor(out=M.x[:, b, :], in0=Y[b % 2], scalar=inv_sums[:, b % 2:b % 2 + 1],
                                         in1=M.x[:, b, :], op0=ALU.mult, op1=ALU.add).then_inc(s.y_added, 1)
                tile_stats(dve, M, b, s.y_added, b + 1)



def ffn3_stage(nc, M, A, xn, rms, out):
    NS = 4
    W = NS * NS + 2 * NS
    ITERS = 50
    UNROLL = 5
    DVE_TILES, POOL_TILES = range(0, 6), range(6, NB)
    with ExitStack() as ctx:
        S = Scope(nc, M, ctx, "f3")
        raw_w = S.sb("raw_w", [P, KC, W])
        w = S.pair("w", [P, KC, W])
        raw_b = S.sb("raw_b", [P, P])
        w_b = S.pair("w_b", [P, P])
        base = S.sb("base", [P, W])
        gate = S.sb("gate", [P, 1])
        keep = S.sb("keep", [P, 1])
        eye = S.sb("eye", [P, NS * NS])
        logits_T = S.sb("logits_T", [W, TOK])
        logits = S.sb("logits", [P, NB, W])
        L = S.sb("L", [P, NB, NS, NS])
        E = S.sb("E", [P, NB, NS, NS])
        peak = S.sb("peak", [P, NB, NS])
        total = S.sb("total", [P, NB, NS])
        H = S.sb("H", [P, NB, NS * NS])
        pp = S.sb("pp", [P, NB, 2, NS])
        pp_peak = S.sb("pp_peak", [P, NB, 2])
        x_pre = S.sb("x_pre", [P, NB, P])
        xT = S.pair("xT", [P, NB, P])
        scaled = S.sb("scaled", [P, NB, P])
        raw_xT = S.sb("raw_xT", [P, NB, P])
        y = S.sb("y", [P, NB, P])
        s = Named()
        s.w_loaded, s.b_loaded, s.small_loaded, s.w_hi = S.sems("w_loaded b_loaded small_loaded w_hi")
        s.w_split, s.b_hi, s.b_split, s.logits_made, s.small = S.sems("w_split b_hi b_split logits_made small")
        s.pp_less, s.pp_exped, s.gated, s.less_max, s.exped = S.sems("pp_less pp_exped gated less_max exped")
        s.summed, s.logged, s.pre_step, s.turned = S.sems("summed logged pre_step turned")
        s.xT_hi, s.xT_split, s.y_made, s.H_exped = S.sems("xT_hi xT_split y_made H_exped")
        s.xT_copied, s.y_copied, s.scaled = S.sems("xT_copied y_copied scaled")
        s.pp_ready, s.H_ready, s.branch_added, s.stored = S.sems("pp_ready H_ready branch_added stored")
        s.dve_mixed, s.pool_mixed = S.sems("dve_mixed pool_mixed")
        [s.stepped] = S.sems("stepped", primed=True)
        s.peaked, s.logits_copied, s.logits_turned = S.sems("peaked logits_copied logits_turned")
        LOG_T = M.bank[5:7]
        HALVES = (Named(), Named())
        for number, half in enumerate(HALVES):
            half.number, half.tiles = number, slice(number * NB // 2, (number + 1) * NB // 2)
        block = S.block()
        LOG, YB = M.bank[0], M.psum[:, 1:3, :].rearrange("p a (b n) -> p (a b) n", n=P)
        XT = M.psum[:, 3:5, :].rearrange("p a (b n) -> p (a b) n", n=P)

        @block.sync
        def _(sp):
            sp.dma_start(raw_w[:], A["L3_ffn_W"]).then_inc(s.w_loaded, 16)
            sp.dma_start(raw_b[:], A["L3_ffn_W_branch"]).then_inc(s.b_loaded, 16)
            for t, name in ((base, "L3_ffn_base"), (gate, "L3_ffn_gate"), (eye, "eye")):
                sp.dma_start(t[:], A[name]).then_inc(s.small_loaded, 16)
            for k, b in enumerate(DVE_TILES):
                sp.wait_ge(s.dve_mixed, NS * NS * (k + 1))
                sp.dma_start(out[b], M.x[:, b, :]).then_inc(s.stored, 16)
            for k, b in enumerate(POOL_TILES):
                sp.wait_ge(s.pool_mixed, NS * (k + 1))
                sp.dma_start(out[b], M.x[:, b, :]).then_inc(s.stored, 16)
            sp.wait_ge(s.stored, 16 * NB)

        @block.gpsimd
        def _(pool):
            products = [0]

            def product(out, a, b):
                pool.tensor_tensor(out, a, b, ALU.mult).then_inc(s.scaled, 1)
                products[0] += 1
                pool.wait_ge(s.scaled, products[0])

            def per_token(weights):
                return weights.unsqueeze(2).to_broadcast([P, NB, P])

            pool.wait_ge(s.pp_ready, 1)
            product(x_pre[:], xn[:, :, tile_of(0)], per_token(pp[:, :, 0, 0]))
            for n in range(1, NS):
                product(scaled[:], xn[:, :, tile_of(n)], per_token(pp[:, :, 0, n]))
                pool.tensor_tensor(x_pre[:], x_pre[:], scaled[:], ALU.add).then_inc(s.pre_step, 1)
                pool.wait_ge(s.pre_step, n)
            pool.wait_ge(s.xT_copied, 1)
            pool.tensor_copy(xT[0][:], raw_xT[:]).then_inc(s.xT_hi, 1)
            pool.wait_ge(s.xT_hi, 1)
            pool.tensor_tensor(xT[1][:], raw_xT[:], f32(xT[0][:]), ALU.subtract).then_inc(s.xT_split, 1)
            pool.wait_ge(s.y_copied, 1)
            for n in range(NS):
                product(scaled[:], y[:], per_token(pp[:, :, 1, n]))
                stream = M.x[:, :, tile_of(n)]
                pool.tensor_tensor(stream, stream, scaled[:], ALU.add).then_inc(s.branch_added, 1)
                pool.wait_ge(s.branch_added, n + 1)
            pool.wait_ge(s.H_ready, 1)
            four = scaled[:, 0:NS, :]
            for k, b in enumerate(POOL_TILES):
                for j in range(NS):
                    column = H[:, b, :].rearrange("p (n j) -> p j n", j=NS)[:, j]
                    product(four, xn[:, b, tile_of(j)].unsqueeze(1).to_broadcast([P, NS, P]),
                            column.unsqueeze(2).to_broadcast([P, NS, P]))
                    x = M.x[:, b, :].rearrange("p (n c) -> p n c", n=NS)
                    pool.tensor_tensor(x, x, four, ALU.add).then_inc(s.pool_mixed, 1)
                    pool.wait_ge(s.pool_mixed, NS * k + j + 1)

        @block.tensor
        def _(pe):
            pe.wait_ge(s.w_split, 1)
            for half in range(2):
                for k in range(KC):
                    last = mm3(pe, LOG_T[half][0:W, :], part(w, slice(None), k),
                               part(M.nT, slice(None), k, slice(half * HALF, (half + 1) * HALF)), k == 0, k == KC - 1)
                last.then_inc(s.logits_made, 1)
            for b in range(NB):
                if b % 4 == 0:
                    pe.wait_ge(s.logits_copied, b // 4 + 1)
                last = pe.transpose(LOG[:, b * W:(b + 1) * W], logits_T[:, tile_of(b)], M.ident[0:W, 0:W])
            last.then_inc(s.logits_turned, 1)
            for b in range(NB):
                pe.wait_ge(s.pre_step, NS - 1)
                last = pe.transpose(XT[:, b, :], x_pre[:, b, :], M.ident[:])
            last.then_inc(s.turned, 1)
            pe.wait_ge(s.b_split, 1)
            pe.wait_ge(s.xT_split, 1)
            for b in range(NB):
                last = mm3(pe, YB[:, b, :], part(xT, slice(None), b), (w_b[0][:], w_b[1][:]), True, True)
            last.then_inc(s.y_made, 1)

        @block.scalar
        def _(act):
            act.wait_ge(s.w_loaded, 16)
            act.activation(w[0][:], raw_w[:], ACT.Copy).then_inc(s.w_hi, 1)
            act.wait_ge(s.b_loaded, 16)
            act.activation(w_b[0][:], raw_b[:], ACT.Copy).then_inc(s.b_hi, 1)
            act.wait_ge(s.small_loaded, 48)
            act.activation(gate[:], gate[:], ACT.Sigmoid).then_inc(s.gated, 1)
            for half in range(2):
                act.wait_ge(s.logits_made, half + 1)
                act.activation(logits_T[:, half * HALF:(half + 1) * HALF], LOG_T[half][0:W, :],
                               ACT.Copy).then_inc(s.logits_copied, 1)
            act.wait_ge(s.pp_less, 1)
            act.activation(pp[:], pp[:], ACT.Exp).then_inc(s.pp_exped, 1)
            act.preload_act_table_set("natural_log_exp_and_others")

            def turn(i):
                for k in range(2 * UNROLL):
                    for half in HALVES:
                        act.wait_ge(s.less_max, nth(i, 4 * UNROLL, 2 * k + half.number + 1))
                        act.activation(E[:, half.tiles], L[:, half.tiles], ACT.Exp).then_inc(s.exped, 1)
                    for half in HALVES:
                        act.wait_ge(s.summed, nth(i, 4 * UNROLL, 2 * k + half.number + 1))
                        act.activation(total[:, half.tiles], total[:, half.tiles], ACT.Ln).then_inc(s.logged, 1)

            with act.Fori(0, 2) as i:
                turn(i)
            act.wait_ge(s.turned, 1)
            act.activation(raw_xT[:], XT, ACT.Copy).then_inc(s.xT_copied, 1)
            with act.Fori(2, 4) as i:
                turn(i)
            act.wait_ge(s.y_made, 1)
            act.activation(y[:], YB, ACT.Copy).then_inc(s.y_copied, 1)
            with act.Fori(4, ITERS // UNROLL) as i:
                turn(i)
            act.wait_ge(s.stepped, primed(0, 0, 4 * ITERS))
            act.activation(E[:], L[:], ACT.Exp).then_inc(s.H_exped, 1)

        @block.vector
        def _(dve):
            steps = [0]

            def step(ins):
                ins.then_inc(s.small, 1)
                steps[0] += 1
                dve.wait_ge(s.small, steps[0])

            dve.wait_ge(s.w_hi, 1)
            dve.tensor_tensor(w[1][:], raw_w[:], f32(w[0][:]), ALU.subtract).then_inc(s.w_split, 1)
            dve.wait_ge(s.b_hi, 1)
            dve.tensor_tensor(w_b[1][:], raw_b[:], f32(w_b[0][:]), ALU.subtract).then_inc(s.b_split, 1)
            dve.wait_ge(s.small_loaded, 48)
            dve.wait_ge(s.gated, 1)
            step(dve.tensor_scalar(keep[:], gate[:], -1.0, 1.0, ALU.mult, ALU.add))
            step(dve.tensor_scalar(eye[:], eye[:], keep[:], None, ALU.mult))
            dve.wait_ge(s.logits_turned, 1)
            step(dve.tensor_tensor(logits[:], LOG[:, 0:NB * W].rearrange("p (b n) -> p b n", n=W),
                                   rms[:].unsqueeze(2).to_broadcast([P, NB, W]), ALU.mult))
            step(dve.tensor_tensor(logits[:], logits[:], base[:].unsqueeze(1).to_broadcast([P, NB, W]), ALU.add))
            pre_post = logits[:, :, NS * NS:W].rearrange("p b (k n) -> p b k n", n=NS)
            step(dve.tensor_reduce(pp_peak[:], pre_post, AX.X, ALU.max))
            dve.tensor_tensor(pp[:], pre_post, pp_peak[:].unsqueeze(3).to_broadcast([P, NB, 2, NS]),
                              ALU.subtract).then_inc(s.pp_less, 1)
            step(dve.tensor_scalar(L[:].rearrange("p b i j -> p b (i j)"), logits[:, :, 0:NS * NS], 10.0, None, ALU.mult))
            dve.wait_ge(s.pp_exped, 1)
            step(dve.tensor_reduce(pp_peak[:], pp[:], AX.X, ALU.add))
            step(dve.reciprocal(pp_peak[:], pp_peak[:]))
            dve.tensor_tensor(pp[:], pp[:], pp_peak[:].unsqueeze(3).to_broadcast([P, NB, 2, NS]),
                              ALU.mult).then_inc(s.pp_ready, 1)
            with dve.Fori(0, ITERS // UNROLL) as i:
                for k in range(2 * UNROLL):
                    def view(full, half):
                        ap = full[:, half.tiles]
                        return ap if k % 2 == 0 else ap.rearrange("p b i j -> p b j i")

                    def spread(small, half):
                        return small[:, half.tiles].unsqueeze(3).to_broadcast([P, NB // 2, NS, NS])

                    for half in HALVES:
                        dve.wait_ge(s.stepped, primed(i, 4 * UNROLL, 2 * k + half.number - 1 if k or half.number else 0))
                        dve.tensor_reduce(peak[:, half.tiles], view(L, half), AX.X, ALU.max).then_inc(s.peaked, 1)
                    for half in HALVES:
                        dve.wait_ge(s.peaked, nth(i, 4 * UNROLL, 2 * k + half.number + 1))
                        dve.tensor_tensor(view(L, half), view(L, half), spread(peak, half), ALU.subtract).then_inc(s.less_max, 1)
                    for half in HALVES:
                        dve.wait_ge(s.exped, nth(i, 4 * UNROLL, 2 * k + half.number + 1))
                        dve.tensor_reduce(total[:, half.tiles], view(E, half), AX.X, ALU.add).then_inc(s.summed, 1)
                    for half in HALVES:
                        dve.wait_ge(s.logged, nth(i, 4 * UNROLL, 2 * k + half.number + 1))
                        dve.tensor_tensor(view(L, half), view(L, half), spread(total, half), ALU.subtract).then_inc(s.stepped, 1)
            dve.wait_ge(s.H_exped, 1)
            step(dve.tensor_scalar(H[:], E[:].rearrange("p b i j -> p b (i j)"), gate[:], None, ALU.mult))
            dve.tensor_tensor(H[:], H[:], eye[:].unsqueeze(1).to_broadcast([P, NB, NS * NS]), ALU.add).then_inc(s.H_ready, 1)
            dve.wait_ge(s.H_ready, 1)
            dve.wait_ge(s.branch_added, NS)
            for k, b in enumerate(DVE_TILES):
                for j in range(NS):
                    for n in range(NS):
                        if j:
                            dve.wait_ge(s.dve_mixed, NS * (NS * k + j - 1) + n + 1)
                        dve.scalar_tensor_tensor(out=M.x[:, b, tile_of(n)], in0=xn[:, b, tile_of(j)],
                                                 scalar=H[:, b, NS * n + j:NS * n + j + 1], in1=M.x[:, b, tile_of(n)],
                                                 op0=ALU.mult, op1=ALU.add).then_inc(s.dve_mixed, 1)


def store_stage(nc, M, out):
    with ExitStack() as ctx:
        S = Scope(nc, M, ctx, "store")
        s = Named()
        [s.stored] = S.sems("stored")
        block = S.block()

        @block.sync
        def _(sp):
            sp.dma_start(out.rearrange("b p d -> p b d"), M.x[:]).then_inc(s.stored, 16)
            sp.wait_ge(s.stored, 16)


STAGES = ("attn0", "ffn0", "attn1", "ffn1", "attn2", "ffn2", "attn3", "ffn3")


def program(nc, A, out, stages=STAGES):
    with ExitStack() as ctx:
        M = Named()
        M.used_semaphores = []
        M.stats_made = False
        S = Scope(nc, M, ctx, "m")
        M.x = S.sb("x", [P, NB, D])
        M.nT = S.pair("nT", [P, KC, TOK])
        M.ident = S.sb("ident", [P, P])
        M.stats = S.sb("stats", [P, NB, 6])
        ln_w = S.sb("ln_w", [P, KC])
        M.neg_half = S.sb("neg_half", [P, 8])
        M.eps = S.sb("eps", [P, 8])
        psum = ctx.enter_context(nc.psum_tensor("banks", [P, 8, 512], F32))
        M.psum = psum
        M.bank = [psum[:, i, :] for i in range(8)]
        with ExitStack() as front:
            M.cT = Scope(nc, M, front, "c1").pair("cT", [P, KC, TOK])
            load_stage(nc, M, A["x"])
            if "attn0" in stages:
                attn0_stage(nc, M, A)
            if "ffn0" in stages:
                ffn0_stage(nc, M, A, ln_w)
                clear_semaphores(nc, M)
            if "attn1" in stages:
                attn1_stage(nc, M, A)
            if "ffn1" in stages:
                ffn1_stage(nc, M, A)
                clear_semaphores(nc, M)
            if "attn2" in stages:
                attn2_stage(nc, M, A)
                clear_semaphores(nc, M)
        if "ffn2" in stages:
            ffn2_stage(nc, M, A)
            clear_semaphores(nc, M)
        if "attn3" in stages:
            with ExitStack() as back:
                M.cT = Scope(nc, M, back, "c2").pair("cT", [P, KC, TOK])
                attn3_stage(nc, M, A)
                clear_semaphores(nc, M)
        if "ffn3" in stages:
            xn = S.sb("xn", [P, NB, D])
            rms = S.sb("rms", [P, NB])
            norm_stage(nc, M, "n7", rms_eps=RMS3_EPS, keep_rms=rms, xn=xn)
            ffn3_stage(nc, M, A, xn, rms, out)
        else:
            store_stage(nc, M, out)



def kc_major(w):
    return w.reshape(-1, P, w.shape[1]).transpose(1, 0, 2)


def column_blocks(w, n):
    k, m = w.shape
    return w.reshape(k // P, P, n, m // n).transpose(2, 1, 0, 3)


def row_blocks(w, n):
    k, m = w.shape
    return w.reshape(n, k // n // P, P, m).transpose(0, 2, 1, 3)


def lay_out(I):
    A = {"x": I["x"], "ctxT": I["ctx_4096"].reshape(TOK, D).T, "mask": I["mask_1x1xSxS2_ff0"].reshape(P, P)}
    A["L0_xattn_Wq"] = column_blocks(I["L0_xattn_Wq"].T, 8)
    A["L0_xattn_Wkv"] = np.concatenate([column_blocks(I["L0_xattn_Wk"].T, 8), column_blocks(I["L0_xattn_Wv"].T, 8)], axis=3)
    A["L0_xattn_Wo"] = row_blocks(I["L0_xattn_Wo"].T, 8)
    A["L0_xattn_q_norm_w"] = I["L0_xattn_q_norm_w"].reshape(P, 1)
    A["L0_xattn_k_norm_w"] = I["L0_xattn_k_norm_w"].reshape(P, 1)
    A["L0_ffn_ln_w"] = I["L0_ffn_ln_w"].reshape(KC, P).T
    A["L0_ffn_Wgu"] = np.stack([column_blocks(I["L0_ffn_gate_w"].T, 7), column_blocks(I["L0_ffn_up_w"].T, 7)], axis=3)
    A["L0_ffn_Wd"] = row_blocks(I["L0_ffn_down_w"].T, 7)
    A["L1_xattn_Wv"] = kc_major(I["L1_xattn_Wv"])
    k_repeated = np.repeat(I["L1_xattn_Wk"].reshape(D, 8, 1, 16), 4, axis=2).reshape(D, D)
    A["L1_xattn_Wqk"] = np.stack([column_blocks(I["L1_xattn_Wq"], 4), column_blocks(k_repeated, 4)], axis=3)
    A["L1_xattn_Wo"] = I["L1_xattn_Wo"].reshape(4, P, D)
    A["head_mask"] = (np.arange(P)[:, None] // 16 % 4 == np.arange(4)[None, :]).astype(np.float32)
    A["L1_ffn_mid"] = kc_major(np.concatenate([I["L1_ffn_lora_A"].transpose(1, 0, 2).reshape(D, P),
                                               I["L1_ffn_router_W"].T], axis=1))
    A["L1_ffn_base"] = kc_major(I["L1_ffn_base_W"].T)
    A["L1_ffn_lora_B"] = I["L1_ffn_lora_B"].reshape(P, D)
    A["expert"] = np.repeat(np.arange(-8, 0, dtype=np.float32)[None, :], P, axis=0)
    A["L2_xattn_Wkv"] = np.stack([column_blocks(I["L2_xattn_Wk"], 4), column_blocks(I["L2_xattn_Wv"], 4)], axis=3)
    A["L2_xattn_Wq"] = column_blocks(I["L2_xattn_Wq"], 8)
    A["L2_xattn_Wo"] = row_blocks(I["L2_xattn_Wo"], 8)
    padded = [np.pad(I["L2_ffn_w_gate"], ((0, C2 * P - I2), (0, 0))), np.pad(I["L2_ffn_w_up"], ((0, C2 * P - I2), (0, 0)))]
    A["L2_ffn_gate_up"] = np.stack([w.reshape(C2, P, D) for w in padded], axis=1)
    A["L2_ffn_down"] = np.pad(I["L2_ffn_w_down"], ((0, 0), (0, C2 * P - I2))).reshape(KC, P, C2 * P)
    A["ctx"] = I["ctx_4096"]
    A["L3_xattn_Wqk"] = np.stack([kc_major(I["L3_xattn_Wq"].T), kc_major(I["L3_xattn_Wk"].T)])
    A["L3_xattn_bias"] = np.stack([I["L3_xattn_bq"].reshape(KC, P).T, I["L3_xattn_bk"].reshape(KC, P).T], axis=1)
    A["L3_ffn_W"] = kc_major(np.concatenate([I["L3_ffn_W_res"], I["L3_ffn_W_pre"], I["L3_ffn_W_post"]]).T)
    A["L3_ffn_W_branch"] = I["L3_ffn_W_branch"]
    base = np.concatenate([I["L3_ffn_H_res_base"].reshape(-1), I["L3_ffn_H_pre_base"], I["L3_ffn_H_post_base"]])
    A["L3_ffn_base"] = np.repeat(base[None, :], P, axis=0)
    A["L3_ffn_gate"] = np.repeat(I["L3_ffn_gate"].reshape(1, 1), P, axis=0)
    A["eye"] = np.repeat(np.eye(4, dtype=np.float32).reshape(1, 16), P, axis=0)
    return {k: np.ascontiguousarray(v) for k, v in A.items()}


def kernel(**inputs):
    import concourse.bacc as bacc
    from concourse.bass_utils import run_bass_kernel_spmd

    nc = bacc.Bacc("TRN2", target_bir_lowering=False, num_devices=1)
    arrays = {f"in_{k}": v for k, v in lay_out({k: np.asarray(v) for k, v in inputs.items()}).items()}
    A = {k[3:]: nc.dram_tensor(k, v.shape, mybir.dt.from_np(v.dtype), kind="ExternalInput").ap()
         for k, v in arrays.items()}
    out = nc.dram_tensor("out_0", (NB, P, D), F32, kind="ExternalOutput").ap()
    program(nc, A, out)
    result = run_bass_kernel_spmd(nc, [arrays], core_ids=[0])
    return result.results[0]["out_0"]
```
